# Optimizing a Trainium2 kernel written in Bass

```python
import numpy as np
import jax
import jax.numpy as jnp

def _softmax(x, axis=-1):
    return jax.nn.softmax(x, axis=axis)

def _gelu(x):
    return jax.nn.gelu(x, approximate=True)

def _silu(x):
    return jax.nn.silu(x)

def _sigmoid(x):
    return jax.nn.sigmoid(x)

def _layernorm(x, axis=-1, eps=1e-05):
    m = jnp.mean(x, axis=axis, keepdims=True)
    v = jnp.var(x, axis=axis, keepdims=True)
    return (x - m) / jnp.sqrt(v + eps)

def _scatter_add(tgt, idx, src, axis=0):
    return tgt.at[idx].add(src)

def _segment_sum(src, seg, n):
    return jax.ops.segment_sum(src, seg, n)
kernel_name = 'mk_macaron_d2_jaxref_r4_c2dba2'

def setup_inputs(seed: int=0):
    np.random.seed(seed)
    _w = jnp.asarray

    def _L0_attn_setup():
        import jax, jax.numpy as jnp
        import numpy as np
        from jax import lax
        B, T, D, H = (2, 1024, 256, 16)
        DK = DV = D // H
        KS = 4
        ALPHA_MIN, BETA_MAX, EPS = (0.1, 1.0, 1e-06)

        def _causal_dwconv(x, w, b):
            C, K = w.shape
            xp = jnp.pad(x, ((0, 0), (K - 1, 0), (0, 0))).transpose(0, 2, 1)
            out = lax.conv_general_dilated(xp, w[:, None, :], (1,), 'VALID', feature_group_count=C, dimension_numbers=('NCH', 'OIH', 'NCH'))
            out = out + b[None, :, None]
            return jax.nn.silu(out).transpose(0, 2, 1)

        def _l2n(t):
            return t / jnp.maximum(jnp.linalg.norm(t, axis=-1, keepdims=True), 1e-06)
        key = jax.random.key(seed)
        ks = jax.random.split(key, 20)

        def w(i, shape, sc=0.02):
            return jax.random.normal(ks[i], shape, jnp.float32) * sc
        return {'x': jax.random.normal(ks[0], (B, T, D), jnp.float32), 'Wq': w(1, (D, H * DK)), 'Wk': w(2, (D, H * DK)), 'Wv': w(3, (D, H * DV)), 'Wo': w(4, (H * DV, D)), 'Wa': w(5, (D, H)), 'ba': jnp.full((H,), 2.0, jnp.float32), 'Wb': w(6, (D, H)), 'bb': jnp.zeros((H,), jnp.float32), 'Wgd': w(7, (D, H * DV // 2)), 'Wgu': w(8, (H * DV // 2, H * DV)), 'rms_w': jnp.ones((H, DV), jnp.float32), 'qcw': w(9, (H * DK, KS), 0.1), 'qcb': jnp.zeros((H * DK,), jnp.float32), 'kcw': w(10, (H * DK, KS), 0.1), 'kcb': jnp.zeros((H * DK,), jnp.float32), 'vcw': w(11, (H * DV, KS), 0.1), 'vcb': jnp.zeros((H * DV,), jnp.float32)}
    _L0_attn_in = _L0_attn_setup()

    def _L0_ffn_setup():
        import jax, jax.numpy as jnp
        import numpy as np
        NEG_INF = -1e+30
        K = 2
        key = jax.random.key(seed)
        ks = jax.random.split(key, 5)
        B, S, D, O, E = (8, 512, 256, 256, 8)
        scale = 1.0 / np.sqrt(D)
        return {'x': jax.random.normal(ks[0], (B, S, D), dtype=jnp.float32), 'gate_w': jax.random.normal(ks[1], (E, D), dtype=jnp.float32) * scale, 'gate_b': jnp.zeros((E,), dtype=jnp.float32), 'expert_w': jax.random.normal(ks[2], (E, O, D), dtype=jnp.float32) * scale, 'expert_b': jnp.zeros((E, O), dtype=jnp.float32)}
    _L0_ffn_in = _L0_ffn_setup()

    def _L1_attn_setup():
        import jax, jax.numpy as jnp
        import numpy as np
        import math
        B, S, E, H = (2, 512, 256, 16)
        HD = E // H
        HX = 64
        P = HX // 2

        def _l2norm(x, eps=1e-12):
            n = jnp.sqrt(jnp.sum(x * x, axis=-1, keepdims=True))
            return x / jnp.maximum(n, eps)

        def _scramble(t):
            b, h, p, s, _ = t.shape
            return jnp.swapaxes(t, -1, -2).reshape(b, h, p, s, 2)
        key = jax.random.key(seed)
        ks = jax.random.split(key, 12)
        sc = 0.02
        return {'x': jax.random.normal(ks[0], (B, S, E), dtype=jnp.float32), 'Wq': jax.random.normal(ks[1], (E, E), dtype=jnp.float32) * sc, 'bq': jnp.zeros((E,), dtype=jnp.float32), 'Wk': jax.random.normal(ks[2], (E, E), dtype=jnp.float32) * sc, 'bk': jnp.zeros((E,), dtype=jnp.float32), 'Wv': jax.random.normal(ks[3], (E, E), dtype=jnp.float32) * sc, 'bv': jnp.zeros((E,), dtype=jnp.float32), 'Wo': jax.random.normal(ks[4], (E, E), dtype=jnp.float32) * sc, 'bo': jnp.zeros((E,), dtype=jnp.float32), 'Whel': jax.random.normal(ks[5], (H, HX, HD), dtype=jnp.float32) * sc, 'bhel': jnp.zeros((H, HX), dtype=jnp.float32)}
    _L1_attn_in = _L1_attn_setup()

    def _L1_ffn_setup():
        import jax, jax.numpy as jnp
        import numpy as np
        IN_DIM, OUT_DIM, N_PROTO, RANK = (256, 256, 32, 16)
        key = jax.random.key(seed)
        ks = jax.random.split(key, 5)
        x = jax.random.normal(ks[0], (2, 1024, IN_DIM), dtype=jnp.float32)
        prototypes = jax.random.normal(ks[1], (N_PROTO, IN_DIM), dtype=jnp.float32) * 0.02
        B = jax.random.normal(ks[2], (N_PROTO, RANK, IN_DIM), dtype=jnp.float32) * 0.02
        A = jax.random.normal(ks[3], (N_PROTO, OUT_DIM, RANK), dtype=jnp.float32) * 0.02
        bias = jnp.zeros((N_PROTO, OUT_DIM), dtype=jnp.float32)
        temp = jnp.asarray(1.0, dtype=jnp.float32)
        return {'x': x, 'prototypes': prototypes, 'B': B, 'A': A, 'bias': bias, 'temp': temp}
    _L1_ffn_in = _L1_ffn_setup()
    _d = {'L0_attn_x': _L0_attn_in['x'], 'L0_attn_Wq': _L0_attn_in['Wq'], 'L0_attn_Wk': _L0_attn_in['Wk'], 'L0_attn_Wv': _L0_attn_in['Wv'], 'L0_attn_Wo': _L0_attn_in['Wo'], 'L0_attn_Wa': _L0_attn_in['Wa'], 'L0_attn_ba': _L0_attn_in['ba'], 'L0_attn_Wb': _L0_attn_in['Wb'], 'L0_attn_bb': _L0_attn_in['bb'], 'L0_attn_Wgd': _L0_attn_in['Wgd'], 'L0_attn_Wgu': _L0_attn_in['Wgu'], 'L0_attn_rms_w': _L0_attn_in['rms_w'], 'L0_attn_qcw': _L0_attn_in['qcw'], 'L0_attn_qcb': _L0_attn_in['qcb'], 'L0_attn_kcw': _L0_attn_in['kcw'], 'L0_attn_kcb': _L0_attn_in['kcb'], 'L0_attn_vcw': _L0_attn_in['vcw'], 'L0_attn_vcb': _L0_attn_in['vcb'], 'L0_ffn_gate_w': _L0_ffn_in['gate_w'], 'L0_ffn_gate_b': _L0_ffn_in['gate_b'], 'L0_ffn_expert_w': _L0_ffn_in['expert_w'], 'L0_ffn_expert_b': _L0_ffn_in['expert_b'], 'L1_attn_Wq': _L1_attn_in['Wq'], 'L1_attn_bq': _L1_attn_in['bq'], 'L1_attn_Wk': _L1_attn_in['Wk'], 'L1_attn_bk': _L1_attn_in['bk'], 'L1_attn_Wv': _L1_attn_in['Wv'], 'L1_attn_bv': _L1_attn_in['bv'], 'L1_attn_Wo': _L1_attn_in['Wo'], 'L1_attn_bo': _L1_attn_in['bo'], 'L1_attn_Whel': _L1_attn_in['Whel'], 'L1_attn_bhel': _L1_attn_in['bhel'], 'L1_ffn_prototypes': _L1_ffn_in['prototypes'], 'L1_ffn_B': _L1_ffn_in['B'], 'L1_ffn_A': _L1_ffn_in['A'], 'L1_ffn_bias': _L1_ffn_in['bias'], 'L1_ffn_temp': _L1_ffn_in['temp']}
    _x0 = _d['L0_attn_x']
    _d['L0_attn_x'] = jax.random.normal(jax.random.fold_in(jax.random.key(seed), 1), (2, 2048, 256), dtype=_x0.dtype)
    del _x0
    return _d

def reference(L0_attn_x, L0_attn_Wq, L0_attn_Wk, L0_attn_Wv, L0_attn_Wo, L0_attn_Wa, L0_attn_ba, L0_attn_Wb, L0_attn_bb, L0_attn_Wgd, L0_attn_Wgu, L0_attn_rms_w, L0_attn_qcw, L0_attn_qcb, L0_attn_kcw, L0_attn_kcb, L0_attn_vcw, L0_attn_vcb, L0_ffn_gate_w, L0_ffn_gate_b, L0_ffn_expert_w, L0_ffn_expert_b, L1_attn_Wq, L1_attn_bq, L1_attn_Wk, L1_attn_bk, L1_attn_Wv, L1_attn_bv, L1_attn_Wo, L1_attn_bo, L1_attn_Whel, L1_attn_bhel, L1_ffn_prototypes, L1_ffn_B, L1_ffn_A, L1_ffn_bias, L1_ffn_temp):

    def _L0_attn_ref(x, Wq, Wk, Wv, Wo, Wa, ba, Wb, bb, Wgd, Wgu, rms_w, qcw, qcb, kcw, kcb, vcw, vcb):
        import jax, jax.numpy as jnp
        import numpy as np
        from jax import lax
        B, T, D, H = (2, 1024, 256, 16)
        DK = DV = D // H
        KS = 4
        ALPHA_MIN, BETA_MAX, EPS = (0.1, 1.0, 1e-06)

        def _causal_dwconv(x, w, b):
            C, K = w.shape
            xp = jnp.pad(x, ((0, 0), (K - 1, 0), (0, 0))).transpose(0, 2, 1)
            out = lax.conv_general_dilated(xp, w[:, None, :], (1,), 'VALID', feature_group_count=C, dimension_numbers=('NCH', 'OIH', 'NCH'))
            out = out + b[None, :, None]
            return jax.nn.silu(out).transpose(0, 2, 1)

        def _l2n(t):
            return t / jnp.maximum(jnp.linalg.norm(t, axis=-1, keepdims=True), 1e-06)
        Bx, Tx, _ = x.shape
        BH = Bx * H
        q = _causal_dwconv(x @ Wq, qcw, qcb)
        k = _causal_dwconv(x @ Wk, kcw, kcb)
        v = _causal_dwconv(x @ Wv, vcw, vcb)

        def heads(t, d):
            return t.reshape(Bx, Tx, H, d).transpose(0, 2, 1, 3).reshape(BH, Tx, d)
        Q = _l2n(heads(q, DK))
        Kh = _l2n(heads(k, DK))
        V = heads(v, DV)
        alpha = jnp.clip(jax.nn.sigmoid(x @ Wa + ba), ALPHA_MIN, 1.0)
        beta = jnp.minimum(jax.nn.sigmoid(x @ Wb + bb), BETA_MAX)
        alpha = alpha.transpose(0, 2, 1).reshape(BH, Tx)
        beta = beta.transpose(0, 2, 1).reshape(BH, Tx)

        def step(S, inp):
            qt, kt, vt, at, bt = inp
            v_hat = jnp.einsum('bij,bi->bj', S, kt)
            err = vt - v_hat
            S = at[:, None, None] * S + bt[:, None, None] * (kt[:, :, None] * err[:, None, :])
            o = jnp.einsum('bij,bi->bj', S, qt)
            return (S, o)
        S0 = jnp.zeros((BH, DK, DV), x.dtype)
        _, O = lax.scan(step, S0, (Q.swapaxes(0, 1), Kh.swapaxes(0, 1), V.swapaxes(0, 1), alpha.T, beta.T))
        O = O.transpose(1, 0, 2).reshape(Bx, H, Tx, DV)
        O = O * lax.rsqrt(jnp.mean(O * O, -1, keepdims=True) + EPS) * rms_w[None, :, None, :]
        g = jax.nn.sigmoid(jax.nn.silu(x @ Wgd) @ Wgu).reshape(Bx, Tx, H, DV).transpose(0, 2, 1, 3)
        O = (O * g).transpose(0, 2, 1, 3).reshape(Bx, Tx, H * DV)
        return O @ Wo

    def _L0_ffn_ref(x, gate_w, gate_b, expert_w, expert_b):
        import jax, jax.numpy as jnp
        import numpy as np
        NEG_INF = -1e+30
        K = 2
        pooled = x.mean(axis=1)
        logits = pooled @ gate_w.T + gate_b
        topk_vals, _ = jax.lax.top_k(logits, K)
        min_topk = topk_vals[:, -1:]
        masked = jnp.where(logits < min_topk, -jnp.inf, logits)
        gates = jax.nn.softmax(masked, axis=-1)
        expert_out = jax.nn.gelu(jnp.einsum('bsd,eod->beso', x, expert_w) + expert_b[None, :, None, :], approximate=False)
        return jnp.einsum('be,beso->bso', gates, expert_out)

    def _L1_attn_ref(x, Wq, bq, Wk, bk, Wv, bv, Wo, bo, Whel, bhel):
        import jax, jax.numpy as jnp
        import numpy as np
        import math
        B, S, E, H = (2, 512, 256, 16)
        HD = E // H
        HX = 64
        P = HX // 2

        def _l2norm(x, eps=1e-12):
            n = jnp.sqrt(jnp.sum(x * x, axis=-1, keepdims=True))
            return x / jnp.maximum(n, eps)

        def _scramble(t):
            b, h, p, s, _ = t.shape
            return jnp.swapaxes(t, -1, -2).reshape(b, h, p, s, 2)
        b, s, e = x.shape
        h, hx, hd = Whel.shape
        p = hx // 2
        q = x @ Wq.T + bq
        k = x @ Wk.T + bk
        v = x @ Wv.T + bv
        qh = q.reshape(b, s, h, hd)
        kh = k.reshape(b, s, h, hd)
        q_hel = jnp.einsum('bshd,hed->bshe', qh, Whel) + bhel
        k_hel = jnp.einsum('bshd,hed->bshe', kh, Whel) + bhel
        qn = _l2norm(q_hel.reshape(b, s, h, p, 2)).transpose(0, 2, 3, 1, 4)
        kn = _l2norm(k_hel.reshape(b, s, h, p, 2)).transpose(0, 2, 3, 1, 4)
        qn = _scramble(qn)
        kn = _scramble(kn)
        helical = jnp.einsum('bhpsc,bhptc->bhst', qn, kn) / p
        dot = jnp.einsum('bshd,bthd->bhst', qh, kh) / math.sqrt(hd)
        alpha = 0.5
        attn = jax.nn.softmax(alpha * dot + (1.0 - alpha) * helical, axis=-1)
        vh = v.reshape(b, s, h, hd)
        out = jnp.einsum('bhst,bthd->bshd', attn, vh).reshape(b, s, e)
        return out @ Wo.T + bo

    def _L1_ffn_ref(x, prototypes, B, A, bias, temp):
        import jax, jax.numpy as jnp
        import numpy as np
        IN_DIM, OUT_DIM, N_PROTO, RANK = (256, 256, 32, 16)
        lead = x.shape[:-1]
        xf = x.reshape(-1, IN_DIM)
        x2 = jnp.sum(xf * xf, axis=1, keepdims=True)
        p2 = jnp.sum(prototypes * prototypes, axis=1)
        d2 = x2 + p2[None, :] - 2.0 * (xf @ prototypes.T)
        dists = jnp.sqrt(jnp.maximum(d2, 0.0))
        t = jnp.maximum(jnp.abs(temp), 0.1)
        w = jax.nn.softmax(-dists / t, axis=1)
        topw, topi = jax.lax.top_k(w, 2)
        topw = topw / jnp.sum(topw, axis=1, keepdims=True)
        out = jnp.zeros((xf.shape[0], OUT_DIM), dtype=xf.dtype)
        for tslot in range(2):
            idx = topi[:, tslot]
            wt = topw[:, tslot:tslot + 1]
            h = jnp.einsum('nri,ni->nr', B[idx], xf)
            y = jnp.einsum('nor,nr->no', A[idx], h) + bias[idx]
            out = out + wt * y
        return out.reshape(*lead, OUT_DIM)
    x = L0_attn_x
    x = x + 0.5 * _L0_ffn_ref(_layernorm(x, axis=-1), L0_ffn_gate_w, L0_ffn_gate_b, L0_ffn_expert_w, L0_ffn_expert_b)
    x = x + _L0_attn_ref(_layernorm(x, axis=-1), L0_attn_Wq, L0_attn_Wk, L0_attn_Wv, L0_attn_Wo, L0_attn_Wa, L0_attn_ba, L0_attn_Wb, L0_attn_bb, L0_attn_Wgd, L0_attn_Wgu, L0_attn_rms_w, L0_attn_qcw, L0_attn_qcb, L0_attn_kcw, L0_attn_kcb, L0_attn_vcw, L0_attn_vcb)
    x = x + 0.5 * _L0_ffn_ref(_layernorm(x, axis=-1), L0_ffn_gate_w, L0_ffn_gate_b, L0_ffn_expert_w, L0_ffn_expert_b)
    x = x + 0.5 * _L1_ffn_ref(_layernorm(x, axis=-1), L1_ffn_prototypes, L1_ffn_B, L1_ffn_A, L1_ffn_bias, L1_ffn_temp)
    x = x + _L1_attn_ref(_layernorm(x, axis=-1), L1_attn_Wq, L1_attn_bq, L1_attn_Wk, L1_attn_bk, L1_attn_Wv, L1_attn_bv, L1_attn_Wo, L1_attn_bo, L1_attn_Whel, L1_attn_bhel)
    x = x + 0.5 * _L1_ffn_ref(_layernorm(x, axis=-1), L1_ffn_prototypes, L1_ffn_B, L1_ffn_A, L1_ffn_bias, L1_ffn_temp)
    return x

_drawn_inputs = setup_inputs


def setup_inputs(seed=0):
    import zlib

    import numpy as np

    out = dict(_drawn_inputs(seed))
    spreads = {'L0_attn_ba': (2.0, 0.6),
     'L0_attn_bb': (0.0, 0.8),
     'L0_attn_rms_w': (1.0, 0.2),
     'L0_attn_qcb': (0.0, 0.1),
     'L0_attn_kcb': (0.0, 0.1),
     'L0_attn_vcb': (0.0, 0.1),
     'L0_ffn_gate_b': (0.0, 0.1),
     'L0_ffn_expert_b': (0.0, 0.1),
     'L1_attn_bq': (0.0, 0.8),
     'L1_attn_bk': (0.0, 0.8),
     'L1_attn_bv': (0.0, 0.273),
     'L1_attn_bo': (0.0, 0.1),
     'L1_attn_bhel': (0.0, 0.8),
     'L1_ffn_bias': (0.0, 0.1)}
    factors = {'L0_attn_Wa': 8.0,
     'L0_attn_Wb': 3.664,
     'L0_attn_Wgd': 8.0,
     'L0_attn_Wgu': 8.0,
     'L1_attn_Wq': 8.0,
     'L1_attn_Wk': 8.0,
     'L1_attn_Wv': 4.712,
     'L1_attn_Whel': 8.0,
     'L1_ffn_B': 3.558,
     'L1_ffn_A': 3.562}
    for name, (base, spread) in spreads.items():
        noise = np.random.default_rng([zlib.crc32(name.encode()), seed]).standard_normal(out[name].shape)
        drawn = base * np.exp(spread * noise) if base else spread * noise
        out[name] = jnp.asarray(drawn.astype(out[name].dtype))
    for name, factor in factors.items():
        out[name] = (out[name] * factor).astype(out[name].dtype)
    return out
```

```python
import math
from contextlib import ExitStack

import concourse.bass as bass
from concourse import mybir

F32 = mybir.dt.float32
F16 = mybir.dt.float16
U32 = mybir.dt.uint32
ALU = mybir.AluOpType
ACT = mybir.ActivationFunctionType
AX = mybir.AxisListType

P = 128
B = 2
T = 2048
N = B * T
D = 256
CT = D // P
BLK = 512
NBLK = N // BLK
LN_EPS = 1e-5
LOG_EXP_SET = "natural_log_exp_and_others"


class Scope:

    def __init__(self, nc, stage):
        self.nc, self.stage, self.stack, self.semaphores = nc, stage, ExitStack(), []

    def __enter__(self):
        return self

    def __exit__(self, *error):
        if self.semaphores:
            self.nc.clear_and_free_semaphores(self.semaphores)
            self.nc.all_engine_barrier()
        return self.stack.__exit__(*error)

    def sb(self, name, shape, dtype=F32):
        return self.stack.enter_context(self.nc.sbuf_tensor(f"{self.stage}_{name}", shape, dtype))

    def ps(self, name, shape, dtype=F32):
        return self.stack.enter_context(self.nc.psum_tensor(f"{self.stage}_{name}", shape, dtype))

    def sem(self, name):
        self.semaphores.append(self.nc.alloc_semaphore(f"{self.stage}_{name}"))
        return self.semaphores[-1]


def tokens(i, size=BLK):
    return bass.ds(i * size, size)


def over_tiles(ap, tiles):
    return ap.unsqueeze(1).broadcast_to([ap.shape[0], tiles, ap.shape[1]])


def load_constants(nc, c, dram):
    loaded = nc.alloc_semaphore("constants_loaded")
    with nc.Block() as block:

        @block.sync
        def _(sp):
            for tile in range(CT):
                sp.dma_start(c["x"][:, tile, :], dram["x"][:, tile, :]).then_inc(loaded, 16)
            for name in ("mean_matrix", "identity", "head_mask", "head_sum"):
                sp.dma_start(c[name][:], dram[name]).then_inc(loaded, 16)
            sp.wait_ge(loaded, 16 * (CT + 4))

        @block.vector
        def _(dve):
            nc.vector.memset(c["ln_eps"][:], LN_EPS)


def store_result(nc, c, dram):
    stored = nc.alloc_semaphore("result_stored")
    with nc.Block() as block:

        @block.sync
        def _(sp):
            for tile in range(CT):
                sp.dma_start(dram["out"][:, tile, :], c["x"][:, tile, :]).then_inc(stored, 16)
            sp.wait_ge(stored, 16 * CT)


def layer_norm(nc, c, stage, xn, sums):
    x, mean_matrix = c["x"], c["mean_matrix"]
    with Scope(nc, stage) as s:
        mean = s.ps("mean", [P, 2, BLK])
        var = s.ps("var", [P, 2, BLK])
        centred = s.sb("centred", [P, 2, CT, BLK])
        squares = s.sb("squares", [P, 2, CT, BLK])
        log_var = s.sb("log_var", [P, 2, BLK])
        rstd = s.sb("rstd", [P, 2, BLK])
        mean_ready, centred_ready, squares_ready = s.sem("mean_ready"), s.sem("centred_ready"), s.sem("squares_ready")
        var_ready, log_ready, rstd_ready, normed = s.sem("var_ready"), s.sem("log_ready"), s.sem("rstd_ready"), s.sem("normed")
        CREDIT = 2

        with nc.Block() as block:

            @block.tensor
            def _(pe):
                with pe.Fori(0, NBLK // 2) as pair:
                    for slot in range(2):
                        pe.wait_ge(centred_ready, pair * 2 + slot + 1)
                        for tile in range(CT):
                            mm = nc.tensor.matmul(mean[:, slot], mean_matrix[:], x[:, tile, tokens(pair * 2 + slot)],
                                                  start=tile == 0, stop=tile == CT - 1)
                        mm.then_inc(mean_ready, 1)
                    for slot in range(2):
                        pe.wait_ge(squares_ready, pair * 2 + slot + 1)
                        pe.wait_ge(log_ready, pair * 2 + slot + 1)
                        for tile in range(CT):
                            mm = nc.tensor.matmul(var[:, slot], mean_matrix[:], squares[:, slot, tile],
                                                  start=tile == 0, stop=tile == CT - 1)
                        mm.then_inc(var_ready, 1)

            @block.scalar
            def _(act):
                nc.scalar.preload_act_table_set(LOG_EXP_SET)
                act.sem_inc(log_ready, CREDIT)
                with act.Fori(0, NBLK // 2) as pair:
                    for slot in range(2):
                        act.wait_ge(centred_ready, pair * 2 + slot + 1 + CREDIT)
                        act.wait_ge(log_ready, pair * 2 + slot + 1)
                        nc.scalar.activation(squares[:, slot], centred[:, slot], ACT.Square).then_inc(squares_ready, 1)
                    for slot in range(2):
                        act.wait_ge(var_ready, pair * 2 + slot + 1)
                        nc.scalar.activation(log_var[:, slot], var[:, slot], ACT.Ln,
                                             bias=c["ln_eps"][:, 0:1]).then_inc(log_ready, 1)
                        act.wait_ge(log_ready, pair * 2 + slot + 1 + CREDIT)
                        act.wait_ge(normed, (pair * 2 + slot) * CT + 1)
                        nc.scalar.activation(rstd[:, slot], log_var[:, slot], ACT.Exp, scale=-0.5).then_inc(rstd_ready, 1)

            @block.vector
            def _(dve):
                dve.sem_inc(centred_ready, CREDIT)
                dve.sem_inc(normed, 1 + CT)
                with dve.Fori(0, NBLK // 2) as pair:
                    for slot in range(2):
                        dve.wait_ge(mean_ready, pair * 2 + slot + 1)
                        dve.wait_ge(normed, (pair * 2 + slot) * CT + 1)
                        nc.vector.tensor_tensor(centred[:, slot], x[:, :, tokens(pair * 2 + slot)],
                                                over_tiles(mean[:, slot], CT), ALU.subtract).then_inc(centred_ready, 1)
                    for slot in range(2):
                        dve.wait_ge(rstd_ready, pair * 2 + slot + 1)
                        for tile in range(CT):
                            if sums is None:
                                mult = nc.vector.tensor_tensor(xn[:, tile, tokens(pair * 2 + slot)], centred[:, slot, tile],
                                                               rstd[:, slot], ALU.mult)
                            else:
                                mult = nc.vector.scalar_tensor_tensor(
                                    xn[:, tile, tokens(pair * 2 + slot)], centred[:, slot, tile], 1.0, rstd[:, slot],
                                    ALU.mult, ALU.mult, accum_out=sums[:, tile, bass.ds(pair * 2 + slot, 1)])
                            mult.then_inc(normed, 1)


def gated_experts(nc, c, dram, stage):
    E = dram["gate_w"].shape[2]
    x = c["x"]
    with Scope(nc, stage) as s:
        xn = s.sb("xn", [P, CT, N])
        sums = s.sb("sums", [P, CT, NBLK])
        layer_norm(nc, c, f"{stage}_ln", xn, sums)

        gate_w = s.sb("gate_w", [P, CT, E])
        gate_b = s.sb("gate_b", [P, E])
        expert = s.sb("expert", [P, 2, CT * D + CT])
        weights = expert[:, :, 0:CT * D].rearrange("p s (t d) -> p s t d", t=CT)
        bias = expert[:, :, CT * D:]
        hidden = s.sb("hidden", [P, 4, BLK])
        pooled = s.sb("pooled", [P, CT, B])
        terms = s.sb("terms", [P, CT, B, E])
        logits = s.sb("logits", [P, B, E])
        top = s.sb("top", [P, B, 8])
        minus_max = s.sb("minus_max", [P, B])
        chosen = s.sb("chosen", [P, B, E])
        powers = s.sb("powers", [P, B, E])
        total = s.sb("total", [P, B])
        gate = s.sb("gate", [P, B, E])
        logit_sum = s.ps("logit_sum", [P, B * E])
        pre = s.ps("pre", [P, 4, BLK])

        tables_loaded = s.sem("tables_loaded")
        expert_loaded = [s.sem(f"expert_loaded{slot}") for slot in range(2)]
        terms_ready, logits_ready, gate_step, powers_ready = s.sem("terms_ready"), s.sem("logits_ready"), s.sem("gate_step"), s.sem("powers_ready")
        pre_ready, hidden_ready, added = s.sem("pre_ready"), s.sem("hidden_ready"), s.sem("added")
        SLOTS = 4
        PER_EXPERT = NBLK * CT
        CREDIT = 2 * PER_EXPERT

        with nc.Block() as block:

            @block.sync
            def _(sp):
                for tile, table in ((gate_w, "gate_w"), (gate_b, "gate_b")):
                    sp.dma_start(tile[:], dram[table]).then_inc(tables_loaded, 16)
                with sp.Fori(0, E // 2) as pair:
                    for slot in range(2):
                        sp.wait_ge(pre_ready, (pair * 2 + slot + 1) * PER_EXPERT)
                        sp.wait_ge(hidden_ready, (pair * 2 + slot + 1) * PER_EXPERT)
                        sp.dma_start(expert[:, slot], dram["expert"][:, bass.ds(pair * 2 + slot, 1)].squeeze(1)
                                     ).then_inc(expert_loaded[slot], 16)

            @block.tensor
            def _(pe):
                pe.wait_ge(terms_ready, 1)
                for tile in range(CT):
                    mm = nc.tensor.matmul(logit_sum[:], c["mean_matrix"][:], terms[:, tile].rearrange("p b e -> p (b e)"),
                                          start=tile == 0, stop=tile == CT - 1)
                mm.then_inc(logits_ready, 1)
                pe.sem_inc(pre_ready, CREDIT)
                with pe.Fori(0, E // 2) as pair:
                    for u in range(2):
                        pe.wait_ge(expert_loaded[u], (pair + 1) * 16)
                        for n in range(NBLK):
                            for o in range(CT):
                                k = (u * NBLK + n) * CT + o
                                pe.wait_ge(hidden_ready, pair * 2 * PER_EXPERT + k + 1 + CREDIT - SLOTS)
                                for tile in range(CT):
                                    mm = nc.tensor.matmul(pre[:, k % SLOTS], weights[:, u, tile, o * P:(o + 1) * P],
                                                          xn[:, tile, tokens(n)], start=tile == 0, stop=tile == CT - 1)
                                mm.then_inc(pre_ready, 1)

            @block.scalar
            def _(act):
                for b in range(B):
                    act.wait_ge(gate_step, 5)
                    nc.scalar.activation(powers[:, b], logits[:, b], ACT.Exp,
                                         bias=minus_max[:, b:b + 1]).then_inc(powers_ready, 1)
                act.sem_inc(hidden_ready, CREDIT)
                with act.Fori(0, E // 2) as pair:
                    for k in range(2 * PER_EXPERT):
                        act.wait_ge(pre_ready, pair * 2 * PER_EXPERT + k + 1 + CREDIT)
                        act.wait_ge(added, pair * 2 * PER_EXPERT + k + 1)
                        nc.scalar.activation(hidden[:, k % SLOTS], pre[:, k % SLOTS], ACT.Gelu,
                                             bias=bias[:, k // PER_EXPERT, k % CT:k % CT + 1]
                                             ).then_inc(hidden_ready, 1)

            @block.vector
            def _(dve):
                dve.wait_ge(tables_loaded, 32)
                nc.vector.tensor_reduce(pooled[:], sums[:].rearrange("p c (b n) -> p c b n", b=B), AX.X, ALU.add).then_inc(gate_step, 1)
                dve.wait_ge(gate_step, 1)
                for tile in range(CT):
                    for b in range(B):
                        last = nc.vector.tensor_scalar(terms[:, tile, b], gate_w[:, tile], pooled[:, tile, b:b + 1], None, ALU.mult)
                last.then_inc(terms_ready, 1)
                dve.wait_ge(logits_ready, 1)
                nc.vector.scalar_tensor_tensor(logits[:], logit_sum[:].rearrange("p (b e) -> p b e", b=B), float(D) / T,
                                               over_tiles(gate_b[:], B), ALU.mult, ALU.add).then_inc(gate_step, 1)
                dve.wait_ge(gate_step, 2)
                for b in range(B):
                    nc.vector.max(top[:, b], logits[:, b]).then_inc(gate_step, 1)
                dve.wait_ge(gate_step, 4)
                nc.vector.tensor_scalar(minus_max[:], top[:, :, 0], -1.0, None, ALU.mult).then_inc(gate_step, 1)
                for b in range(B):
                    nc.vector.tensor_scalar(chosen[:, b], logits[:, b], top[:, b, 1:2], None, ALU.is_ge).then_inc(gate_step, 1)
                dve.wait_ge(gate_step, 7)
                dve.wait_ge(powers_ready, 2)
                nc.vector.tensor_tensor(chosen[:], chosen[:], powers[:], ALU.mult).then_inc(gate_step, 1)
                dve.wait_ge(gate_step, 8)
                nc.vector.tensor_reduce(total[:], chosen[:], AX.X, ALU.add).then_inc(gate_step, 1)
                dve.wait_ge(gate_step, 9)
                nc.vector.reciprocal(total[:], total[:]).then_inc(gate_step, 1)
                dve.wait_ge(gate_step, 10)
                for b in range(B):
                    nc.vector.tensor_scalar(gate[:, b], chosen[:, b], total[:, b:b + 1], 0.5, ALU.mult, ALU.mult).then_inc(gate_step, 1)
                dve.wait_ge(gate_step, 12)
                dve.sem_inc(added, SLOTS)
                with dve.Fori(0, E // 2) as pair:
                    for u in range(2):
                        for n in range(NBLK):
                            for o in range(CT):
                                k = (u * NBLK + n) * CT + o
                                b = n * BLK // T
                                dve.wait_ge(hidden_ready, pair * 2 * PER_EXPERT + k + 1 + CREDIT)
                                dve.wait_ge(added, pair * 2 * PER_EXPERT + k + 1)
                                nc.vector.scalar_tensor_tensor(x[:, o, tokens(n)], hidden[:, k % SLOTS],
                                                               gate[:, b, bass.ds(pair * 2 + u, 1)], x[:, o, tokens(n)],
                                                               ALU.mult, ALU.add).then_inc(added, 1)


def prototype_mixture(nc, c, dram, stage):
    NP = dram["proto_rows"].shape[0]
    RANK = dram["proto_B"].shape[2] // NP
    RT = NP * RANK // P
    TILES = N // P
    PER_BLK = BLK // P
    x = c["x"]
    with Scope(nc, stage) as s:
        xn = s.sb("xn", [P, CT, N])
        layer_norm(nc, c, f"{stage}_ln", xn, None)

        proto = s.sb("proto", [P, CT, NP])
        proto_rows = s.sb("proto_rows", [NP, D])
        proto_sq = s.sb("proto_sq", [NP, D])
        p2 = s.sb("p2", [NP, 1])
        ones = s.sb("ones", [P, NP])
        temp = s.sb("temp", [P, 1])
        minus_inv_t = s.sb("minus_inv_t", [P, 1])
        down = s.sb("down", [P, CT, NP * RANK])
        up = s.sb("up", [P, RT, D])
        bias = s.sb("bias", [NP, D])
        spread = s.sb("spread", [NP, NP * RANK])
        numbers = s.sb("numbers", [P, NP])
        squares = s.sb("squares", [P, 2, CT, BLK])
        clamped = s.sb("clamped", [NP, N])
        dist = s.sb("dist", [NP, N])
        scores = s.sb("scores", [P, TILES, NP])
        top = s.sb("top", [P, TILES, 8])
        which = s.sb("which", [P, TILES, 8], U32)
        whichf = s.sb("whichf", [P, TILES, 8])
        gap = s.sb("gap", [P, TILES])
        ratio = s.sb("ratio", [P, TILES])
        share = s.sb("share", [P, 2, TILES])
        picked = s.sb("picked", [P, 2, TILES, NP])
        mix = s.sb("mix", [NP, N])
        wide = s.sb("wide", [P, 2, BLK])
        low = s.sb("low", [P, 4, BLK])

        d2 = s.ps("d2", [P, 2, BLK])
        turned = s.ps("turned", [P, 2, BLK])
        low_sum = s.ps("low_sum", [P, 2, BLK])
        out = s.ps("out", [P, 2, BLK])
        mix_turned, wide_sum = d2, turned

        loaded, table_step = s.sem("loaded"), s.sem("table_step")
        squares_ready, d2_ready, clamped_ready, dist_ready = s.sem("squares_ready"), s.sem("d2_ready"), s.sem("clamped_ready"), s.sem("dist_ready")
        turned_ready, route_step, ratio_ready, picked_ready = s.sem("turned_ready"), s.sem("route_step"), s.sem("ratio_ready"), s.sem("picked_ready")
        mix_turned_ready, mix_ready = s.sem("mix_turned_ready"), s.sem("mix_ready")
        sums_ready, wide_ready, low_ready, out_ready, added = s.sem("sums_ready"), s.sem("wide_ready"), s.sem("low_ready"), s.sem("out_ready"), s.sem("added")
        CREDIT = 4

        with nc.Block() as block:

            @block.sync
            def _(sp):
                for tile, table in ((proto, "proto"), (proto_rows, "proto_rows"), (temp, "temp"), (numbers, "numbers"), (down, "proto_B"),
                                    (up, "proto_A"), (bias, "proto_bias"), (spread, "proto_spread")):
                    sp.dma_start(tile[:], dram[table]).then_inc(loaded, 16)

            def turn_distances(pe, n):
                pe.wait_ge(dist_ready, n + 1)
                for k in range(PER_BLK):
                    tile = n * PER_BLK + k
                    half, at = divmod(tile * NP, BLK)
                    mm = nc.tensor.transpose(turned[:, half, at:at + NP], dist[:, tile * P:(tile + 1) * P], c["identity"][0:NP, 0:NP])
                mm.then_inc(turned_ready, 1)

            @block.tensor
            def _(pe):
                pe.wait_ge(table_step, 4)
                for n in range(NBLK):
                    if n >= 2:
                        pe.wait_ge(clamped_ready, n - 1)
                    for tile in range(CT):
                        nc.tensor.matmul(d2[0:NP, n % 2], proto[:, tile], xn[:, tile, tokens(n)], start=tile == 0, stop=False)
                    pe.wait_ge(squares_ready, n + 1)
                    for tile in range(CT):
                        mm = nc.tensor.matmul(d2[0:NP, n % 2], ones[:], squares[:, n % 2, tile], start=False, stop=tile == CT - 1)
                    mm.then_inc(d2_ready, 1)
                    if n >= 1:
                        turn_distances(pe, n - 1)
                turn_distances(pe, NBLK - 1)
                pe.wait_ge(clamped_ready, NBLK)
                for n in range(NBLK):
                    pe.wait_ge(picked_ready, 1)
                    if n >= 2:
                        pe.wait_ge(mix_ready, n - 1)
                    for k in range(PER_BLK):
                        mm = nc.tensor.transpose(mix_turned[0:NP, n % 2, k * P:(k + 1) * P], picked[:, 0, n * PER_BLK + k], c["identity"][:])
                    mm.then_inc(mix_turned_ready, 1)
                pe.wait_ge(mix_ready, NBLK)
                with pe.Fori(0, NBLK // 2) as pair:
                    for u in range(2):
                        n = pair * 2 + u
                        for m in range(RT + 1):
                            if m < RT:
                                k = u * RT + m
                                pe.wait_ge(wide_ready, pair * 2 * RT + k + 1)
                                pe.wait_ge(low_ready, pair * 2 * RT + k + 1 + CREDIT - 2)
                                for tile in range(CT):
                                    nc.tensor.matmul(low_sum[:, m % 2], down[:, tile, m * P:(m + 1) * P], xn[:, tile, tokens(n)],
                                                     start=tile == 0, stop=tile == CT - 1)
                                nc.tensor.matmul(wide_sum[:, m % 2], spread[:, m * P:(m + 1) * P], mix[:, tokens(n)],
                                                 start=True, stop=True).then_inc(sums_ready, 1)
                            if m >= 1:
                                k = u * RT + m - 1
                                pe.wait_ge(low_ready, pair * 2 * RT + k + 1 + CREDIT)
                                if m == 1:
                                    pe.wait_ge(added, (n + 1) * CT)
                                for o in range(CT):
                                    nc.tensor.matmul(out[:, o], up[:, m - 1, o * P:(o + 1) * P], low[:, (m - 1) % 4],
                                                     start=m == 1, stop=False)
                        for o in range(CT):
                            nc.tensor.matmul(out[:, o], bias[:, o * P:(o + 1) * P], mix[:, tokens(n)],
                                             start=False, stop=True).then_inc(out_ready, 1)

            @block.scalar
            def _(act):
                for n in range(NBLK + 1):
                    if n < NBLK:
                        if n >= 2:
                            act.wait_ge(d2_ready, n - 1)
                        nc.scalar.activation(squares[:, n % 2], xn[:, :, tokens(n)], ACT.Square).then_inc(squares_ready, 1)
                    if n >= 1:
                        act.wait_ge(clamped_ready, n)
                        nc.scalar.activation(dist[:, tokens(n - 1)], clamped[:, tokens(n - 1)], ACT.Sqrt).then_inc(dist_ready, 1)
                act.wait_ge(route_step, 2 + 2 * TILES)
                nc.scalar.activation(ratio[:], gap[:], ACT.Exp).then_inc(ratio_ready, 1)
                act.sem_inc(wide_ready, 2)
                with act.Fori(0, NBLK // 2) as pair:
                    for k in range(2 * RT):
                        act.wait_ge(sums_ready, pair * 2 * RT + k + 1)
                        act.wait_ge(low_ready, pair * 2 * RT + k + 1 + CREDIT - 2)
                        nc.scalar.activation(wide[:, k % 2], wide_sum[:, k % 2], ACT.Copy).then_inc(wide_ready, 1)

            @block.vector
            def _(dve):
                nc.vector.memset(ones[:], 1.0).then_inc(table_step, 1)
                dve.wait_ge(loaded, 16 * 8)
                for tile in range(CT):
                    nc.vector.tensor_scalar(proto[:, tile], proto[:, tile], -2.0, None, ALU.mult).then_inc(table_step, 1)
                nc.vector.scalar_tensor_tensor(proto_sq[:], proto_rows[:], 1.0, proto_rows[:], ALU.mult, ALU.mult,
                                               accum_out=p2[:, 0:1]).then_inc(table_step, 1)
                nc.vector.scalar_tensor_tensor(minus_inv_t[:], temp[:], -1.0, temp[:], ALU.mult, ALU.max).then_inc(table_step, 1)
                dve.wait_ge(table_step, 5)
                nc.vector.tensor_scalar(temp[:], minus_inv_t[:], 0.1, -1.0, ALU.max, ALU.mult).then_inc(table_step, 1)
                dve.wait_ge(table_step, 6)
                nc.vector.reciprocal(minus_inv_t[:], temp[:]).then_inc(table_step, 1)
                dve.wait_ge(table_step, 7)
                for n in range(NBLK):
                    dve.wait_ge(d2_ready, n + 1)
                    nc.vector.tensor_scalar(clamped[:, tokens(n)], d2[0:NP, n % 2], p2[:, 0:1], 0.0, ALU.add, ALU.max).then_inc(clamped_ready, 1)
                dve.wait_ge(turned_ready, NBLK)
                nc.vector.tensor_scalar(scores[:].rearrange("p t n -> p (t n)"), turned[:].rearrange("p a b -> p (a b)"),
                                        minus_inv_t[:, 0:1], None, ALU.mult).then_inc(route_step, 1)
                dve.wait_ge(route_step, 1)
                for tile in range(TILES):
                    nc.vector.max(top[:, tile], scores[:, tile]).then_inc(route_step, 1)
                for tile in range(TILES):
                    dve.wait_ge(route_step, 2 + tile)
                    nc.vector.max_index(which[:, tile], top[:, tile], scores[:, tile]).then_inc(route_step, 1)
                nc.vector.tensor_tensor(gap[:], top[:, :, 1], top[:, :, 0], ALU.subtract).then_inc(route_step, 1)
                done = 2 + 2 * TILES
                dve.wait_ge(route_step, done)
                nc.vector.tensor_copy(whichf[:], which[:]).then_inc(route_step, 1)
                dve.wait_ge(ratio_ready, 1)
                nc.vector.tensor_scalar(share[:, 1], ratio[:], 1.0, None, ALU.add).then_inc(route_step, 1)
                dve.wait_ge(route_step, done + 2)
                nc.vector.reciprocal(share[:, 0], share[:, 1]).then_inc(route_step, 1)
                dve.wait_ge(route_step, done + 3)
                nc.vector.tensor_scalar(share[:, 0], share[:, 0], 0.5, None, ALU.mult).then_inc(route_step, 1)
                dve.wait_ge(route_step, done + 4)
                nc.vector.tensor_tensor(share[:, 1], share[:, 0], ratio[:], ALU.mult).then_inc(route_step, 1)
                for rank in range(2):
                    nc.vector.tensor_tensor(picked[:, rank], numbers[:].unsqueeze(1).broadcast_to([P, TILES, NP]),
                                            whichf[:, :, rank:rank + 1].broadcast_to([P, TILES, NP]), ALU.is_equal).then_inc(route_step, 1)
                dve.wait_ge(route_step, done + 7)
                for rank in range(2):
                    nc.vector.tensor_tensor(picked[:, rank], picked[:, rank],
                                            share[:, rank].unsqueeze(2).broadcast_to([P, TILES, NP]), ALU.mult).then_inc(route_step, 1)
                dve.wait_ge(route_step, done + 9)
                nc.vector.tensor_tensor(picked[:, 0], picked[:, 0], picked[:, 1], ALU.add).then_inc(picked_ready, 1)
                for n in range(NBLK):
                    dve.wait_ge(mix_turned_ready, n + 1)
                    nc.vector.tensor_copy(mix[:, tokens(n)], mix_turned[0:NP, n % 2]).then_inc(mix_ready, 1)
                dve.sem_inc(low_ready, CREDIT)
                dve.sem_inc(added, CT)
                with dve.Fori(0, NBLK // 2) as pair:
                    for u in range(2):
                        n = pair * 2 + u
                        for m in range(RT):
                            k = u * RT + m
                            dve.wait_ge(wide_ready, pair * 2 * RT + k + 1 + 2)
                            dve.wait_ge(added, (n + 1) * CT)
                            nc.vector.tensor_tensor(low[:, m % 4], low_sum[:, m % 2], wide[:, m % 2], ALU.mult).then_inc(low_ready, 1)
                        for o in range(CT):
                            dve.wait_ge(out_ready, n * CT + o + 1)
                            nc.vector.tensor_tensor(x[:, o, tokens(n)], x[:, o, tokens(n)], out[:, o], ALU.add).then_inc(added, 1)


HEADS = 16
HD = D // HEADS
HX = 64
PAIRS = HX // 2
BH = B * HEADS
QG = P // PAIRS
QT = T // P
LOGIT_SCALE = 1.0 / 64
DOT_SCALE = 8.0
MAX_ROW = HX + 3 * HD
V_SCALE = 16.0
PROB_SCALE = 256.0
ONES = 2 * HD
V_COLS = ONES + 1


def project_qkv(nc, c, dram, stage, xn, qk, v):
    with Scope(nc, stage) as s:
        w_qk = s.sb("w_qk", [P, 2, CT, D])
        w_v = s.sb("w_v", [P, CT, D])
        b_qk = s.sb("b_qk", [P, 2, CT])
        b_v = s.sb("b_v", [P, D])
        v_sum = s.sb("v_sum", [P, 2, D])
        high = s.sb("high", [P, 2, T], F16)
        rest = s.sb("rest", [P, 2, T], F16)
        acc = s.ps("acc", [P, 4, BLK])
        loaded, acc_ready, qk_ready, v_ready = s.sem("loaded"), s.sem("acc_ready"), s.sem("qk_ready"), s.sem("v_ready")
        high_ready, rest_ready, v_step = s.sem("high_ready"), s.sem("rest_ready"), s.sem("v_step")
        stored = [s.sem(f"stored{slot}") for slot in range(2)]
        steps = [(w, tile, n) for w in range(2) for tile in range(CT) for n in range(NBLK)]
        HALF = NBLK // B

        with nc.Block() as block:

            @block.sync
            def _(sp):
                for tile, table in ((w_qk, "att_w_qk"), (w_v, "att_w_v"), (b_qk, "att_b_qk"), (b_v, "att_b_v")):
                    sp.dma_start(tile[:], dram[table]).then_inc(loaded, 16)
                for r in range(len(steps) // HALF):
                    w, tile, n = steps[r * HALF]
                    rows = w * BH * HD + (n // HALF) * D + tile * P
                    sp.wait_ge(rest_ready, (r + 1) * HALF)
                    sp.dma_start(dram["att_dot"][0, rows:rows + P], high[:, r % 2]).then_inc(stored[r % 2], 16)
                    sp.dma_start(dram["att_dot"][1, rows:rows + P], rest[:, r % 2]).then_inc(stored[r % 2], 16)
                for slot in range(2):
                    sp.wait_ge(stored[slot], len(steps) // HALF * 16)

            @block.tensor
            def _(pe):
                pe.wait_ge(loaded, 64)
                for k, (w, tile, n) in enumerate(steps):
                    if k >= 4:
                        pe.wait_ge(qk_ready, k - 3)
                    for t in range(CT):
                        mm = nc.tensor.matmul(acc[:, k % 4], w_qk[:, w, t, tile * P:(tile + 1) * P], xn[:, t, tokens(n)],
                                              start=t == 0, stop=t == CT - 1)
                    mm.then_inc(acc_ready, 1)
                for i in range(N // P):
                    k = len(steps) + i
                    if i < 4:
                        pe.wait_ge(qk_ready, k - 3)
                    else:
                        pe.wait_ge(v_ready, i - 3)
                    for t in range(CT):
                        mm = nc.tensor.matmul(acc[:, k % 4, 0:D], xn[:, t, i * P:(i + 1) * P], w_v[:, t], start=t == 0, stop=t == CT - 1)
                    mm.then_inc(acc_ready, 1)

            @block.scalar
            def _(act):
                for k, (w, tile, n) in enumerate(steps):
                    act.wait_ge(acc_ready, k + 1)
                    nc.scalar.activation(qk[:, tile, w, tokens(n)], acc[:, k % 4], ACT.Identity,
                                         bias=b_qk[:, w, tile:tile + 1]).then_inc(qk_ready, 1)

            @block.vector
            def _(dve):
                for k, (w, tile, n) in enumerate(steps):
                    r, at = divmod(k, HALF)
                    scale = 1.0 if w else DOT_SCALE
                    dve.wait_ge(qk_ready, k + 1)
                    if r >= 2:
                        dve.wait_ge(stored[r % 2], r // 2 * 32)
                    nc.vector.tensor_scalar(high[:, r % 2, tokens(at)], qk[:, tile, w, tokens(n)], scale, None, ALU.mult).then_inc(high_ready, 1)
                    dve.wait_ge(high_ready, k + 1)
                    nc.vector.scalar_tensor_tensor(rest[:, r % 2, tokens(at)], qk[:, tile, w, tokens(n)], scale,
                                                   high[:, r % 2, tokens(at)], ALU.mult, ALU.subtract).then_inc(rest_ready, 1)
                for i in range(N // P):
                    k = len(steps) + i
                    dve.wait_ge(acc_ready, k + 1)
                    nc.vector.tensor_tensor(v_sum[:, i % 2], acc[:, k % 4, 0:D], b_v[:], ALU.add).then_inc(v_ready, 1)
                    by_head = v_sum[:, i % 2].rearrange("p (h d) -> p h d", h=HEADS)
                    columns = v[:, i // QT * HEADS:(i // QT + 1) * HEADS, i % QT]
                    dve.wait_ge(v_ready, i + 1)
                    nc.vector.tensor_scalar(columns[:, :, 0:HD], by_head, V_SCALE, None, ALU.mult).then_inc(v_step, 1)
                    dve.wait_ge(v_step, 2 * i + 1)
                    nc.vector.scalar_tensor_tensor(columns[:, :, HD:ONES], by_head, V_SCALE, columns[:, :, 0:HD],
                                                   ALU.mult, ALU.subtract).then_inc(v_step, 1)
                nc.vector.memset(v[:, :, :, ONES], V_SCALE)


def helical_features(nc, c, dram, stage, qk):
    with Scope(nc, stage) as s:
        w_hel = s.sb("w", [P, CT, 2, 2, P])
        bias = s.sb("bias", [P, CT, 2, 2])
        raw = s.sb("raw", [P, 2, 2, BLK])
        squares = s.sb("squares", [P, 2, 2, BLK])
        norm_sq = s.sb("norm_sq", [P, 2, BLK])
        log_sq = s.sb("log_sq", [P, 2, BLK])
        inv = s.sb("inv", [P, 2, BLK])
        unit = s.sb("unit", [P, 2, 2, BLK])
        high = s.sb("high", [P, B, 2, 2, T // 2], F16)
        rest = s.sb("rest", [P, B, 2, 2, T // 2], F16)
        acc = s.ps("acc", [P, 2, 2, BLK])
        loaded, acc_ready, raw_ready, squares_ready = s.sem("loaded"), s.sem("acc_ready"), s.sem("raw_ready"), s.sem("squares_ready")
        norm_ready, log_ready, inv_ready, unit_ready = s.sem("norm_ready"), s.sem("log_ready"), s.sem("inv_ready"), s.sem("unit_ready")
        high_ready, rest_ready = s.sem("high_ready"), s.sem("rest_ready")
        stored = [s.sem(f"stored{b}") for b in range(B)]
        CREDIT = 2
        STEPS = T // BLK
        ROUNDS = 2 * CT * 2

        def number(group, w, b, n):
            return ((w + group * 2) * B + b) * STEPS + n

        with nc.Block() as block:

            @block.sync
            def _(sp):
                sp.dma_start(w_hel[:], dram["att_hel_w"]).then_inc(loaded, 16)
                sp.dma_start(bias[:], dram["att_hel_b"]).then_inc(loaded, 16)
                for group in range(2 * CT):
                    with sp.Fori(0, 2) as w:
                        for b in range(B):
                            sp.wait_ge(rest_ready, number(group, w, b, STEPS) + CREDIT)
                            rows = bass.ds((w * B + b) * (HEADS * PAIRS) + group * P, P)
                            for parity in range(2):
                                for part, tile in ((0, high), (1, rest)):
                                    sp.dma_start(dram["att_hel"][part, parity, rows].rearrange("r (i u) -> r i u", i=2),
                                                 tile[:, b, :, parity]).then_inc(stored[b], 16)
                for b in range(B):
                    sp.wait_ge(stored[b], ROUNDS * 64 + 1)

            @block.tensor
            def _(pe):
                pe.wait_ge(loaded, 32)
                for group in range(2 * CT):
                    tile, half = divmod(group, 2)
                    with pe.Fori(0, 2) as w:
                        for b in range(B):
                            for n in range(STEPS):
                                k = number(group, w, b, n)
                                pe.wait_ge(raw_ready, k * 2 + 2)
                                pe.wait_ge(squares_ready, k * 2 + 2)
                                for comp in range(2):
                                    mm = nc.tensor.matmul(acc[:, n % 2, comp], w_hel[:, tile, half, comp],
                                                          qk[:, tile].rearrange("p w n -> p (w n)")[:, bass.ds(w * N + b * T + n * BLK, BLK)],
                                                          start=True, stop=True)
                                mm.then_inc(acc_ready, 1)

            @block.scalar
            def _(act):
                nc.scalar.preload_act_table_set(LOG_EXP_SET)
                act.sem_inc(raw_ready, 2 * CREDIT)
                act.sem_inc(squares_ready, 2 * CREDIT)
                act.sem_inc(log_ready, CREDIT)
                for group in range(2 * CT):
                    tile, half = divmod(group, 2)
                    with act.Fori(0, 2) as w:
                        for b in range(B):
                            for n in range(STEPS):
                                k = number(group, w, b, n)
                                act.wait_ge(acc_ready, k + 1)
                                act.wait_ge(norm_ready, k + 1)
                                for comp in range(2):
                                    nc.scalar.activation(squares[:, n % 2, comp], acc[:, n % 2, comp], ACT.Square,
                                                         bias=bias[:, tile, half, comp:comp + 1]).then_inc(squares_ready, 1)
                                act.wait_ge(unit_ready, k + 1)
                                for comp in range(2):
                                    nc.scalar.activation(raw[:, n % 2, comp], acc[:, n % 2, comp], ACT.Identity,
                                                         bias=bias[:, tile, half, comp:comp + 1]).then_inc(raw_ready, 1)
                                act.wait_ge(norm_ready, k + 1 + CREDIT)
                                nc.scalar.activation(log_sq[:, n % 2], norm_sq[:, n % 2], ACT.Ln).then_inc(log_ready, 1)
                                act.wait_ge(log_ready, k + 1 + CREDIT)
                                act.wait_ge(unit_ready, k + 1)
                                nc.scalar.activation(inv[:, n % 2], log_sq[:, n % 2], ACT.Exp, scale=-0.5).then_inc(inv_ready, 1)

            @block.vector
            def _(dve):
                dve.sem_inc(norm_ready, CREDIT)
                dve.sem_inc(unit_ready, CREDIT)
                for b in range(B):
                    dve.sem_inc(stored[b], 1)
                for group in range(2 * CT):
                    with dve.Fori(0, 2) as w:
                        for b in range(B):
                            for n in range(STEPS):
                                k = number(group, w, b, n)
                                half_blk = slice(n * BLK // 2, (n + 1) * BLK // 2)
                                dve.wait_ge(squares_ready, k * 2 + 2 + 2 * CREDIT)
                                dve.wait_ge(log_ready, k + 1)
                                nc.vector.tensor_tensor(norm_sq[:, n % 2], squares[:, n % 2, 0], squares[:, n % 2, 1], ALU.add).then_inc(norm_ready, 1)
                                dve.wait_ge(inv_ready, k + 1)
                                dve.wait_ge(rest_ready, k + 1)
                                nc.vector.scalar_tensor_tensor(unit[:, n % 2], over_tiles(inv[:, n % 2], 2), 1e12, raw[:, n % 2],
                                                               ALU.min, ALU.mult).then_inc(unit_ready, 1)
                                dve.wait_ge(unit_ready, k + 1 + CREDIT)
                                if n == 0:
                                    dve.wait_ge(stored[b], (w + group * 2) * 64 + 1)
                                nc.vector.tensor_copy(high[:, b, :, :, half_blk], unit[:, n % 2].rearrange("p i (u c) -> p i c u", c=2)).then_inc(high_ready, 1)

            @block.gpsimd
            def _(pool):
                pool.sem_inc(rest_ready, CREDIT)
                for group in range(2 * CT):
                    with pool.Fori(0, 2) as w:
                        for b in range(B):
                            for n in range(STEPS):
                                half_blk = slice(n * BLK // 2, (n + 1) * BLK // 2)
                                pool.wait_ge(high_ready, number(group, w, b, n) + 1)
                                nc.gpsimd.tensor_tensor(rest[:, b, :, :, half_blk], unit[:, n % 2].rearrange("p i (u c) -> p i c u", c=2),
                                                        high[:, b, :, :, half_blk], ALU.subtract).then_inc(rest_ready, 1)


def head_attention(nc, c, dram, stage, v):
    with Scope(nc, stage) as s:
        q = s.sb("q", [P, 2, 2, T], F16)
        k = s.sb("k", [P, 2, 2, T], F16)
        probs = s.sb("probs", [P, 2, T // 2])
        high = s.sb("high", [P, 4, T // 2], F16)
        rest = s.sb("rest", [P, 4, T // 2], F16)
        log_scale = s.sb("log_scale", [P, 1])
        v_head = s.sb("v_head", [P, 2, QT, V_COLS], F16)
        maxima = s.sb("maxima", [P, QT * 4])
        tile_max = s.sb("tile_max", [P, QT])
        shift = s.sb("shift", [P, QT])
        shift_row = s.sb("shift_row", [QT, P], F16)
        out_copy = s.sb("out_copy", [V_COLS, 2, T // 2])
        scores = s.ps("scores", [P, 2, T // 2])
        peek = s.ps("peek", [P, 2, BLK])
        out = s.ps("out", [P, T // 2])

        ones_ready = s.sem("ones_ready")
        loaded = [s.sem(f"loaded{slot}") for slot in range(2)]
        shift_stored = [s.sem(f"shift_stored{slot}") for slot in range(2)]
        out_stored = [s.sem(f"out_stored{half}") for half in range(2)]
        v_ready, peek_ready, peek_read = s.sem("v_ready"), s.sem("peek_ready"), s.sem("peek_read")
        max_step, shift_ready, shift_turned, shift_row_ready = s.sem("max_step"), s.sem("shift_ready"), s.sem("shift_turned"), s.sem("shift_row_ready")
        scores_ready, probs_ready, high_ready = s.sem("scores_ready"), s.sem("probs_ready"), s.sem("high_ready")
        rest_a_ready, rest_b_ready, weighed, out_copied = s.sem("rest_a_ready"), s.sem("rest_b_ready"), s.sem("weighed"), s.sem("out_copied")
        STEPS = 2 * QT
        AHEAD = 2
        PEEKS = QT * 4
        FIRST_PEEK = 4
        TURN_AT = FIRST_PEEK + (PEEKS + 2) // 3
        LOADS = 18 * 16
        SPLIT = 384
        W_CREDIT, H_CREDIT, R_CREDIT, K_CREDIT = 2 * STEPS, 2, 2, 2

        def peeks_at(step):
            first = 3 * (step - FIRST_PEEK)
            return range(first, min(first + 3, PEEKS)) if step >= FIRST_PEEK else range(0)

        with nc.Block() as block:

            @block.sync
            def _(sp):
                hel, dot = dram["att_hel"], dram["att_dot"]

                def load(pair, slot):
                    head = pair * 2 + slot
                    at_q, at_k = bass.ds(head * PAIRS, PAIRS), bass.ds(head * PAIRS + BH * PAIRS, PAIRS)
                    for parity in range(2):
                        rows = slice(parity * PAIRS, (parity + 1) * PAIRS)
                        more_rows = slice(HX + parity * PAIRS, HX + (parity + 1) * PAIRS)
                        for tile, rows_of, number, source in (
                                (q, rows, 0, hel[0, parity, at_q]), (k, rows, 0, hel[0, parity, at_k]),
                                (q, rows, 1, hel[0, parity, at_q]), (k, rows, 1, hel[1, parity, at_k]),
                                (q, more_rows, 1, hel[1, parity, at_q]), (k, more_rows, 1, hel[0, parity, at_k])):
                            sp.dma_start(tile[rows_of, slot, number], source).then_inc(loaded[slot], 16)
                    for part, (q_part, k_part) in enumerate(((0, 0), (0, 1), (1, 0))):
                        rows = slice(HX + part * HD, HX + (part + 1) * HD)
                        sp.dma_start(q[rows, slot, 0], dot[q_part, bass.ds(head * HD, HD)]).then_inc(loaded[slot], 16)
                        sp.dma_start(k[rows, slot, 0], dot[k_part, bass.ds(head * HD + BH * HD, HD)]).then_inc(loaded[slot], 16)

                def store_shift(pair, slot):
                    sp.wait_ge(shift_row_ready, pair * 2 + slot + 1)
                    sp.dma_start(q[MAX_ROW:MAX_ROW + 1, slot, 0].rearrange("a (t n) -> a t n", t=QT), shift_row[:]
                                 ).then_inc(shift_stored[slot], 16)

                def store_out(pair, slot, half):
                    head = pair * 2 + slot
                    queries = slice(half * T // 2, (half + 1) * T // 2)
                    sp.wait_ge(out_copied, head * 2 + half + 1 + 1)
                    for part in range(2):
                        sp.dma_start(dram["att_o"][part, bass.ds(head * HD, HD), queries], out_copy[part * HD:(part + 1) * HD, half]
                                     ).then_inc(out_stored[half], 16)
                    sp.dma_start(dram["att_sum"][bass.ds(head, 1), queries], out_copy[ONES:V_COLS, half]).then_inc(out_stored[half], 16)

                def follow(pair, slot, more_shift, more_load):
                    store_out(pair, slot, 0)
                    if more_shift:
                        store_shift(pair + slot, 1 - slot)
                    if more_load:
                        sp.wait_ge(scores_ready, (pair * 2 + slot + 1) * STEPS)
                        load(pair + 1, slot)
                    store_out(pair, slot, 1)

                sp.wait_ge(ones_ready, 2)
                load(0, 0)
                load(0, 1)
                store_shift(0, 0)
                with sp.Fori(0, BH // 2 - 1) as pair:
                    for slot in range(2):
                        follow(pair, slot, True, True)
                follow(BH // 2 - 1, 0, True, False)
                follow(BH // 2 - 1, 1, False, False)
                for half in range(2):
                    sp.wait_ge(out_stored[half], BH * 48 + 1)

            @block.gpsimd
            def _(pool):
                pool.sem_inc(rest_b_ready, R_CREDIT)
                with pool.Fori(0, BH // 2) as pair:
                    for slot in range(2):
                        head = pair * 2 + slot
                        pool.wait_ge(weighed, (head + 1) * STEPS)
                        nc.gpsimd.tensor_copy(v_head[:, slot], v[:, bass.ds(head, 1)].squeeze(1)).then_inc(v_ready, 1)
                        for step in range(STEPS):
                            pool.wait_ge(high_ready, head * STEPS + step + 1 + H_CREDIT)
                            nc.gpsimd.tensor_tensor(rest[:, step % 4, SPLIT:], probs[:, step % 2, SPLIT:], high[:, step % 4, SPLIT:],
                                                    ALU.subtract).then_inc(rest_b_ready, 1)

            @block.tensor
            def _(pe):
                def peek_scores(pair, slot, numbers):
                    head = pair * 2 + slot
                    for m in numbers:
                        tile, blk = divmod(m, 4)
                        if m == 0:
                            pe.wait_ge(loaded[slot], (pair + 1) * LOADS)
                        pe.wait_ge(peek_read, head * PEEKS + m + 1)
                        nc.tensor.matmul(peek[:, m % 2], q[0:MAX_ROW, slot, 0, tile * P:(tile + 1) * P], k[0:MAX_ROW, slot, 0, tokens(blk)],
                                         start=True, stop=True).then_inc(peek_ready, 1)

                def turn_shifts(pair, slot):
                    pe.wait_ge(shift_ready, pair * 2 + slot + 1)
                    nc.tensor.transpose(peek[0:QT, 0, 0:P], shift[:], c["identity"][:]).then_inc(shift_turned, 1)

                def score(pair, slot, step):
                    half, tile = divmod(step, QT)
                    head = pair * 2 + slot
                    if step == 0:
                        pe.wait_ge(shift_stored[slot], (pair + 1) * 16)
                    pe.wait_ge(high_ready, head * STEPS + step + 1)
                    for number, rows in ((1, P), (0, MAX_ROW + 1)):
                        for j in range(2):
                            mm = nc.tensor.matmul(scores[:, step % 2, tokens(j)], k[0:rows, slot, number, tile * P:(tile + 1) * P],
                                                  q[0:rows, slot, number, tokens(half * 2 + j)], start=number == 1, stop=number == 0)
                    mm.then_inc(scores_ready, 1)

                def weigh(pair, slot, step):
                    half, tile = divmod(step, QT)
                    head = pair * 2 + slot
                    if step == 0:
                        pe.wait_ge(v_ready, head + 1)
                    if tile == 0:
                        pe.wait_ge(out_copied, head * 2 + half + 1)
                    pe.wait_ge(rest_a_ready, head * STEPS + step + 1 + R_CREDIT)
                    pe.wait_ge(rest_b_ready, head * STEPS + step + 1 + R_CREDIT)
                    for part in (high, rest):
                        for j in range(2):
                            mm = nc.tensor.matmul(out[0:V_COLS, tokens(j)], v_head[:, slot, tile], part[:, step % 4, tokens(j)],
                                                  start=tile == 0 and part is high, stop=tile == QT - 1 and part is rest)
                    mm.then_inc(weighed, 1)

                def attend(pair, slot, more):
                    ahead = (pair + slot, 1 - slot)
                    for step in range(STEPS):
                        if step + AHEAD < STEPS:
                            score(pair, slot, step + AHEAD)
                        elif more:
                            score(*ahead, step + AHEAD - STEPS)
                        if more:
                            peek_scores(*ahead, peeks_at(step))
                        weigh(pair, slot, step)
                        if more and step == TURN_AT:
                            turn_shifts(*ahead)

                pe.sem_inc(weighed, W_CREDIT)
                peek_scores(0, 0, range(PEEKS))
                turn_shifts(0, 0)
                for step in range(AHEAD):
                    score(0, 0, step)
                with pe.Fori(0, BH // 2 - 1) as pair:
                    for slot in range(2):
                        attend(pair, slot, True)
                attend(BH // 2 - 1, 0, True)
                attend(BH // 2 - 1, 1, False)

            @block.scalar
            def _(act):
                def powers(head, step):
                    count = head * STEPS + step
                    act.wait_ge(scores_ready, count + 1)
                    act.wait_ge(rest_a_ready, count + 1)
                    act.wait_ge(rest_b_ready, count + 1)
                    nc.scalar.activation(probs[:, step % 2], scores[:, step % 2], ACT.Exp, bias=log_scale[:, 0:1], scale=LOGIT_SCALE).then_inc(probs_ready, 1)
                    act.wait_ge(weighed, count + 1 + W_CREDIT - 4)
                    nc.scalar.activation(high[:, step % 4], scores[:, step % 2], ACT.Exp, bias=log_scale[:, 0:1], scale=LOGIT_SCALE).then_inc(high_ready, 1)

                def copy_out(head, half):
                    act.wait_ge(weighed, head * STEPS + (half + 1) * QT + W_CREDIT)
                    act.wait_ge(out_stored[half], head * 48 + 1)
                    nc.scalar.activation(out_copy[:, half], out[0:V_COLS], ACT.Copy).then_inc(out_copied, 1)

                def turn(head, more):
                    for step in range(AHEAD, STEPS + AHEAD if more else STEPS):
                        powers(head, step)
                        if step == QT + AHEAD - 1:
                            copy_out(head, 0)
                    copy_out(head, 1)

                act.wait_ge(ones_ready, 3)
                act.sem_inc(high_ready, H_CREDIT)
                act.sem_inc(out_copied, 1)
                for step in range(AHEAD):
                    powers(0, step)
                with act.Fori(0, BH - 1) as head:
                    turn(head, True)
                turn(BH - 1, False)

            @block.vector
            def _(dve):
                def read_peeks(head, numbers):
                    for m in numbers:
                        dve.wait_ge(peek_ready, head * PEEKS + m + 1)
                        if m == 0:
                            dve.wait_ge(max_step, head + 1)
                        nc.vector.tensor_reduce(maxima[:, m:m + 1], peek[:, m % 2], AX.X, ALU.max).then_inc(peek_read, 1)

                def shifts(head):
                    dve.wait_ge(peek_read, (head + 1) * PEEKS + K_CREDIT)
                    nc.vector.tensor_reduce(tile_max[:], maxima[:].rearrange("p (t b) -> p t b", b=4), AX.X, ALU.max).then_inc(max_step, 1)
                    dve.wait_ge(max_step, head + 2)
                    nc.vector.tensor_scalar(shift[:], tile_max[:], -LOGIT_SCALE, None, ALU.mult).then_inc(shift_ready, 1)

                def shift_rows(pair, slot, stored):
                    head = pair * 2 + slot
                    dve.wait_ge(shift_turned, head + 1)
                    if stored:
                        dve.wait_ge(shift_stored[1 - slot], (pair + slot) * 16)
                    nc.vector.tensor_copy(shift_row[:], peek[0:QT, 0, 0:P]).then_inc(shift_row_ready, 1)

                def turn(pair, slot, more):
                    head = pair * 2 + slot
                    ahead = (pair + slot, 1 - slot)
                    for step in range(STEPS):
                        dve.wait_ge(high_ready, head * STEPS + step + 1 + H_CREDIT)
                        nc.vector.tensor_tensor(rest[:, step % 4, 0:SPLIT], probs[:, step % 2, 0:SPLIT], high[:, step % 4, 0:SPLIT],
                                                ALU.subtract).then_inc(rest_a_ready, 1)
                        if more:
                            read_peeks(head + 1, peeks_at(step))
                            if step == TURN_AT:
                                shifts(head + 1)
                            if step == TURN_AT + 1:
                                shift_rows(*ahead, True)

                for slot in range(2):
                    nc.vector.memset(k[96:P, slot, 0], 1.0 / LOGIT_SCALE).then_inc(ones_ready, 1)
                nc.vector.memset(log_scale[:], math.log(PROB_SCALE)).then_inc(ones_ready, 1)
                dve.sem_inc(peek_read, K_CREDIT)
                dve.sem_inc(max_step, 1)
                dve.sem_inc(rest_a_ready, R_CREDIT)
                for half in range(2):
                    dve.sem_inc(out_stored[half], 1)
                read_peeks(0, range(PEEKS))
                shifts(0)
                shift_rows(0, 0, False)
                with dve.Fori(0, BH // 2 - 1) as pair:
                    for slot in range(2):
                        turn(pair, slot, True)
                turn(BH // 2 - 1, 0, True)
                turn(BH // 2 - 1, 1, False)


def project_out(nc, c, dram, stage):
    x = c["x"]
    ROWS = P // BH
    with Scope(nc, stage) as s:
        w_o = s.sb("w_o", [P, CT, D])
        b_o = s.sb("b_o", [P, CT])
        sums = s.sb("sums", [P, T // ROWS])
        inv = s.sb("inv", [P, CT, N])
        parts = s.sb("parts", [P, 2, CT, N])
        acc = s.ps("acc", [P, 2, CT, BLK])
        sums_loaded, inverted, inv_stored, inv_loaded = s.sem("sums_loaded"), s.sem("inverted"), s.sem("inv_stored"), s.sem("inv_loaded")
        loaded, whole, att_ready, acc_ready, added = s.sem("loaded"), s.sem("whole"), s.sem("att_ready"), s.sem("acc_ready"), s.sem("added")

        with nc.Block() as block:

            @block.sync
            def _(sp):
                sp.dma_start(sums[:], dram["att_sum"].rearrange("h (r t) -> (h r) t", r=ROWS)).then_inc(sums_loaded, 16)
                sp.wait_ge(inverted, 1)
                sp.dma_start(dram["att_inv"].rearrange("h (r t) -> (h r) t", r=ROWS), sums[:]).then_inc(inv_stored, 16)
                sp.wait_ge(inv_stored, 16)
                for b in range(B):
                    for tile in range(CT):
                        first = b * HEADS + tile * HEADS // CT
                        sp.dma_start(inv[:, tile, b * T:(b + 1) * T],
                                     dram["att_inv"][first:first + HEADS // CT].unsqueeze(1).broadcast_to([HEADS // CT, HD, T])).then_inc(inv_loaded, 16)

            @block.scalar
            def _(act):
                act.dma_start(w_o[:], dram["att_w_o"]).then_inc(loaded, 16)
                act.dma_start(b_o[:], dram["att_b_o"]).then_inc(loaded, 16)
                for b in range(B):
                    for part in range(2):
                        for tile in range(CT):
                            act.dma_start(parts[:, part, tile, b * T:(b + 1) * T], dram["att_o"][part, b * D + tile * P:b * D + (tile + 1) * P]
                                          ).then_inc(loaded, 16)

            @block.tensor
            def _(pe):
                pe.wait_ge(loaded, (2 + 4 * B) * 16)
                for n in range(NBLK):
                    pe.wait_ge(att_ready, n + 1)
                    if n >= 2:
                        pe.wait_ge(added, (n - 1) * CT)
                    for o in range(CT):
                        for tile in range(CT):
                            mm = nc.tensor.matmul(acc[:, n % 2, o], w_o[:, tile, o * P:(o + 1) * P], parts[:, 0, tile, tokens(n)],
                                                  start=tile == 0, stop=tile == CT - 1)
                        mm.then_inc(acc_ready, 1)

            @block.vector
            def _(dve):
                def add(n):
                    for o in range(CT):
                        dve.wait_ge(acc_ready, n * CT + o + 1)
                        nc.vector.scalar_tensor_tensor(x[:, o, tokens(n)], acc[:, n % 2, o], b_o[:, o:o + 1], x[:, o, tokens(n)],
                                                       ALU.add, ALU.add).then_inc(added, 1)

                dve.wait_ge(sums_loaded, 16)
                nc.vector.reciprocal(sums[:], sums[:]).then_inc(inverted, 1)
                dve.wait_ge(loaded, (2 + 4 * B) * 16)
                for n in range(NBLK):
                    nc.vector.tensor_tensor(parts[:, 0, :, tokens(n)], parts[:, 0, :, tokens(n)], parts[:, 1, :, tokens(n)], ALU.add).then_inc(whole, 1)
                dve.wait_ge(inv_loaded, 16 * B * CT)
                for n in range(NBLK):
                    dve.wait_ge(whole, n + 1)
                    nc.vector.tensor_tensor(parts[:, 0, :, tokens(n)], parts[:, 0, :, tokens(n)], inv[:, :, tokens(n)], ALU.mult).then_inc(att_ready, 1)
                    if n >= 1:
                        add(n - 1)
                add(NBLK - 1)


def helical_attention(nc, c, dram, stage):
    dram["att_dot"] = nc.dram_tensor("att_dot", (2, 2 * BH * HD, T), F16, kind="Internal").ap()
    dram["att_hel"] = nc.dram_tensor("att_hel", (2, 2, 2 * BH * PAIRS, T), F16, kind="Internal").ap()
    dram["att_o"] = nc.dram_tensor("att_o", (2, BH * HD, T), F32, kind="Internal").ap()
    dram["att_sum"] = nc.dram_tensor("att_sum", (BH, T), F32, kind="Internal").ap()
    dram["att_inv"] = nc.dram_tensor("att_inv", (BH, T), F32, kind="Internal").ap()
    with Scope(nc, stage) as s:
        v = s.sb("v", [P, BH, QT, V_COLS], F16)
        with Scope(nc, f"{stage}_prepare") as prepare:
            qk = prepare.sb("qk", [P, CT, 2, N])
            with Scope(nc, f"{stage}_normed") as normed:
                xn = normed.sb("xn", [P, CT, N])
                layer_norm(nc, c, f"{stage}_ln", xn, None)
                project_qkv(nc, c, dram, f"{stage}_qkv", xn, qk, v)
            helical_features(nc, c, dram, f"{stage}_hel", qk)
        head_attention(nc, c, dram, f"{stage}_heads", v)
    project_out(nc, c, dram, f"{stage}_out")

TAPS = 4
ALPHA_MIN = 0.1
RMS_EPS = 1e-6
QUARTERS = 4
JQ = 16 // QUARTERS
SPAN = 64
GROUP = 16


def delta_gates(nc, c, dram, stage, xn):
    with Scope(nc, stage) as s:
        w_ab = s.sb("w_ab", [P, CT, 2 * HEADS])
        b_ab = s.sb("b_ab", [2 * HEADS, 2])
        w_down = s.sb("w_down", [P, CT, P])
        w_up = s.sb("w_up", [P, D])
        ab = s.sb("ab", [2 * HEADS, N])
        down = s.sb("down", [P, 2, BLK])
        gate = s.sb("gate", [P, CT, N])
        acc = s.ps("acc", [P, 2, BLK])
        acc_down = s.ps("acc_down", [P, 2, BLK])
        acc_up = s.ps("acc_up", [P, 2, CT, BLK])
        loaded, ab_sum, ab_ready, ab_clipped = s.sem("loaded"), s.sem("ab_sum"), s.sem("ab_ready"), s.sem("ab_clipped")
        down_sum, down_ready, up_sum, gate_ready, stored = s.sem("down_sum"), s.sem("down_ready"), s.sem("up_sum"), s.sem("gate_ready"), s.sem("stored")

        with nc.Block() as block:

            @block.sync
            def _(sp):
                for tile, table in ((w_ab, "delta_w_ab"), (b_ab, "delta_b_ab"), (w_down, "delta_w_down"), (w_up, "delta_w_up")):
                    sp.dma_start(tile[:], dram[table]).then_inc(loaded, 16)
                sp.wait_ge(ab_clipped, NBLK)
                for b in range(B):
                    sp.dma_start(dram["delta_ab"][b], ab[:, b * T:(b + 1) * T]).then_inc(stored, 16)
                sp.wait_ge(gate_ready, NBLK * CT)
                sp.dma_start(dram["delta_gate"], gate[:]).then_inc(stored, 16)
                sp.wait_ge(stored, (B + 1) * 16)

            @block.tensor
            def _(pe):
                pe.wait_ge(loaded, 64)
                for n in range(NBLK + 1):
                    if n < NBLK:
                        if n >= 2:
                            pe.wait_ge(ab_ready, n - 1)
                            pe.wait_ge(down_ready, n - 1)
                        for t in range(CT):
                            mm = nc.tensor.matmul(acc[0:2 * HEADS, n % 2], w_ab[:, t], xn[:, t, tokens(n)], start=t == 0, stop=t == CT - 1)
                        mm.then_inc(ab_sum, 1)
                        for t in range(CT):
                            mm = nc.tensor.matmul(acc_down[:, n % 2], w_down[:, t], xn[:, t, tokens(n)], start=t == 0, stop=t == CT - 1)
                        mm.then_inc(down_sum, 1)
                    if n >= 1:
                        pe.wait_ge(down_ready, n)
                        if n >= 3:
                            pe.wait_ge(gate_ready, (n - 2) * CT)
                        for o in range(CT):
                            nc.tensor.matmul(acc_up[:, (n - 1) % 2, o], w_up[:, o * P:(o + 1) * P], down[:, (n - 1) % 2],
                                             start=True, stop=True).then_inc(up_sum, 1)

            @block.scalar
            def _(act):
                def gates(act, n):
                    for o in range(CT):
                        act.wait_ge(up_sum, n * CT + o + 1)
                        nc.scalar.activation(gate[:, o, tokens(n)], acc_up[:, n % 2, o], ACT.Sigmoid).then_inc(gate_ready, 1)

                act.wait_ge(loaded, 64)
                for n in range(NBLK):
                    act.wait_ge(ab_sum, n + 1)
                    nc.scalar.activation(ab[:, tokens(n)], acc[0:2 * HEADS, n % 2], ACT.Sigmoid, bias=b_ab[:, 0:1]).then_inc(ab_ready, 1)
                    act.wait_ge(down_sum, n + 1)
                    if n >= 2:
                        act.wait_ge(up_sum, (n - 1) * CT)
                    nc.scalar.activation(down[:, n % 2], acc_down[:, n % 2], ACT.Silu).then_inc(down_ready, 1)
                    if n >= 1:
                        gates(act, n - 1)
                gates(act, NBLK - 1)

            @block.vector
            def _(dve):
                for n in range(NBLK):
                    dve.wait_ge(ab_ready, n + 1)
                    nc.vector.tensor_scalar(ab[:, tokens(n)], ab[:, tokens(n)], b_ab[:, 1:2], 1.0, ALU.max, ALU.min).then_inc(ab_clipped, 1)


def delta_projections(nc, c, dram, stage, xn, qkv):
    with Scope(nc, stage) as s:
        w_in = s.sb("w_in", [P, 3, CT, D])
        taps = s.sb("taps", [P, 3, CT, TAPS + 1])
        pre = s.sb("pre", [P, 2, B, T + TAPS - 1])
        acc = s.ps("acc", [P, 4, BLK])
        loaded, zeroed, acc_ready, pre_ready, tap_done, silu_done = (
            s.sem("loaded"), s.sem("zeroed"), s.sem("acc_ready"), s.sem("pre_ready"), s.sem("tap_done"), s.sem("silu_done"))
        rounds = [(w, tile) for w in range(3) for tile in range(CT)]
        PER_ROUND = TAPS * B
        HALF = NBLK // B

        with nc.Block() as block:

            @block.sync
            def _(sp):
                sp.dma_start(w_in[:], dram["delta_w_in"]).then_inc(loaded, 16)
                sp.dma_start(taps[:], dram["delta_taps"]).then_inc(loaded, 16)

            @block.tensor
            def _(pe):
                pe.wait_ge(loaded, 32)
                for r, (w, tile) in enumerate(rounds):
                    for n in range(NBLK):
                        k = r * NBLK + n
                        if k >= 4:
                            pe.wait_ge(pre_ready, k - 3)
                        for t in range(CT):
                            mm = nc.tensor.matmul(acc[:, k % 4], w_in[:, w, t, tile * P:(tile + 1) * P], xn[:, t, tokens(n)],
                                                  start=t == 0, stop=t == CT - 1)
                        mm.then_inc(acc_ready, 1)

            @block.scalar
            def _(act):
                def silu(r):
                    w, tile = rounds[r]
                    for b in range(B):
                        act.wait_ge(tap_done, r * PER_ROUND + (TAPS - 1) * B + b + 1)
                        part = qkv[:, w, tile, b * T:(b + 1) * T]
                        nc.scalar.activation(part, part, ACT.Silu, bias=taps[:, w, tile, TAPS:TAPS + 1]).then_inc(silu_done, 1)

                act.wait_ge(zeroed, 1)
                for r in range(len(rounds)):
                    if r >= 2:
                        act.wait_ge(tap_done, (r - 1) * PER_ROUND)
                    for n in range(NBLK):
                        act.wait_ge(acc_ready, r * NBLK + n + 1)
                        at = TAPS - 1 + n % HALF * BLK
                        nc.scalar.activation(pre[:, r % 2, n // HALF, at:at + BLK], acc[:, (r * NBLK + n) % 4], ACT.Copy).then_inc(pre_ready, 1)
                    if r >= 1:
                        silu(r - 1)
                silu(len(rounds) - 1)

            @block.vector
            def _(dve):
                nc.vector.memset(pre[:, :, :, 0:TAPS - 1], 0.0).then_inc(zeroed, 1)
                for r, (w, tile) in enumerate(rounds):
                    for tap in range(TAPS):
                        for b in range(B):
                            part = qkv[:, w, tile, b * T:(b + 1) * T]
                            moved = pre[:, r % 2, b, tap:tap + T]
                            if tap == 0:
                                dve.wait_ge(pre_ready, r * NBLK + (b + 1) * HALF)
                                ins = nc.vector.tensor_scalar(part, moved, taps[:, w, tile, tap:tap + 1], None, ALU.mult)
                            else:
                                dve.wait_ge(tap_done, r * PER_ROUND + (tap - 1) * B + b + 1)
                                ins = nc.vector.scalar_tensor_tensor(part, moved, taps[:, w, tile, tap:tap + 1], part, ALU.mult, ALU.add)
                            ins.then_inc(tap_done, 1)


def delta_normalise(nc, c, dram, stage, qkv, xn_space):
    with Scope(nc, stage) as s:
        ab = s.sb("ab", [2 * HEADS, B, T])
        spread = s.sb("spread", [2 * HEADS, CT, P])
        squares = s.sb("squares", [P, 2, BLK])
        log_sq = s.sb("log_sq", [P, 2, BLK])
        inv = s.sb("inv", [P, 2, BLK])
        scaled = xn_space
        sums = s.ps("sums", [P, 2, BLK])
        beta = s.ps("beta", [P, 2, BLK])
        loaded, squares_ready, sums_ready, log_ready, inv_ready, unit_ready = (
            s.sem("loaded"), s.sem("squares_ready"), s.sem("sums_ready"), s.sem("log_ready"), s.sem("inv_ready"), s.sem("unit_ready"))
        beta_ready, scaled_ready, negated, stored = s.sem("beta_ready"), s.sem("scaled_ready"), s.sem("negated"), s.sem("stored")
        steps = [(w, tile, n) for w in range(2) for tile in range(CT) for n in range(NBLK)]
        beta_steps = [(tile, n) for tile in range(CT) for n in range(NBLK)]

        with nc.Block() as block:

            @block.sync
            def _(sp):
                def put(sp, name, tiles):
                    for b in range(B):
                        for tile in range(CT):
                            sp.dma_start(dram[name][b, :, tile * P:(tile + 1) * P].rearrange("r p t -> p r t"),
                                         tiles[:, tile, b * T:(b + 1) * T].rearrange("p (r t) -> p r t", t=SPAN)).then_inc(stored, 16)

                for b in range(B):
                    sp.dma_start(ab[:, b], dram["delta_ab"][b]).then_inc(loaded, 16)
                sp.dma_start(spread[:], dram["delta_spread"]).then_inc(loaded, 16)
                sp.wait_ge(negated, CT)
                put(sp, "delta_v", qkv[:, 2])
                sp.wait_ge(unit_ready, len(steps))
                put(sp, "delta_q", qkv[:, 0])
                put(sp, "delta_k", qkv[:, 1])
                sp.wait_ge(scaled_ready, len(beta_steps))
                put(sp, "delta_kb", scaled)
                sp.wait_ge(stored, 4 * CT * B * 16)

            @block.tensor
            def _(pe):
                for k, (w, tile, n) in enumerate(steps):
                    pe.wait_ge(squares_ready, k + 1)
                    if k >= 2:
                        pe.wait_ge(log_ready, k - 1)
                    nc.tensor.matmul(sums[:, k % 2], c["head_sum"][:], squares[:, k % 2], start=True, stop=True).then_inc(sums_ready, 1)
                pe.wait_ge(loaded, 48)
                for k, (tile, n) in enumerate(beta_steps):
                    if k >= 2:
                        pe.wait_ge(scaled_ready, k - 1)
                    nc.tensor.matmul(beta[:, k % 2], spread[:, tile], ab[:].rearrange("p b t -> p (b t)")[:, tokens(n)],
                                     start=True, stop=True).then_inc(beta_ready, 1)

            @block.scalar
            def _(act):
                def lengths(k):
                    act.wait_ge(sums_ready, k + 1)
                    nc.scalar.activation(log_sq[:, k % 2], sums[:, k % 2], ACT.Ln).then_inc(log_ready, 1)
                    act.wait_ge(log_ready, k + 1)
                    if k >= 2:
                        act.wait_ge(unit_ready, k - 1)
                    nc.scalar.activation(inv[:, k % 2], log_sq[:, k % 2], ACT.Exp, scale=-0.5).then_inc(inv_ready, 1)

                nc.scalar.preload_act_table_set(LOG_EXP_SET)
                for k, (w, tile, n) in enumerate(steps):
                    if k >= 2:
                        act.wait_ge(sums_ready, k - 1)
                    nc.scalar.activation(squares[:, k % 2], qkv[:, w, tile, tokens(n)], ACT.Square).then_inc(squares_ready, 1)
                    if k >= 1:
                        lengths(k - 1)
                lengths(len(steps) - 1)

            @block.vector
            def _(dve):
                for tile in range(CT):
                    nc.vector.tensor_scalar(qkv[:, 2, tile], qkv[:, 2, tile], -1.0, None, ALU.mult).then_inc(negated, 1)
                for k, (w, tile, n) in enumerate(steps):
                    dve.wait_ge(inv_ready, k + 1)
                    part = qkv[:, w, tile, tokens(n)]
                    nc.vector.scalar_tensor_tensor(part, inv[:, k % 2], 1e6, part, ALU.min, ALU.mult).then_inc(unit_ready, 1)
                for k, (tile, n) in enumerate(beta_steps):
                    dve.wait_ge(beta_ready, k + 1)
                    dve.wait_ge(unit_ready, (CT + tile) * NBLK + n + 1)
                    nc.vector.tensor_tensor(scaled[:, tile, tokens(n)], qkv[:, 1, tile, tokens(n)], beta[:, k % 2], ALU.mult).then_inc(scaled_ready, 1)


def delta_recurrence(nc, c, dram, stage):
    with Scope(nc, stage) as s:
        kt = s.sb("kt", [P, 2, 16, SPAN])
        kb = s.sb("kb", [P, 2, 16, SPAN])
        qt = s.sb("qt", [P, 2, 16, SPAN])
        vt = s.sb("vt", [P, 2, JQ, SPAN])
        at = s.sb("at", [P, 2, SPAN])
        RING = 2 * GROUP
        state = s.sb("state", [P, RING, JQ, 16])
        terms = s.sb("terms", [P, RING, JQ, 16 + 1])
        error = s.sb("error", [P, 2, JQ])
        outer = s.sb("outer", [P, 2, JQ, 16])
        o_terms = s.sb("o_terms", [P, 2, GROUP, JQ, 16])
        o_out = s.sb("o_out", [P, 2, JQ, SPAN])
        loaded = [s.sem(f"loaded{slot}") for slot in range(2)]
        stored = [s.sem(f"stored{slot}") for slot in range(2)]
        chain, v_ready, o_terms_ready, o_ready = s.sem("chain"), s.sem("v_ready"), s.sem("o_terms_ready"), s.sem("o_ready")
        GROUPS = SPAN // GROUP
        ROUNDS = T // SPAN
        LOADS = 5 * B * 16
        STEP = 4
        C0 = 1 + STEP * RING

        with nc.Block() as block:

            @block.sync
            def _(sp):
                def load(pair, slot):
                    for b in range(B):
                        half = slice(b * P // B, (b + 1) * P // B)
                        chunk = bass.ds(pair * 2 + slot, 1)
                        for tile, name in ((kt, "delta_k"), (kb, "delta_kb"), (qt, "delta_q")):
                            sp.dma_start(tile[half, slot], dram[name][b, chunk].rearrange("r (h i) t -> (r h) (i t)", i=16).unsqueeze(1)
                                         .broadcast_to([HEADS, QUARTERS, 16 * SPAN])).then_inc(loaded[slot], 16)
                        sp.dma_start(vt[half, slot], dram["delta_v"][b, chunk].rearrange("r (p j) t -> (r p) (j t)", j=JQ)).then_inc(loaded[slot], 16)
                        sp.dma_start(at[half, slot], dram["delta_ab"][b, 0:HEADS][:, bass.ds((pair * 2 + slot) * SPAN, SPAN)].unsqueeze(1)
                                     .broadcast_to([HEADS, QUARTERS, SPAN])).then_inc(loaded[slot], 16)

                def store(pair, slot):
                    sp.wait_ge(o_ready, (pair * 2 + slot + 3) * GROUPS)
                    for b in range(B):
                        half = slice(b * P // B, (b + 1) * P // B)
                        sp.dma_start(dram["delta_o"][b, bass.ds(pair * 2 + slot, 1)].rearrange("r (p j) t -> (r p) (j t)", j=JQ),
                                     o_out[half, slot]).then_inc(stored[slot], 16)

                for slot in range(2):
                    load(0, slot)
                with sp.Fori(1, ROUNDS // 2) as pair:
                    for slot in range(2):
                        store(pair - 1, slot)
                        load(pair, slot)
                for slot in range(2):
                    store(ROUNDS // 2 - 1, slot)
                for slot in range(2):
                    sp.wait_ge(stored[slot], ROUNDS // 2 * 32 + 32)

            @block.scalar
            def _(act):
                with act.Fori(0, ROUNDS // 2) as pair:
                    for slot in range(2):
                        act.wait_ge(loaded[slot], (pair + 1) * LOADS)
                        for g in range(GROUPS):
                            ring = g % 2 * GROUP
                            act.wait_ge(chain, ((pair * 2 + slot) * GROUPS + g) * GROUP * STEP + C0 - GROUP * STEP)
                            nc.scalar.activation(terms[:, ring:ring + GROUP, :, 16], vt[:, slot, :, g * GROUP:(g + 1) * GROUP]
                                                 .rearrange("p j t -> p t j"), ACT.Copy).then_inc(v_ready, 1)

            @block.gpsimd
            def _(pool):
                with pool.Fori(0, ROUNDS // 2) as pair:
                    for slot in range(2):
                        pool.wait_ge(loaded[slot], (pair + 1) * LOADS)
                        for g in range(GROUPS):
                            number = (pair * 2 + slot) * GROUPS + g
                            ring = g % 2 * GROUP
                            pool.wait_ge(chain, (number + 1) * GROUP * STEP + C0)
                            pool.wait_ge(o_ready, number + 2 * GROUPS - 1)
                            nc.gpsimd.tensor_tensor(o_terms[:, g % 2], state[:, ring:ring + GROUP],
                                                    qt[:, slot, :, g * GROUP:(g + 1) * GROUP].rearrange("p i t -> p t i").unsqueeze(2)
                                                    .broadcast_to([P, GROUP, JQ, 16]), ALU.mult).then_inc(o_terms_ready, 1)

            @block.vector
            def _(dve):
                def outputs(pair, slot, g):
                    dve.wait_ge(o_terms_ready, (pair * 2 + slot) * GROUPS + g + 1)
                    if g == 0:
                        dve.wait_ge(stored[slot], pair * 32 + 32)
                    nc.vector.tensor_reduce(o_out[:, slot, :, g * GROUP:(g + 1) * GROUP].rearrange("p j t -> p t j"), o_terms[:, g % 2],
                                            AX.X, ALU.add).then_inc(o_ready, 1)

                dve.sem_inc(chain, C0 - 1)
                dve.wait_ge(chain, C0 - 1)
                nc.vector.memset(state[:, RING - 1], 0.0).then_inc(chain, 1)
                dve.sem_inc(o_ready, 2 * GROUPS)
                for slot in range(2):
                    dve.sem_inc(stored[slot], 32)
                with dve.Fori(0, ROUNDS // 2) as pair:
                    for slot in range(2):
                        for g in range(GROUPS):
                            number = (pair * 2 + slot) * GROUPS + g
                            dve.wait_ge(v_ready, number + 1)
                            for u in range(GROUP):
                                step = g * GROUP + u
                                at_ring = step % RING
                                before = (step - 1) % RING
                                done = number * GROUP * STEP + u * STEP + C0
                                k_row = kt[:, slot, :, step].unsqueeze(1).broadcast_to([P, JQ, 16])
                                kb_row = kb[:, slot, :, step].unsqueeze(1).broadcast_to([P, JQ, 16])
                                dve.wait_ge(chain, done)
                                nc.vector.tensor_tensor(terms[:, at_ring, :, 0:16], state[:, before], k_row, ALU.mult).then_inc(chain, 1)
                                dve.wait_ge(chain, done + 1)
                                nc.vector.tensor_reduce(error[:, u % 2], terms[:, at_ring], AX.X, ALU.add, negate=True).then_inc(chain, 1)
                                dve.wait_ge(chain, done + 2)
                                nc.vector.tensor_tensor(outer[:, u % 2], error[:, u % 2].unsqueeze(2).broadcast_to([P, JQ, 16]), kb_row,
                                                        ALU.mult).then_inc(chain, 1)
                                dve.wait_ge(chain, done + 3)
                                nc.vector.scalar_tensor_tensor(state[:, at_ring], state[:, before], at[:, slot, step:step + 1], outer[:, u % 2],
                                                               ALU.mult, ALU.add).then_inc(chain, 1)
                                if u == GROUP // 2 and g >= 1:
                                    outputs(pair, slot, g - 1)
                        outputs(pair, slot, GROUPS - 1)


def delta_output(nc, c, dram, stage):
    x = c["x"]
    with Scope(nc, stage) as s:
        o_all = s.sb("o_all", [P, CT, N])
        gate = s.sb("gate", [P, CT, N])
        w_o = s.sb("w_o", [P, CT, D])
        rms_w = s.sb("rms_w", [P, CT])
        eps = s.sb("eps", [P, 1])
        squares = s.sb("squares", [P, 2, CT, BLK])
        log_sq = s.sb("log_sq", [P, 2, CT, BLK])
        inv = s.sb("inv", [P, 2, CT, BLK])
        sums = s.ps("sums", [P, 2, CT, BLK])
        acc = s.ps("acc", [P, 2, CT, BLK])
        loaded, eps_ready, squares_ready, sums_ready, log_ready, inv_ready, step_done, acc_ready, added = (
            s.sem("loaded"), s.sem("eps_ready"), s.sem("squares_ready"), s.sem("sums_ready"), s.sem("log_ready"), s.sem("inv_ready"),
            s.sem("step_done"), s.sem("acc_ready"), s.sem("added"))

        with nc.Block() as block:

            @block.sync
            def _(sp):
                for tile in range(CT):
                    for b in range(B):
                        sp.dma_start(o_all[:, tile, b * T:(b + 1) * T].rearrange("p (r t) -> p r t", t=SPAN),
                                     dram["delta_o"][b, :, tile * P:(tile + 1) * P].rearrange("r p t -> p r t")).then_inc(loaded, 16)
                for tile, table in ((gate, "delta_gate"), (w_o, "delta_w_o"), (rms_w, "delta_rms_w")):
                    sp.dma_start(tile[:], dram[table]).then_inc(loaded, 16)

            @block.tensor
            def _(pe):
                for n in range(NBLK + 1):
                    if n < NBLK:
                        pe.wait_ge(squares_ready, n + 1)
                        if n >= 2:
                            pe.wait_ge(log_ready, n - 1)
                        for tile in range(CT):
                            mm = nc.tensor.matmul(sums[:, n % 2, tile], c["head_sum"][:], squares[:, n % 2, tile], start=True, stop=True)
                        mm.then_inc(sums_ready, 1)
                    if n >= 1:
                        pe.wait_ge(step_done, n * 2 * CT)
                        if n >= 3:
                            pe.wait_ge(added, n - 2)
                        for o in range(CT):
                            for tile in range(CT):
                                mm = nc.tensor.matmul(acc[:, (n - 1) % 2, o], w_o[:, tile, o * P:(o + 1) * P], o_all[:, tile, tokens(n - 1)],
                                                      start=tile == 0, stop=tile == CT - 1)
                        mm.then_inc(acc_ready, 1)

            @block.scalar
            def _(act):
                def lengths(n):
                    act.wait_ge(sums_ready, n + 1)
                    nc.scalar.activation(log_sq[:, n % 2], sums[:, n % 2], ACT.Ln, bias=eps[:, 0:1], scale=1.0 / 16).then_inc(log_ready, 1)
                    act.wait_ge(log_ready, n + 1)
                    if n >= 2:
                        act.wait_ge(step_done, (n - 1) * 2 * CT)
                    nc.scalar.activation(inv[:, n % 2], log_sq[:, n % 2], ACT.Exp, scale=-0.5).then_inc(inv_ready, 1)

                nc.scalar.preload_act_table_set(LOG_EXP_SET)
                act.wait_ge(eps_ready, 1)
                act.wait_ge(loaded, 16 * (CT * B + 3))
                for n in range(NBLK):
                    if n >= 2:
                        act.wait_ge(sums_ready, n - 1)
                    nc.scalar.activation(squares[:, n % 2], o_all[:, :, tokens(n)], ACT.Square).then_inc(squares_ready, 1)
                    if n >= 1:
                        lengths(n - 1)
                lengths(NBLK - 1)

            @block.vector
            def _(dve):
                nc.vector.memset(eps[:], RMS_EPS).then_inc(eps_ready, 1)
                dve.wait_ge(loaded, 16 * (CT * B + 3))
                for n in range(NBLK + 1):
                    if n < NBLK:
                        dve.wait_ge(inv_ready, n + 1)
                        for tile in range(CT):
                            nc.vector.scalar_tensor_tensor(inv[:, n % 2, tile], inv[:, n % 2, tile], rms_w[:, tile:tile + 1], gate[:, tile, tokens(n)],
                                                           ALU.mult, ALU.mult).then_inc(step_done, 1)
                        for tile in range(CT):
                            dve.wait_ge(step_done, n * 2 * CT + tile + 1)
                            nc.vector.tensor_tensor(o_all[:, tile, tokens(n)], o_all[:, tile, tokens(n)], inv[:, n % 2, tile], ALU.mult).then_inc(step_done, 1)
                    if n >= 1:
                        dve.wait_ge(acc_ready, n)
                        nc.vector.tensor_tensor(x[:, :, tokens(n - 1)], x[:, :, tokens(n - 1)], acc[:, (n - 1) % 2], ALU.add).then_inc(added, 1)


def delta_attention(nc, c, dram, stage):
    for name in ("delta_q", "delta_k", "delta_kb", "delta_v", "delta_o"):
        dram[name] = nc.dram_tensor(name, (B, T // SPAN, D, SPAN), F32, kind="Internal").ap()
    dram["delta_ab"] = nc.dram_tensor("delta_ab", (B, 2 * HEADS, T), F32, kind="Internal").ap()
    dram["delta_gate"] = nc.dram_tensor("delta_gate", (P, CT, N), F32, kind="Internal").ap()
    with Scope(nc, stage) as normed:
        xn = normed.sb("xn", [P, CT, N])
        layer_norm(nc, c, f"{stage}_ln", xn, None)
        delta_gates(nc, c, dram, f"{stage}_gates", xn)
        with Scope(nc, f"{stage}_qkv") as s:
            qkv = s.sb("qkv", [P, 3, CT, N])
            delta_projections(nc, c, dram, f"{stage}_in", xn, qkv)
            delta_normalise(nc, c, dram, f"{stage}_unit", qkv, xn)
    delta_recurrence(nc, c, dram, f"{stage}_scan")
    delta_output(nc, c, dram, f"{stage}_out")



def build(nc, dram):
    with Scope(nc, "main") as s:
        c = {
            "x": s.sb("x", [P, CT, N]),
            "mean_matrix": s.sb("mean_matrix", [P, P]),
            "identity": s.sb("identity", [P, P]),
            "head_mask": s.sb("head_mask", [P, 8]),
            "head_sum": s.sb("head_sum", [P, P]),
            "ln_eps": s.sb("ln_eps", [P, 1]),
        }
        load_constants(nc, c, dram)
        gated_experts(nc, c, dram, "ffn0")
        delta_attention(nc, c, dram, "delta")
        gated_experts(nc, c, dram, "ffn1")
        prototype_mixture(nc, c, dram, "mix0")
        helical_attention(nc, c, dram, "att")
        prototype_mixture(nc, c, dram, "mix1")
        store_result(nc, c, dram)


def lay_out(inputs):
    import numpy as np

    def rows(a):
        return np.ascontiguousarray(a.reshape(CT, P, -1).transpose(1, 0, 2))

    def helical_weights(w):
        out = np.zeros((8, HD, CT, 2, 2, QG, PAIRS), np.float32)
        for head in range(HEADS):
            tile, of_eight = divmod(head, 8)
            half, of_four = divmod(of_eight, QG)
            out[of_eight, :, tile, half, :, of_four] = w[head].reshape(PAIRS, 2, HD).transpose(2, 1, 0)
        return out.reshape(P, CT, 2, 2, P)

    arrays = {
        "x": rows(inputs["L0_attn_x"].reshape(N, D).T),
        "mean_matrix": np.full((P, P), 1.0 / D, np.float32),
        "identity": np.eye(P, dtype=np.float32),
        "head_mask": np.kron(np.eye(8, dtype=np.float32), np.ones((16, 1), np.float32)),
        "head_sum": np.kron(np.eye(8, dtype=np.float32), np.ones((16, 16), np.float32)),
        "gate_w": rows(inputs["L0_ffn_gate_w"].T),
        "gate_b": np.tile(inputs["L0_ffn_gate_b"], (P, 1)),
        "expert": np.concatenate([
            inputs["L0_ffn_expert_w"].transpose(0, 2, 1).reshape(-1, CT, P, D).transpose(2, 0, 1, 3).reshape(P, -1, CT * D),
            inputs["L0_ffn_expert_b"].reshape(-1, CT, P).transpose(2, 0, 1)], axis=2),
        "proto": rows(inputs["L1_ffn_prototypes"].T),
        "proto_rows": inputs["L1_ffn_prototypes"],
        "temp": np.full((P, 1), inputs["L1_ffn_temp"]),
        "numbers": np.tile(np.arange(inputs["L1_ffn_prototypes"].shape[0], dtype=np.float32), (P, 1)),
        "proto_B": rows(inputs["L1_ffn_B"].reshape(-1, D).T),
        "proto_A": np.ascontiguousarray(inputs["L1_ffn_A"].transpose(0, 2, 1).reshape(-1, P, D).transpose(1, 0, 2)),
        "proto_bias": inputs["L1_ffn_bias"],
        "proto_spread": np.kron(np.eye(inputs["L1_ffn_B"].shape[0], dtype=np.float32), np.ones((1, inputs["L1_ffn_B"].shape[1]), np.float32)),
        "att_w_qk": np.stack([rows(inputs["L1_attn_Wq"].T), rows(inputs["L1_attn_Wk"].T)], axis=1),
        "att_w_v": rows(inputs["L1_attn_Wv"].T),
        "att_b_qk": np.stack([inputs["L1_attn_bq"].reshape(CT, P), inputs["L1_attn_bk"].reshape(CT, P)]).transpose(2, 0, 1).copy(),
        "att_b_v": np.tile(inputs["L1_attn_bv"], (P, 1)),
        "att_w_o": rows(inputs["L1_attn_Wo"].T),
        "att_b_o": inputs["L1_attn_bo"].reshape(CT, P).T.copy(),
        "att_hel_w": helical_weights(inputs["L1_attn_Whel"]),
        "att_hel_b": np.ascontiguousarray(inputs["L1_attn_bhel"].reshape(CT, 2, QG, PAIRS, 2).transpose(2, 3, 0, 1, 4).reshape(P, CT, 2, 2)),
        "delta_w_in": np.stack([rows(inputs[f"L0_attn_W{n}"]) for n in "qkv"], axis=1),
        "delta_taps": np.stack([np.concatenate([inputs[f"L0_attn_{n}cw"], inputs[f"L0_attn_{n}cb"][:, None]], axis=1).reshape(CT, P, TAPS + 1)
                                for n in "qkv"]).transpose(2, 0, 1, 3).copy(),
        "delta_w_ab": np.concatenate([rows(inputs["L0_attn_Wa"]), rows(inputs["L0_attn_Wb"])], axis=2),
        "delta_b_ab": np.stack([np.concatenate([inputs["L0_attn_ba"], inputs["L0_attn_bb"]]),
                                np.repeat(np.array([ALPHA_MIN, 0.0], np.float32), HEADS)], axis=1),
        "delta_w_down": rows(inputs["L0_attn_Wgd"]),
        "delta_w_up": inputs["L0_attn_Wgu"],
        "delta_spread": np.concatenate([np.zeros((HEADS, D), np.float32), np.kron(np.eye(HEADS, dtype=np.float32), np.ones((1, HD), np.float32))]
                                       ).reshape(2 * HEADS, CT, P),
        "delta_w_o": rows(inputs["L0_attn_Wo"]),
        "delta_rms_w": inputs["L0_attn_rms_w"].reshape(CT, P).T.copy(),
    }
    return arrays


def kernel(**inputs):
    import numpy as np
    import concourse.bacc as bacc
    from concourse.bass_utils import run_bass_kernel_spmd

    nc = bacc.Bacc("TRN2", target_bir_lowering=False, num_devices=1)
    arrays, dram = {}, {}
    for name, a in lay_out({k: np.asarray(v) for k, v in inputs.items()}).items():
        arrays[f"in_{name}"] = a
        dram[name] = nc.dram_tensor(f"in_{name}", a.shape, mybir.dt.from_np(a.dtype), kind="ExternalInput").ap()
    dram["out"] = nc.dram_tensor("out_x", (P, CT, N), F32, kind="ExternalOutput").ap()
    build(nc, dram)
    r = run_bass_kernel_spmd(nc, [arrays], core_ids=[0])
    return r.results[0]["out_x"].transpose(1, 0, 2).reshape(D, N).T.reshape(B, T, D)
```

```python
import math
from contextlib import ExitStack

import concourse.bass as bass
from concourse import mybir

F32 = mybir.dt.float32
F16 = mybir.dt.float16
U32 = mybir.dt.uint32
ALU = mybir.AluOpType
ACT = mybir.ActivationFunctionType
AX = mybir.AxisListType

P = 128
B = 2
T = 2048
N = B * T
D = 256
CT = D // P
BLK = 512
NBLK = N // BLK
LN_EPS = 1e-5
LOG_EXP_SET = "natural_log_exp_and_others"


class Scope:

    def __init__(self, nc, stage):
        self.nc, self.stage, self.stack, self.semaphores = nc, stage, ExitStack(), []

    def __enter__(self):
        return self

    def __exit__(self, *error):
        if self.semaphores:
            self.nc.clear_and_free_semaphores(self.semaphores)
            self.nc.all_engine_barrier()
        return self.stack.__exit__(*error)

    def sb(self, name, shape, dtype=F32):
        return self.stack.enter_context(self.nc.sbuf_tensor(f"{self.stage}_{name}", shape, dtype))

    def ps(self, name, shape, dtype=F32):
        return self.stack.enter_context(self.nc.psum_tensor(f"{self.stage}_{name}", shape, dtype))

    def sem(self, name):
        self.semaphores.append(self.nc.alloc_semaphore(f"{self.stage}_{name}"))
        return self.semaphores[-1]


def tokens(i, size=BLK):
    return bass.ds(i * size, size)


def over_tiles(ap, tiles):
    return ap.unsqueeze(1).broadcast_to([ap.shape[0], tiles, ap.shape[1]])


def load_constants(nc, c, dram):
    loaded = nc.alloc_semaphore("constants_loaded")
    with nc.Block() as block:

        @block.sync
        def _(sp):
            for tile in range(CT):
                sp.dma_start(c["x"][:, tile, :], dram["x"][:, tile, :]).then_inc(loaded, 16)
            for name in ("mean_matrix", "identity", "head_mask", "head_sum"):
                sp.dma_start(c[name][:], dram[name]).then_inc(loaded, 16)
            sp.wait_ge(loaded, 16 * (CT + 4))

        @block.vector
        def _(dve):
            nc.vector.memset(c["ln_eps"][:], LN_EPS)


def store_result(nc, c, dram):
    stored = nc.alloc_semaphore("result_stored")
    with nc.Block() as block:

        @block.sync
        def _(sp):
            for tile in range(CT):
                sp.dma_start(dram["out"][:, tile, :], c["x"][:, tile, :]).then_inc(stored, 16)
            sp.wait_ge(stored, 16 * CT)


def layer_norm(nc, c, stage, xn, sums):
    x, mean_matrix = c["x"], c["mean_matrix"]
    with Scope(nc, stage) as s:
        mean = s.ps("mean", [P, 2, BLK])
        var = s.ps("var", [P, 2, BLK])
        centred = s.sb("centred", [P, 2, CT, BLK])
        squares = s.sb("squares", [P, 2, CT, BLK])
        log_var = s.sb("log_var", [P, 2, BLK])
        rstd = s.sb("rstd", [P, 2, BLK])
        mean_ready, centred_ready, squares_ready = s.sem("mean_ready"), s.sem("centred_ready"), s.sem("squares_ready")
        var_ready, log_ready, rstd_ready, normed = s.sem("var_ready"), s.sem("log_ready"), s.sem("rstd_ready"), s.sem("normed")
        CREDIT = 2

        with nc.Block() as block:

            @block.tensor
            def _(pe):
                with pe.Fori(0, NBLK // 2) as pair:
                    for slot in range(2):
                        pe.wait_ge(centred_ready, pair * 2 + slot + 1)
                        for tile in range(CT):
                            mm = nc.tensor.matmul(mean[:, slot], mean_matrix[:], x[:, tile, tokens(pair * 2 + slot)],
                                                  start=tile == 0, stop=tile == CT - 1)
                        mm.then_inc(mean_ready, 1)
                    for slot in range(2):
                        pe.wait_ge(squares_ready, pair * 2 + slot + 1)
                        pe.wait_ge(log_ready, pair * 2 + slot + 1)
                        for tile in range(CT):
                            mm = nc.tensor.matmul(var[:, slot], mean_matrix[:], squares[:, slot, tile],
                                                  start=tile == 0, stop=tile == CT - 1)
                        mm.then_inc(var_ready, 1)

            @block.scalar
            def _(act):
                nc.scalar.preload_act_table_set(LOG_EXP_SET)
                act.sem_inc(log_ready, CREDIT)
                with act.Fori(0, NBLK // 2) as pair:
                    for slot in range(2):
                        act.wait_ge(centred_ready, pair * 2 + slot + 1 + CREDIT)
                        act.wait_ge(log_ready, pair * 2 + slot + 1)
                        nc.scalar.activation(squares[:, slot], centred[:, slot], ACT.Square).then_inc(squares_ready, 1)
                    for slot in range(2):
                        act.wait_ge(var_ready, pair * 2 + slot + 1)
                        nc.scalar.activation(log_var[:, slot], var[:, slot], ACT.Ln,
                                             bias=c["ln_eps"][:, 0:1]).then_inc(log_ready, 1)
                        act.wait_ge(log_ready, pair * 2 + slot + 1 + CREDIT)
                        act.wait_ge(normed, (pair * 2 + slot) * CT + 1)
                        nc.scalar.activation(rstd[:, slot], log_var[:, slot], ACT.Exp, scale=-0.5).then_inc(rstd_ready, 1)

            @block.vector
            def _(dve):
                dve.sem_inc(centred_ready, CREDIT)
                dve.sem_inc(normed, 1 + CT)
                with dve.Fori(0, NBLK // 2) as pair:
                    for slot in range(2):
                        dve.wait_ge(mean_ready, pair * 2 + slot + 1)
                        dve.wait_ge(normed, (pair * 2 + slot) * CT + 1)
                        nc.vector.tensor_tensor(centred[:, slot], x[:, :, tokens(pair * 2 + slot)],
                                                over_tiles(mean[:, slot], CT), ALU.subtract).then_inc(centred_ready, 1)
                    for slot in range(2):
                        dve.wait_ge(rstd_ready, pair * 2 + slot + 1)
                        for tile in range(CT):
                            if sums is None:
                                mult = nc.vector.tensor_tensor(xn[:, tile, tokens(pair * 2 + slot)], centred[:, slot, tile],
                                                               rstd[:, slot], ALU.mult)
                            else:
                                mult = nc.vector.scalar_tensor_tensor(
                                    xn[:, tile, tokens(pair * 2 + slot)], centred[:, slot, tile], 1.0, rstd[:, slot],
                                    ALU.mult, ALU.mult, accum_out=sums[:, tile, bass.ds(pair * 2 + slot, 1)])
                            mult.then_inc(normed, 1)


def gated_experts(nc, c, dram, stage):
    E = dram["gate_w"].shape[2]
    x = c["x"]
    with Scope(nc, stage) as s:
        xn = s.sb("xn", [P, CT, N])
        sums = s.sb("sums", [P, CT, NBLK])
        layer_norm(nc, c, f"{stage}_ln", xn, sums)

        gate_w = s.sb("gate_w", [P, CT, E])
        gate_b = s.sb("gate_b", [P, E])
        expert = s.sb("expert", [P, 2, CT * D + CT])
        weights = expert[:, :, 0:CT * D].rearrange("p s (t d) -> p s t d", t=CT)
        bias = expert[:, :, CT * D:]
        hidden = s.sb("hidden", [P, 4, BLK])
        pooled = s.sb("pooled", [P, CT, B])
        terms = s.sb("terms", [P, CT, B, E])
        logits = s.sb("logits", [P, B, E])
        top = s.sb("top", [P, B, 8])
        minus_max = s.sb("minus_max", [P, B])
        chosen = s.sb("chosen", [P, B, E])
        powers = s.sb("powers", [P, B, E])
        total = s.sb("total", [P, B])
        gate = s.sb("gate", [P, B, E])
        logit_sum = s.ps("logit_sum", [P, B * E])
        pre = s.ps("pre", [P, 4, BLK])

        tables_loaded = s.sem("tables_loaded")
        expert_loaded = [s.sem(f"expert_loaded{slot}") for slot in range(2)]
        terms_ready, logits_ready, gate_step, powers_ready = s.sem("terms_ready"), s.sem("logits_ready"), s.sem("gate_step"), s.sem("powers_ready")
        pre_ready, hidden_ready, added = s.sem("pre_ready"), s.sem("hidden_ready"), s.sem("added")
        SLOTS = 4
        PER_EXPERT = NBLK * CT
        CREDIT = 2 * PER_EXPERT

        with nc.Block() as block:

            @block.sync
            def _(sp):
                for tile, table in ((gate_w, "gate_w"), (gate_b, "gate_b")):
                    sp.dma_start(tile[:], dram[table]).then_inc(tables_loaded, 16)
                with sp.Fori(0, E // 2) as pair:
                    for slot in range(2):
                        sp.wait_ge(pre_ready, (pair * 2 + slot + 1) * PER_EXPERT)
                        sp.wait_ge(hidden_ready, (pair * 2 + slot + 1) * PER_EXPERT)
                        sp.dma_start(expert[:, slot], dram["expert"][:, bass.ds(pair * 2 + slot, 1)].squeeze(1)
                                     ).then_inc(expert_loaded[slot], 16)

            @block.tensor
            def _(pe):
                pe.wait_ge(terms_ready, 1)
                for tile in range(CT):
                    mm = nc.tensor.matmul(logit_sum[:], c["mean_matrix"][:], terms[:, tile].rearrange("p b e -> p (b e)"),
                                          start=tile == 0, stop=tile == CT - 1)
                mm.then_inc(logits_ready, 1)
                pe.sem_inc(pre_ready, CREDIT)
                with pe.Fori(0, E // 2) as pair:
                    for u in range(2):
                        pe.wait_ge(expert_loaded[u], (pair + 1) * 16)
                        for n in range(NBLK):
                            for o in range(CT):
                                k = (u * NBLK + n) * CT + o
                                pe.wait_ge(hidden_ready, pair * 2 * PER_EXPERT + k + 1 + CREDIT - SLOTS)
                                for tile in range(CT):
                                    mm = nc.tensor.matmul(pre[:, k % SLOTS], weights[:, u, tile, o * P:(o + 1) * P],
                                                          xn[:, tile, tokens(n)], start=tile == 0, stop=tile == CT - 1)
                                mm.then_inc(pre_ready, 1)

            @block.scalar
            def _(act):
                for b in range(B):
                    act.wait_ge(gate_step, 5)
                    nc.scalar.activation(powers[:, b], logits[:, b], ACT.Exp,
                                         bias=minus_max[:, b:b + 1]).then_inc(powers_ready, 1)
                act.sem_inc(hidden_ready, CREDIT)
                with act.Fori(0, E // 2) as pair:
                    for k in range(2 * PER_EXPERT):
                        act.wait_ge(pre_ready, pair * 2 * PER_EXPERT + k + 1 + CREDIT)
                        act.wait_ge(added, pair * 2 * PER_EXPERT + k + 1)
                        nc.scalar.activation(hidden[:, k % SLOTS], pre[:, k % SLOTS], ACT.Gelu,
                                             bias=bias[:, k // PER_EXPERT, k % CT:k % CT + 1]
                                             ).then_inc(hidden_ready, 1)

            @block.vector
            def _(dve):
                dve.wait_ge(tables_loaded, 32)
                nc.vector.tensor_reduce(pooled[:], sums[:].rearrange("p c (b n) -> p c b n", b=B), AX.X, ALU.add).then_inc(gate_step, 1)
                dve.wait_ge(gate_step, 1)
                for tile in range(CT):
                    for b in range(B):
                        last = nc.vector.tensor_scalar(terms[:, tile, b], gate_w[:, tile], pooled[:, tile, b:b + 1], None, ALU.mult)
                last.then_inc(terms_ready, 1)
                dve.wait_ge(logits_ready, 1)
                nc.vector.scalar_tensor_tensor(logits[:], logit_sum[:].rearrange("p (b e) -> p b e", b=B), float(D) / T,
                                               over_tiles(gate_b[:], B), ALU.mult, ALU.add).then_inc(gate_step, 1)
                dve.wait_ge(gate_step, 2)
                for b in range(B):
                    nc.vector.max(top[:, b], logits[:, b]).then_inc(gate_step, 1)
                dve.wait_ge(gate_step, 4)
                nc.vector.tensor_scalar(minus_max[:], top[:, :, 0], -1.0, None, ALU.mult).then_inc(gate_step, 1)
                for b in range(B):
                    nc.vector.tensor_scalar(chosen[:, b], logits[:, b], top[:, b, 1:2], None, ALU.is_ge).then_inc(gate_step, 1)
                dve.wait_ge(gate_step, 7)
                dve.wait_ge(powers_ready, 2)
                nc.vector.tensor_tensor(chosen[:], chosen[:], powers[:], ALU.mult).then_inc(gate_step, 1)
                dve.wait_ge(gate_step, 8)
                nc.vector.tensor_reduce(total[:], chosen[:], AX.X, ALU.add).then_inc(gate_step, 1)
                dve.wait_ge(gate_step, 9)
                nc.vector.reciprocal(total[:], total[:]).then_inc(gate_step, 1)
                dve.wait_ge(gate_step, 10)
                for b in range(B):
                    nc.vector.tensor_scalar(gate[:, b], chosen[:, b], total[:, b:b + 1], 0.5, ALU.mult, ALU.mult).then_inc(gate_step, 1)
                dve.wait_ge(gate_step, 12)
                dve.sem_inc(added, SLOTS)
                with dve.Fori(0, E // 2) as pair:
                    for u in range(2):
                        for n in range(NBLK):
                            for o in range(CT):
                                k = (u * NBLK + n) * CT + o
                                b = n * BLK // T
                                dve.wait_ge(hidden_ready, pair * 2 * PER_EXPERT + k + 1 + CREDIT)
                                dve.wait_ge(added, pair * 2 * PER_EXPERT + k + 1)
                                nc.vector.scalar_tensor_tensor(x[:, o, tokens(n)], hidden[:, k % SLOTS],
                                                               gate[:, b, bass.ds(pair * 2 + u, 1)], x[:, o, tokens(n)],
                                                               ALU.mult, ALU.add).then_inc(added, 1)


def prototype_mixture(nc, c, dram, stage):
    NP = dram["proto_rows"].shape[0]
    RANK = dram["proto_B"].shape[2] // NP
    RT = NP * RANK // P
    TILES = N // P
    PER_BLK = BLK // P
    x = c["x"]
    with Scope(nc, stage) as s:
        xn = s.sb("xn", [P, CT, N])
        layer_norm(nc, c, f"{stage}_ln", xn, None)

        proto = s.sb("proto", [P, CT, NP])
        proto_rows = s.sb("proto_rows", [NP, D])
        proto_sq = s.sb("proto_sq", [NP, D])
        p2 = s.sb("p2", [NP, 1])
        ones = s.sb("ones", [P, NP])
        temp = s.sb("temp", [P, 1])
        minus_inv_t = s.sb("minus_inv_t", [P, 1])
        down = s.sb("down", [P, CT, NP * RANK])
        up = s.sb("up", [P, RT, D])
        bias = s.sb("bias", [NP, D])
        spread = s.sb("spread", [NP, NP * RANK])
        numbers = s.sb("numbers", [P, NP])
        squares = s.sb("squares", [P, 2, CT, BLK])
        clamped = s.sb("clamped", [NP, N])
        dist = s.sb("dist", [NP, N])
        scores = s.sb("scores", [P, TILES, NP])
        top = s.sb("top", [P, TILES, 8])
        which = s.sb("which", [P, TILES, 8], U32)
        whichf = s.sb("whichf", [P, TILES, 8])
        gap = s.sb("gap", [P, TILES])
        ratio = s.sb("ratio", [P, TILES])
        share = s.sb("share", [P, 2, TILES])
        picked = s.sb("picked", [P, 2, TILES, NP])
        mix = s.sb("mix", [NP, N])
        wide = s.sb("wide", [P, 2, BLK])
        low = s.sb("low", [P, 4, BLK])

        d2 = s.ps("d2", [P, 2, BLK])
        turned = s.ps("turned", [P, 2, BLK])
        low_sum = s.ps("low_sum", [P, 2, BLK])
        out = s.ps("out", [P, 2, BLK])
        mix_turned, wide_sum = d2, turned

        loaded, table_step = s.sem("loaded"), s.sem("table_step")
        squares_ready, d2_ready, clamped_ready, dist_ready = s.sem("squares_ready"), s.sem("d2_ready"), s.sem("clamped_ready"), s.sem("dist_ready")
        turned_ready, route_step, ratio_ready, picked_ready = s.sem("turned_ready"), s.sem("route_step"), s.sem("ratio_ready"), s.sem("picked_ready")
        mix_turned_ready, mix_ready = s.sem("mix_turned_ready"), s.sem("mix_ready")
        sums_ready, wide_ready, low_ready, out_ready, added = s.sem("sums_ready"), s.sem("wide_ready"), s.sem("low_ready"), s.sem("out_ready"), s.sem("added")
        CREDIT = 4

        with nc.Block() as block:

            @block.sync
            def _(sp):
                for tile, table in ((proto, "proto"), (proto_rows, "proto_rows"), (temp, "temp"), (numbers, "numbers"), (down, "proto_B"),
                                    (up, "proto_A"), (bias, "proto_bias"), (spread, "proto_spread")):
                    sp.dma_start(tile[:], dram[table]).then_inc(loaded, 16)

            def turn_distances(pe, n):
                pe.wait_ge(dist_ready, n + 1)
                for k in range(PER_BLK):
                    tile = n * PER_BLK + k
                    half, at = divmod(tile * NP, BLK)
                    mm = nc.tensor.transpose(turned[:, half, at:at + NP], dist[:, tile * P:(tile + 1) * P], c["identity"][0:NP, 0:NP])
                mm.then_inc(turned_ready, 1)

            @block.tensor
            def _(pe):
                pe.wait_ge(table_step, 4)
                for n in range(NBLK):
                    if n >= 2:
                        pe.wait_ge(clamped_ready, n - 1)
                    for tile in range(CT):
                        nc.tensor.matmul(d2[0:NP, n % 2], proto[:, tile], xn[:, tile, tokens(n)], start=tile == 0, stop=False)
                    pe.wait_ge(squares_ready, n + 1)
                    for tile in range(CT):
                        mm = nc.tensor.matmul(d2[0:NP, n % 2], ones[:], squares[:, n % 2, tile], start=False, stop=tile == CT - 1)
                    mm.then_inc(d2_ready, 1)
                    if n >= 1:
                        turn_distances(pe, n - 1)
                turn_distances(pe, NBLK - 1)
                pe.wait_ge(clamped_ready, NBLK)
                for n in range(NBLK):
                    pe.wait_ge(picked_ready, 1)
                    if n >= 2:
                        pe.wait_ge(mix_ready, n - 1)
                    for k in range(PER_BLK):
                        mm = nc.tensor.transpose(mix_turned[0:NP, n % 2, k * P:(k + 1) * P], picked[:, 0, n * PER_BLK + k], c["identity"][:])
                    mm.then_inc(mix_turned_ready, 1)
                pe.wait_ge(mix_ready, NBLK)
                with pe.Fori(0, NBLK // 2) as pair:
                    for u in range(2):
                        n = pair * 2 + u
                        for m in range(RT + 1):
                            if m < RT:
                                k = u * RT + m
                                pe.wait_ge(wide_ready, pair * 2 * RT + k + 1)
                                pe.wait_ge(low_ready, pair * 2 * RT + k + 1 + CREDIT - 2)
                                for tile in range(CT):
                                    nc.tensor.matmul(low_sum[:, m % 2], down[:, tile, m * P:(m + 1) * P], xn[:, tile, tokens(n)],
                                                     start=tile == 0, stop=tile == CT - 1)
                                nc.tensor.matmul(wide_sum[:, m % 2], spread[:, m * P:(m + 1) * P], mix[:, tokens(n)],
                                                 start=True, stop=True).then_inc(sums_ready, 1)
                            if m >= 1:
                                k = u * RT + m - 1
                                pe.wait_ge(low_ready, pair * 2 * RT + k + 1 + CREDIT)
                                if m == 1:
                                    pe.wait_ge(added, (n + 1) * CT)
                                for o in range(CT):
                                    nc.tensor.matmul(out[:, o], up[:, m - 1, o * P:(o + 1) * P], low[:, (m - 1) % 4],
                                                     start=m == 1, stop=False)
                        for o in range(CT):
                            nc.tensor.matmul(out[:, o], bias[:, o * P:(o + 1) * P], mix[:, tokens(n)],
                                             start=False, stop=True).then_inc(out_ready, 1)

            @block.scalar
            def _(act):
                for n in range(NBLK + 1):
                    if n < NBLK:
                        if n >= 2:
                            act.wait_ge(d2_ready, n - 1)
                        nc.scalar.activation(squares[:, n % 2], xn[:, :, tokens(n)], ACT.Square).then_inc(squares_ready, 1)
                    if n >= 1:
                        act.wait_ge(clamped_ready, n)
                        nc.scalar.activation(dist[:, tokens(n - 1)], clamped[:, tokens(n - 1)], ACT.Sqrt).then_inc(dist_ready, 1)
                act.wait_ge(route_step, 2 + 2 * TILES)
                nc.scalar.activation(ratio[:], gap[:], ACT.Exp).then_inc(ratio_ready, 1)
                act.sem_inc(wide_ready, 2)
                with act.Fori(0, NBLK // 2) as pair:
                    for k in range(2 * RT):
                        act.wait_ge(sums_ready, pair * 2 * RT + k + 1)
                        act.wait_ge(low_ready, pair * 2 * RT + k + 1 + CREDIT - 2)
                        nc.scalar.activation(wide[:, k % 2], wide_sum[:, k % 2], ACT.Copy).then_inc(wide_ready, 1)

            @block.vector
            def _(dve):
                nc.vector.memset(ones[:], 1.0).then_inc(table_step, 1)
                dve.wait_ge(loaded, 16 * 8)
                for tile in range(CT):
                    nc.vector.tensor_scalar(proto[:, tile], proto[:, tile], -2.0, None, ALU.mult).then_inc(table_step, 1)
                nc.vector.scalar_tensor_tensor(proto_sq[:], proto_rows[:], 1.0, proto_rows[:], ALU.mult, ALU.mult,
                                               accum_out=p2[:, 0:1]).then_inc(table_step, 1)
                nc.vector.scalar_tensor_tensor(minus_inv_t[:], temp[:], -1.0, temp[:], ALU.mult, ALU.max).then_inc(table_step, 1)
                dve.wait_ge(table_step, 5)
                nc.vector.tensor_scalar(temp[:], minus_inv_t[:], 0.1, -1.0, ALU.max, ALU.mult).then_inc(table_step, 1)
                dve.wait_ge(table_step, 6)
                nc.vector.reciprocal(minus_inv_t[:], temp[:]).then_inc(table_step, 1)
                dve.wait_ge(table_step, 7)
                for n in range(NBLK):
                    dve.wait_ge(d2_ready, n + 1)
                    nc.vector.tensor_scalar(clamped[:, tokens(n)], d2[0:NP, n % 2], p2[:, 0:1], 0.0, ALU.add, ALU.max).then_inc(clamped_ready, 1)
                dve.wait_ge(turned_ready, NBLK)
                nc.vector.tensor_scalar(scores[:].rearrange("p t n -> p (t n)"), turned[:].rearrange("p a b -> p (a b)"),
                                        minus_inv_t[:, 0:1], None, ALU.mult).then_inc(route_step, 1)
                dve.wait_ge(route_step, 1)
                for tile in range(TILES):
                    nc.vector.max(top[:, tile], scores[:, tile]).then_inc(route_step, 1)
                for tile in range(TILES):
                    dve.wait_ge(route_step, 2 + tile)
                    nc.vector.max_index(which[:, tile], top[:, tile], scores[:, tile]).then_inc(route_step, 1)
                nc.vector.tensor_tensor(gap[:], top[:, :, 1], top[:, :, 0], ALU.subtract).then_inc(route_step, 1)
                done = 2 + 2 * TILES
                dve.wait_ge(route_step, done)
                nc.vector.tensor_copy(whichf[:], which[:]).then_inc(route_step, 1)
                dve.wait_ge(ratio_ready, 1)
                nc.vector.tensor_scalar(share[:, 1], ratio[:], 1.0, None, ALU.add).then_inc(route_step, 1)
                dve.wait_ge(route_step, done + 2)
                nc.vector.reciprocal(share[:, 0], share[:, 1]).then_inc(route_step, 1)
                dve.wait_ge(route_step, done + 3)
                nc.vector.tensor_scalar(share[:, 0], share[:, 0], 0.5, None, ALU.mult).then_inc(route_step, 1)
                dve.wait_ge(route_step, done + 4)
                nc.vector.tensor_tensor(share[:, 1], share[:, 0], ratio[:], ALU.mult).then_inc(route_step, 1)
                for rank in range(2):
                    nc.vector.tensor_tensor(picked[:, rank], numbers[:].unsqueeze(1).broadcast_to([P, TILES, NP]),
                                            whichf[:, :, rank:rank + 1].broadcast_to([P, TILES, NP]), ALU.is_equal).then_inc(route_step, 1)
                dve.wait_ge(route_step, done + 7)
                for rank in range(2):
                    nc.vector.tensor_tensor(picked[:, rank], picked[:, rank],
                                            share[:, rank].unsqueeze(2).broadcast_to([P, TILES, NP]), ALU.mult).then_inc(route_step, 1)
                dve.wait_ge(route_step, done + 9)
                nc.vector.tensor_tensor(picked[:, 0], picked[:, 0], picked[:, 1], ALU.add).then_inc(picked_ready, 1)
                for n in range(NBLK):
                    dve.wait_ge(mix_turned_ready, n + 1)
                    nc.vector.tensor_copy(mix[:, tokens(n)], mix_turned[0:NP, n % 2]).then_inc(mix_ready, 1)
                dve.sem_inc(low_ready, CREDIT)
                dve.sem_inc(added, CT)
                with dve.Fori(0, NBLK // 2) as pair:
                    for u in range(2):
                        n = pair * 2 + u
                        for m in range(RT):
                            k = u * RT + m
                            dve.wait_ge(wide_ready, pair * 2 * RT + k + 1 + 2)
                            dve.wait_ge(added, (n + 1) * CT)
                            nc.vector.tensor_tensor(low[:, m % 4], low_sum[:, m % 2], wide[:, m % 2], ALU.mult).then_inc(low_ready, 1)
                        for o in range(CT):
                            dve.wait_ge(out_ready, n * CT + o + 1)
                            nc.vector.tensor_tensor(x[:, o, tokens(n)], x[:, o, tokens(n)], out[:, o], ALU.add).then_inc(added, 1)


HEADS = 16
HD = D // HEADS
HX = 64
PAIRS = HX // 2
BH = B * HEADS
QG = P // PAIRS
QT = T // P
LOGIT_SCALE = 1.0 / 64
DOT_SCALE = 8.0
MAX_ROW = HX + 3 * HD
V_SCALE = 16.0
PROB_SCALE = 256.0
ONES = 2 * HD
V_COLS = ONES + 1


def project_qkv(nc, c, dram, stage, xn, qk, v):
    with Scope(nc, stage) as s:
        w_qk = s.sb("w_qk", [P, 2, CT, D])
        w_v = s.sb("w_v", [P, CT, D])
        b_qk = s.sb("b_qk", [P, 2, CT])
        b_v = s.sb("b_v", [P, D])
        v_sum = s.sb("v_sum", [P, 2, D])
        high = s.sb("high", [P, 2, T], F16)
        rest = s.sb("rest", [P, 2, T], F16)
        acc = s.ps("acc", [P, 4, BLK])
        loaded, acc_ready, qk_ready, v_ready = s.sem("loaded"), s.sem("acc_ready"), s.sem("qk_ready"), s.sem("v_ready")
        high_ready, rest_ready, v_step = s.sem("high_ready"), s.sem("rest_ready"), s.sem("v_step")
        stored = [s.sem(f"stored{slot}") for slot in range(2)]
        steps = [(w, tile, n) for w in range(2) for tile in range(CT) for n in range(NBLK)]
        HALF = NBLK // B

        with nc.Block() as block:

            @block.sync
            def _(sp):
                for tile, table in ((w_qk, "att_w_qk"), (w_v, "att_w_v"), (b_qk, "att_b_qk"), (b_v, "att_b_v")):
                    sp.dma_start(tile[:], dram[table]).then_inc(loaded, 16)
                for r in range(len(steps) // HALF):
                    w, tile, n = steps[r * HALF]
                    rows = w * BH * HD + (n // HALF) * D + tile * P
                    sp.wait_ge(rest_ready, (r + 1) * HALF)
                    sp.dma_start(dram["att_dot"][0, rows:rows + P], high[:, r % 2]).then_inc(stored[r % 2], 16)
                    sp.dma_start(dram["att_dot"][1, rows:rows + P], rest[:, r % 2]).then_inc(stored[r % 2], 16)
                for slot in range(2):
                    sp.wait_ge(stored[slot], len(steps) // HALF * 16)

            @block.tensor
            def _(pe):
                pe.wait_ge(loaded, 64)
                for k, (w, tile, n) in enumerate(steps):
                    if k >= 4:
                        pe.wait_ge(qk_ready, k - 3)
                    for t in range(CT):
                        mm = nc.tensor.matmul(acc[:, k % 4], w_qk[:, w, t, tile * P:(tile + 1) * P], xn[:, t, tokens(n)],
                                              start=t == 0, stop=t == CT - 1)
                    mm.then_inc(acc_ready, 1)
                for i in range(N // P):
                    k = len(steps) + i
                    if i < 4:
                        pe.wait_ge(qk_ready, k - 3)
                    else:
                        pe.wait_ge(v_ready, i - 3)
                    for t in range(CT):
                        mm = nc.tensor.matmul(acc[:, k % 4, 0:D], xn[:, t, i * P:(i + 1) * P], w_v[:, t], start=t == 0, stop=t == CT - 1)
                    mm.then_inc(acc_ready, 1)

            @block.scalar
            def _(act):
                for k, (w, tile, n) in enumerate(steps):
                    act.wait_ge(acc_ready, k + 1)
                    nc.scalar.activation(qk[:, tile, w, tokens(n)], acc[:, k % 4], ACT.Identity,
                                         bias=b_qk[:, w, tile:tile + 1]).then_inc(qk_ready, 1)

            @block.vector
            def _(dve):
                for k, (w, tile, n) in enumerate(steps):
                    r, at = divmod(k, HALF)
                    scale = 1.0 if w else DOT_SCALE
                    dve.wait_ge(qk_ready, k + 1)
                    if r >= 2:
                        dve.wait_ge(stored[r % 2], r // 2 * 32)
                    nc.vector.tensor_scalar(high[:, r % 2, tokens(at)], qk[:, tile, w, tokens(n)], scale, None, ALU.mult).then_inc(high_ready, 1)
                    dve.wait_ge(high_ready, k + 1)
                    nc.vector.scalar_tensor_tensor(rest[:, r % 2, tokens(at)], qk[:, tile, w, tokens(n)], scale,
                                                   high[:, r % 2, tokens(at)], ALU.mult, ALU.subtract).then_inc(rest_ready, 1)
                for i in range(N // P):
                    k = len(steps) + i
                    dve.wait_ge(acc_ready, k + 1)
                    nc.vector.tensor_tensor(v_sum[:, i % 2], acc[:, k % 4, 0:D], b_v[:], ALU.add).then_inc(v_ready, 1)
                    by_head = v_sum[:, i % 2].rearrange("p (h d) -> p h d", h=HEADS)
                    columns = v[:, i // QT * HEADS:(i // QT + 1) * HEADS, i % QT]
                    dve.wait_ge(v_ready, i + 1)
                    nc.vector.tensor_scalar(columns[:, :, 0:HD], by_head, V_SCALE, None, ALU.mult).then_inc(v_step, 1)
                    dve.wait_ge(v_step, 2 * i + 1)
                    nc.vector.scalar_tensor_tensor(columns[:, :, HD:ONES], by_head, V_SCALE, columns[:, :, 0:HD],
                                                   ALU.mult, ALU.subtract).then_inc(v_step, 1)
                nc.vector.memset(v[:, :, :, ONES], V_SCALE)


def helical_features(nc, c, dram, stage, qk):
    with Scope(nc, stage) as s:
        w_hel = s.sb("w", [P, CT, 2, 2, P])
        bias = s.sb("bias", [P, CT, 2, 2])
        raw = s.sb("raw", [P, 2, 2, BLK])
        squares = s.sb("squares", [P, 2, 2, BLK])
        norm_sq = s.sb("norm_sq", [P, 2, BLK])
        log_sq = s.sb("log_sq", [P, 2, BLK])
        inv = s.sb("inv", [P, 2, BLK])
        unit = s.sb("unit", [P, 2, 2, BLK])
        high = s.sb("high", [P, B, 2, 2, T // 2], F16)
        rest = s.sb("rest", [P, B, 2, 2, T // 2], F16)
        acc = s.ps("acc", [P, 2, 2, BLK])
        loaded, acc_ready, raw_ready, squares_ready = s.sem("loaded"), s.sem("acc_ready"), s.sem("raw_ready"), s.sem("squares_ready")
        norm_ready, log_ready, inv_ready, unit_ready = s.sem("norm_ready"), s.sem("log_ready"), s.sem("inv_ready"), s.sem("unit_ready")
        high_ready, rest_ready = s.sem("high_ready"), s.sem("rest_ready")
        stored = [s.sem(f"stored{b}") for b in range(B)]
        CREDIT = 2
        STEPS = T // BLK
        ROUNDS = 2 * CT * 2

        def number(group, w, b, n):
            return ((w + group * 2) * B + b) * STEPS + n

        with nc.Block() as block:

            @block.sync
            def _(sp):
                sp.dma_start(w_hel[:], dram["att_hel_w"]).then_inc(loaded, 16)
                sp.dma_start(bias[:], dram["att_hel_b"]).then_inc(loaded, 16)
                for group in range(2 * CT):
                    with sp.Fori(0, 2) as w:
                        for b in range(B):
                            sp.wait_ge(rest_ready, number(group, w, b, STEPS) + CREDIT)
                            rows = bass.ds((w * B + b) * (HEADS * PAIRS) + group * P, P)
                            for parity in range(2):
                                for part, tile in ((0, high), (1, rest)):
                                    sp.dma_start(dram["att_hel"][part, parity, rows].rearrange("r (i u) -> r i u", i=2),
                                                 tile[:, b, :, parity]).then_inc(stored[b], 16)
                for b in range(B):
                    sp.wait_ge(stored[b], ROUNDS * 64 + 1)

            @block.tensor
            def _(pe):
                pe.wait_ge(loaded, 32)
                for group in range(2 * CT):
                    tile, half = divmod(group, 2)
                    with pe.Fori(0, 2) as w:
                        for b in range(B):
                            for n in range(STEPS):
                                k = number(group, w, b, n)
                                pe.wait_ge(raw_ready, k * 2 + 2)
                                pe.wait_ge(squares_ready, k * 2 + 2)
                                for comp in range(2):
                                    mm = nc.tensor.matmul(acc[:, n % 2, comp], w_hel[:, tile, half, comp],
                                                          qk[:, tile].rearrange("p w n -> p (w n)")[:, bass.ds(w * N + b * T + n * BLK, BLK)],
                                                          start=True, stop=True)
                                mm.then_inc(acc_ready, 1)

            @block.scalar
            def _(act):
                nc.scalar.preload_act_table_set(LOG_EXP_SET)
                act.sem_inc(raw_ready, 2 * CREDIT)
                act.sem_inc(squares_ready, 2 * CREDIT)
                act.sem_inc(log_ready, CREDIT)
                for group in range(2 * CT):
                    tile, half = divmod(group, 2)
                    with act.Fori(0, 2) as w:
                        for b in range(B):
                            for n in range(STEPS):
                                k = number(group, w, b, n)
                                act.wait_ge(acc_ready, k + 1)
                                act.wait_ge(norm_ready, k + 1)
                                for comp in range(2):
                                    nc.scalar.activation(squares[:, n % 2, comp], acc[:, n % 2, comp], ACT.Square,
                                                         bias=bias[:, tile, half, comp:comp + 1]).then_inc(squares_ready, 1)
                                act.wait_ge(unit_ready, k + 1)
                                for comp in range(2):
                                    nc.scalar.activation(raw[:, n % 2, comp], acc[:, n % 2, comp], ACT.Identity,
                                                         bias=bias[:, tile, half, comp:comp + 1]).then_inc(raw_ready, 1)
                                act.wait_ge(norm_ready, k + 1 + CREDIT)
                                nc.scalar.activation(log_sq[:, n % 2], norm_sq[:, n % 2], ACT.Ln).then_inc(log_ready, 1)
                                act.wait_ge(log_ready, k + 1 + CREDIT)
                                act.wait_ge(unit_ready, k + 1)
                                nc.scalar.activation(inv[:, n % 2], log_sq[:, n % 2], ACT.Exp, scale=-0.5).then_inc(inv_ready, 1)

            @block.vector
            def _(dve):
                dve.sem_inc(norm_ready, CREDIT)
                dve.sem_inc(unit_ready, CREDIT)
                for b in range(B):
                    dve.sem_inc(stored[b], 1)
                for group in range(2 * CT):
                    with dve.Fori(0, 2) as w:
                        for b in range(B):
                            for n in range(STEPS):
                                k = number(group, w, b, n)
                                half_blk = slice(n * BLK // 2, (n + 1) * BLK // 2)
                                dve.wait_ge(squares_ready, k * 2 + 2 + 2 * CREDIT)
                                dve.wait_ge(log_ready, k + 1)
                                nc.vector.tensor_tensor(norm_sq[:, n % 2], squares[:, n % 2, 0], squares[:, n % 2, 1], ALU.add).then_inc(norm_ready, 1)
                                dve.wait_ge(inv_ready, k + 1)
                                dve.wait_ge(rest_ready, k + 1)
                                nc.vector.scalar_tensor_tensor(unit[:, n % 2], over_tiles(inv[:, n % 2], 2), 1e12, raw[:, n % 2],
                                                               ALU.min, ALU.mult).then_inc(unit_ready, 1)
                                dve.wait_ge(unit_ready, k + 1 + CREDIT)
                                if n == 0:
                                    dve.wait_ge(stored[b], (w + group * 2) * 64 + 1)
                                nc.vector.tensor_copy(high[:, b, :, :, half_blk], unit[:, n % 2].rearrange("p i (u c) -> p i c u", c=2)).then_inc(high_ready, 1)

            @block.gpsimd
            def _(pool):
                pool.sem_inc(rest_ready, CREDIT)
                for group in range(2 * CT):
                    with pool.Fori(0, 2) as w:
                        for b in range(B):
                            for n in range(STEPS):
                                half_blk = slice(n * BLK // 2, (n + 1) * BLK // 2)
                                pool.wait_ge(high_ready, number(group, w, b, n) + 1)
                                nc.gpsimd.tensor_tensor(rest[:, b, :, :, half_blk], unit[:, n % 2].rearrange("p i (u c) -> p i c u", c=2),
                                                        high[:, b, :, :, half_blk], ALU.subtract).then_inc(rest_ready, 1)


def head_attention(nc, c, dram, stage, v):
    with Scope(nc, stage) as s:
        q = s.sb("q", [P, 2, 2, T], F16)
        k = s.sb("k", [P, 2, 2, T], F16)
        probs = s.sb("probs", [P, 2, T // 2])
        high = s.sb("high", [P, 4, T // 2], F16)
        rest = s.sb("rest", [P, 4, T // 2], F16)
        log_scale = s.sb("log_scale", [P, 1])
        v_head = s.sb("v_head", [P, 2, QT, V_COLS], F16)
        maxima = s.sb("maxima", [P, QT * 4])
        tile_max = s.sb("tile_max", [P, QT])
        shift = s.sb("shift", [P, QT])
        shift_row = s.sb("shift_row", [QT, P], F16)
        out_copy = s.sb("out_copy", [V_COLS, 2, T // 2])
        scores = s.ps("scores", [P, 2, T // 2])
        peek = s.ps("peek", [P, 2, BLK])
        out = s.ps("out", [P, T // 2])

        ones_ready = s.sem("ones_ready")
        loaded = [s.sem(f"loaded{slot}") for slot in range(2)]
        shift_stored = [s.sem(f"shift_stored{slot}") for slot in range(2)]
        out_stored = [s.sem(f"out_stored{half}") for half in range(2)]
        v_ready, peek_ready, peek_read = s.sem("v_ready"), s.sem("peek_ready"), s.sem("peek_read")
        max_step, shift_ready, shift_turned, shift_row_ready = s.sem("max_step"), s.sem("shift_ready"), s.sem("shift_turned"), s.sem("shift_row_ready")
        scores_ready, probs_ready, high_ready = s.sem("scores_ready"), s.sem("probs_ready"), s.sem("high_ready")
        rest_a_ready, rest_b_ready, weighed, out_copied = s.sem("rest_a_ready"), s.sem("rest_b_ready"), s.sem("weighed"), s.sem("out_copied")
        STEPS = 2 * QT
        AHEAD = 3
        BEFORE_COPY = 2
        PEEKS = QT * 4
        FIRST_PEEK = 2
        TURN_AT = FIRST_PEEK + (PEEKS + 2) // 3
        LOADS = 18 * 16
        SPLIT = 384
        W_CREDIT, H_CREDIT, R_CREDIT, K_CREDIT = 2 * STEPS, 2, 2, 2

        def peeks_at(step):
            first = 3 * (step - FIRST_PEEK)
            return range(first, min(first + 3, PEEKS)) if step >= FIRST_PEEK else range(0)

        with nc.Block() as block:

            @block.sync
            def _(sp):
                hel, dot = dram["att_hel"], dram["att_dot"]

                def load(pair, slot):
                    head = pair * 2 + slot
                    at_q, at_k = bass.ds(head * PAIRS, PAIRS), bass.ds(head * PAIRS + BH * PAIRS, PAIRS)
                    for parity in range(2):
                        rows = slice(parity * PAIRS, (parity + 1) * PAIRS)
                        more_rows = slice(HX + parity * PAIRS, HX + (parity + 1) * PAIRS)
                        for tile, rows_of, number, source in (
                                (q, rows, 0, hel[0, parity, at_q]), (k, rows, 0, hel[0, parity, at_k]),
                                (q, rows, 1, hel[0, parity, at_q]), (k, rows, 1, hel[1, parity, at_k]),
                                (q, more_rows, 1, hel[1, parity, at_q]), (k, more_rows, 1, hel[0, parity, at_k])):
                            sp.dma_start(tile[rows_of, slot, number], source).then_inc(loaded[slot], 16)
                    for part, (q_part, k_part) in enumerate(((0, 0), (0, 1), (1, 0))):
                        rows = slice(HX + part * HD, HX + (part + 1) * HD)
                        sp.dma_start(q[rows, slot, 0], dot[q_part, bass.ds(head * HD, HD)]).then_inc(loaded[slot], 16)
                        sp.dma_start(k[rows, slot, 0], dot[k_part, bass.ds(head * HD + BH * HD, HD)]).then_inc(loaded[slot], 16)

                def store_shift(pair, slot):
                    sp.wait_ge(shift_row_ready, pair * 2 + slot + 1)
                    sp.dma_start(q[MAX_ROW:MAX_ROW + 1, slot, 0].rearrange("a (t n) -> a t n", t=QT), shift_row[:]
                                 ).then_inc(shift_stored[slot], 16)

                def store_out(pair, slot, half):
                    head = pair * 2 + slot
                    queries = slice(half * T // 2, (half + 1) * T // 2)
                    sp.wait_ge(out_copied, head * 2 + half + 1 + 1)
                    for part in range(2):
                        sp.dma_start(dram["att_o"][part, bass.ds(head * HD, HD), queries], out_copy[part * HD:(part + 1) * HD, half]
                                     ).then_inc(out_stored[half], 16)
                    sp.dma_start(dram["att_sum"][bass.ds(head, 1), queries], out_copy[ONES:V_COLS, half]).then_inc(out_stored[half], 16)

                def follow(pair, slot, more_shift, more_load):
                    store_out(pair, slot, 0)
                    if more_shift:
                        store_shift(pair + slot, 1 - slot)
                    if more_load:
                        sp.wait_ge(scores_ready, (pair * 2 + slot + 1) * STEPS)
                        load(pair + 1, slot)
                    store_out(pair, slot, 1)

                sp.wait_ge(ones_ready, 2)
                load(0, 0)
                load(0, 1)
                store_shift(0, 0)
                with sp.Fori(0, BH // 2 - 1) as pair:
                    for slot in range(2):
                        follow(pair, slot, True, True)
                follow(BH // 2 - 1, 0, True, False)
                follow(BH // 2 - 1, 1, False, False)
                for half in range(2):
                    sp.wait_ge(out_stored[half], BH * 48 + 1)

            @block.gpsimd
            def _(pool):
                pool.sem_inc(rest_b_ready, R_CREDIT)
                with pool.Fori(0, BH // 2) as pair:
                    for slot in range(2):
                        head = pair * 2 + slot
                        pool.wait_ge(weighed, (head + 1) * STEPS)
                        nc.gpsimd.tensor_copy(v_head[:, slot], v[:, bass.ds(head, 1)].squeeze(1)).then_inc(v_ready, 1)
                        for step in range(STEPS):
                            pool.wait_ge(high_ready, head * STEPS + step + 1 + H_CREDIT)
                            nc.gpsimd.tensor_tensor(rest[:, step % 4, SPLIT:], probs[:, step % 2, SPLIT:], high[:, step % 4, SPLIT:],
                                                    ALU.subtract).then_inc(rest_b_ready, 1)

            @block.tensor
            def _(pe):
                def peek_scores(pair, slot, numbers):
                    head = pair * 2 + slot
                    for m in numbers:
                        tile, blk = divmod(m, 4)
                        if m == 0:
                            pe.wait_ge(loaded[slot], (pair + 1) * LOADS)
                        pe.wait_ge(peek_read, head * PEEKS + m + 1)
                        nc.tensor.matmul(peek[:, m % 2], q[0:MAX_ROW, slot, 0, tile * P:(tile + 1) * P], k[0:MAX_ROW, slot, 0, tokens(blk)],
                                         start=True, stop=True).then_inc(peek_ready, 1)

                def turn_shifts(pair, slot):
                    pe.wait_ge(shift_ready, pair * 2 + slot + 1)
                    nc.tensor.transpose(peek[0:QT, 0, 0:P], shift[:], c["identity"][:]).then_inc(shift_turned, 1)

                def score(pair, slot, step):
                    half, tile = divmod(step, QT)
                    head = pair * 2 + slot
                    if step == 0:
                        pe.wait_ge(shift_stored[slot], (pair + 1) * 16)
                    pe.wait_ge(high_ready, head * STEPS + step + 1)
                    for number, rows in ((1, P), (0, MAX_ROW + 1)):
                        for j in range(2):
                            mm = nc.tensor.matmul(scores[:, step % 2, tokens(j)], k[0:rows, slot, number, tile * P:(tile + 1) * P],
                                                  q[0:rows, slot, number, tokens(half * 2 + j)], start=number == 1, stop=number == 0)
                    mm.then_inc(scores_ready, 1)

                def weigh(pair, slot, step):
                    half, tile = divmod(step, QT)
                    head = pair * 2 + slot
                    if step == 0:
                        pe.wait_ge(v_ready, head + 1)
                    if tile == 0:
                        pe.wait_ge(out_copied, head * 2 + half + 1)
                    pe.wait_ge(rest_a_ready, head * STEPS + step + 1 + R_CREDIT)
                    pe.wait_ge(rest_b_ready, head * STEPS + step + 1 + R_CREDIT)
                    for part in (high, rest):
                        for j in range(2):
                            mm = nc.tensor.matmul(out[0:V_COLS, tokens(j)], v_head[:, slot, tile], part[:, step % 4, tokens(j)],
                                                  start=tile == 0 and part is high, stop=tile == QT - 1 and part is rest)
                    mm.then_inc(weighed, 1)

                def attend(pair, slot, more):
                    ahead = (pair + slot, 1 - slot)
                    for step in range(STEPS):
                        peeks = peeks_at(step) if more else range(0)
                        peek_scores(*ahead, peeks[0:1])
                        if step + AHEAD < STEPS:
                            score(pair, slot, step + AHEAD)
                        elif more:
                            score(*ahead, step + AHEAD - STEPS)
                        peek_scores(*ahead, peeks[1:2])
                        weigh(pair, slot, step)
                        peek_scores(*ahead, peeks[2:])
                        if more and step == TURN_AT:
                            turn_shifts(*ahead)

                pe.sem_inc(weighed, W_CREDIT)
                peek_scores(0, 0, range(PEEKS))
                turn_shifts(0, 0)
                for step in range(AHEAD):
                    score(0, 0, step)
                with pe.Fori(0, BH // 2 - 1) as pair:
                    for slot in range(2):
                        attend(pair, slot, True)
                attend(BH // 2 - 1, 0, True)
                attend(BH // 2 - 1, 1, False)

            @block.scalar
            def _(act):
                def powers(head, step):
                    count = head * STEPS + step
                    act.wait_ge(scores_ready, count + 1)
                    act.wait_ge(rest_a_ready, count + 1)
                    act.wait_ge(rest_b_ready, count + 1)
                    nc.scalar.activation(probs[:, step % 2], scores[:, step % 2], ACT.Exp, bias=log_scale[:, 0:1], scale=LOGIT_SCALE).then_inc(probs_ready, 1)
                    act.wait_ge(weighed, count + 1 + W_CREDIT - 4)
                    nc.scalar.activation(high[:, step % 4], scores[:, step % 2], ACT.Exp, bias=log_scale[:, 0:1], scale=LOGIT_SCALE).then_inc(high_ready, 1)

                def copy_out(head, half):
                    act.wait_ge(weighed, head * STEPS + (half + 1) * QT + W_CREDIT)
                    act.wait_ge(out_stored[half], head * 48 + 1)
                    nc.scalar.activation(out_copy[:, half], out[0:V_COLS], ACT.Copy).then_inc(out_copied, 1)

                def turn(head, more):
                    for step in range(BEFORE_COPY, STEPS + BEFORE_COPY if more else STEPS):
                        powers(head, step)
                        if step == QT + BEFORE_COPY - 1:
                            copy_out(head, 0)
                    copy_out(head, 1)

                act.wait_ge(ones_ready, 3)
                act.sem_inc(high_ready, H_CREDIT)
                act.sem_inc(out_copied, 1)
                for step in range(BEFORE_COPY):
                    powers(0, step)
                with act.Fori(0, BH - 1) as head:
                    turn(head, True)
                turn(BH - 1, False)

            @block.vector
            def _(dve):
                def read_peeks(head, numbers):
                    for m in numbers:
                        dve.wait_ge(peek_ready, head * PEEKS + m + 1)
                        if m == 0:
                            dve.wait_ge(max_step, head + 1)
                        nc.vector.tensor_reduce(maxima[:, m:m + 1], peek[:, m % 2], AX.X, ALU.max).then_inc(peek_read, 1)

                def shifts(head):
                    dve.wait_ge(peek_read, (head + 1) * PEEKS + K_CREDIT)
                    nc.vector.tensor_reduce(tile_max[:], maxima[:].rearrange("p (t b) -> p t b", b=4), AX.X, ALU.max).then_inc(max_step, 1)
                    dve.wait_ge(max_step, head + 2)
                    nc.vector.tensor_scalar(shift[:], tile_max[:], -LOGIT_SCALE, None, ALU.mult).then_inc(shift_ready, 1)

                def shift_rows(pair, slot, stored):
                    head = pair * 2 + slot
                    dve.wait_ge(shift_turned, head + 1)
                    if stored:
                        dve.wait_ge(shift_stored[1 - slot], (pair + slot) * 16)
                    nc.vector.tensor_copy(shift_row[:], peek[0:QT, 0, 0:P]).then_inc(shift_row_ready, 1)

                def split(head, step):
                    dve.wait_ge(high_ready, head * STEPS + step + 1 + H_CREDIT)
                    nc.vector.tensor_tensor(rest[:, step % 4, 0:SPLIT], probs[:, step % 2, 0:SPLIT], high[:, step % 4, 0:SPLIT],
                                            ALU.subtract).then_inc(rest_a_ready, 1)

                def turn(pair, slot, more):
                    head = pair * 2 + slot
                    ahead = (pair + slot, 1 - slot)
                    for step in range(STEPS):
                        if more or step + 1 < STEPS:
                            split(head, step + 1)
                        if more:
                            read_peeks(head + 1, peeks_at(step))
                            if step == TURN_AT:
                                shifts(head + 1)
                            if step == TURN_AT + 1:
                                shift_rows(*ahead, True)

                for slot in range(2):
                    nc.vector.memset(k[96:P, slot, 0], 1.0 / LOGIT_SCALE).then_inc(ones_ready, 1)
                nc.vector.memset(log_scale[:], math.log(PROB_SCALE)).then_inc(ones_ready, 1)
                dve.sem_inc(peek_read, K_CREDIT)
                dve.sem_inc(max_step, 1)
                dve.sem_inc(rest_a_ready, R_CREDIT)
                for half in range(2):
                    dve.sem_inc(out_stored[half], 1)
                read_peeks(0, range(PEEKS))
                shifts(0)
                shift_rows(0, 0, False)
                split(0, 0)
                with dve.Fori(0, BH // 2 - 1) as pair:
                    for slot in range(2):
                        turn(pair, slot, True)
                turn(BH // 2 - 1, 0, True)
                turn(BH // 2 - 1, 1, False)


def project_out(nc, c, dram, stage):
    x = c["x"]
    ROWS = P // BH
    with Scope(nc, stage) as s:
        w_o = s.sb("w_o", [P, CT, D])
        b_o = s.sb("b_o", [P, CT])
        sums = s.sb("sums", [P, T // ROWS])
        inv = s.sb("inv", [P, CT, N])
        parts = s.sb("parts", [P, 2, CT, N])
        acc = s.ps("acc", [P, 2, CT, BLK])
        sums_loaded, inverted, inv_stored, inv_loaded = s.sem("sums_loaded"), s.sem("inverted"), s.sem("inv_stored"), s.sem("inv_loaded")
        loaded, whole, att_ready, acc_ready, added = s.sem("loaded"), s.sem("whole"), s.sem("att_ready"), s.sem("acc_ready"), s.sem("added")

        with nc.Block() as block:

            @block.sync
            def _(sp):
                sp.dma_start(sums[:], dram["att_sum"].rearrange("h (r t) -> (h r) t", r=ROWS)).then_inc(sums_loaded, 16)
                sp.wait_ge(inverted, 1)
                sp.dma_start(dram["att_inv"].rearrange("h (r t) -> (h r) t", r=ROWS), sums[:]).then_inc(inv_stored, 16)
                sp.wait_ge(inv_stored, 16)
                for b in range(B):
                    for tile in range(CT):
                        first = b * HEADS + tile * HEADS // CT
                        sp.dma_start(inv[:, tile, b * T:(b + 1) * T],
                                     dram["att_inv"][first:first + HEADS // CT].unsqueeze(1).broadcast_to([HEADS // CT, HD, T])).then_inc(inv_loaded, 16)

            @block.scalar
            def _(act):
                act.dma_start(w_o[:], dram["att_w_o"]).then_inc(loaded, 16)
                act.dma_start(b_o[:], dram["att_b_o"]).then_inc(loaded, 16)
                for b in range(B):
                    for part in range(2):
                        for tile in range(CT):
                            act.dma_start(parts[:, part, tile, b * T:(b + 1) * T], dram["att_o"][part, b * D + tile * P:b * D + (tile + 1) * P]
                                          ).then_inc(loaded, 16)

            @block.tensor
            def _(pe):
                pe.wait_ge(loaded, (2 + 4 * B) * 16)
                for n in range(NBLK):
                    pe.wait_ge(att_ready, n + 1)
                    if n >= 2:
                        pe.wait_ge(added, (n - 1) * CT)
                    for o in range(CT):
                        for tile in range(CT):
                            mm = nc.tensor.matmul(acc[:, n % 2, o], w_o[:, tile, o * P:(o + 1) * P], parts[:, 0, tile, tokens(n)],
                                                  start=tile == 0, stop=tile == CT - 1)
                        mm.then_inc(acc_ready, 1)

            @block.vector
            def _(dve):
                def add(n):
                    for o in range(CT):
                        dve.wait_ge(acc_ready, n * CT + o + 1)
                        nc.vector.scalar_tensor_tensor(x[:, o, tokens(n)], acc[:, n % 2, o], b_o[:, o:o + 1], x[:, o, tokens(n)],
                                                       ALU.add, ALU.add).then_inc(added, 1)

                dve.wait_ge(sums_loaded, 16)
                nc.vector.reciprocal(sums[:], sums[:]).then_inc(inverted, 1)
                dve.wait_ge(loaded, (2 + 4 * B) * 16)
                for n in range(NBLK):
                    nc.vector.tensor_tensor(parts[:, 0, :, tokens(n)], parts[:, 0, :, tokens(n)], parts[:, 1, :, tokens(n)], ALU.add).then_inc(whole, 1)
                dve.wait_ge(inv_loaded, 16 * B * CT)
                for n in range(NBLK):
                    dve.wait_ge(whole, n + 1)
                    nc.vector.tensor_tensor(parts[:, 0, :, tokens(n)], parts[:, 0, :, tokens(n)], inv[:, :, tokens(n)], ALU.mult).then_inc(att_ready, 1)
                    if n >= 1:
                        add(n - 1)
                add(NBLK - 1)


def helical_attention(nc, c, dram, stage):
    dram["att_dot"] = nc.dram_tensor("att_dot", (2, 2 * BH * HD, T), F16, kind="Internal").ap()
    dram["att_hel"] = nc.dram_tensor("att_hel", (2, 2, 2 * BH * PAIRS, T), F16, kind="Internal").ap()
    dram["att_o"] = nc.dram_tensor("att_o", (2, BH * HD, T), F32, kind="Internal").ap()
    dram["att_sum"] = nc.dram_tensor("att_sum", (BH, T), F32, kind="Internal").ap()
    dram["att_inv"] = nc.dram_tensor("att_inv", (BH, T), F32, kind="Internal").ap()
    with Scope(nc, stage) as s:
        v = s.sb("v", [P, BH, QT, V_COLS], F16)
        with Scope(nc, f"{stage}_prepare") as prepare:
            qk = prepare.sb("qk", [P, CT, 2, N])
            with Scope(nc, f"{stage}_normed") as normed:
                xn = normed.sb("xn", [P, CT, N])
                layer_norm(nc, c, f"{stage}_ln", xn, None)
                project_qkv(nc, c, dram, f"{stage}_qkv", xn, qk, v)
            helical_features(nc, c, dram, f"{stage}_hel", qk)
        head_attention(nc, c, dram, f"{stage}_heads", v)
    project_out(nc, c, dram, f"{stage}_out")

TAPS = 4
ALPHA_MIN = 0.1
RMS_EPS = 1e-6
QUARTERS = 4
JQ = 16 // QUARTERS
SPAN = 64
CHUNK = 8
CHUNKS = SPAN // CHUNK
SOLVE, MIX = 0, CHUNK * CHUNK
K_IN = MIX + CHUNK * CHUNK
K_OUT = K_IN + CHUNK * HD
Q_IN = K_OUT + CHUNK * HD
DECAY = Q_IN + CHUNK * HD
RECORD = DECAY + 1


def delta_gates(nc, c, dram, stage, xn):
    with Scope(nc, stage) as s:
        w_ab = s.sb("w_ab", [P, CT, 2 * HEADS])
        b_ab = s.sb("b_ab", [2 * HEADS, 2])
        w_down = s.sb("w_down", [P, CT, P])
        w_up = s.sb("w_up", [P, D])
        ab = s.sb("ab", [2 * HEADS, N])
        down = s.sb("down", [P, 2, BLK])
        gate = s.sb("gate", [P, CT, N])
        acc = s.ps("acc", [P, 2, BLK])
        acc_down = s.ps("acc_down", [P, 2, BLK])
        acc_up = s.ps("acc_up", [P, 2, CT, BLK])
        loaded, ab_sum, ab_ready, ab_clipped = s.sem("loaded"), s.sem("ab_sum"), s.sem("ab_ready"), s.sem("ab_clipped")
        down_sum, down_ready, up_sum, gate_ready, stored = s.sem("down_sum"), s.sem("down_ready"), s.sem("up_sum"), s.sem("gate_ready"), s.sem("stored")

        with nc.Block() as block:

            @block.sync
            def _(sp):
                for tile, table in ((w_ab, "delta_w_ab"), (b_ab, "delta_b_ab"), (w_down, "delta_w_down"), (w_up, "delta_w_up")):
                    sp.dma_start(tile[:], dram[table]).then_inc(loaded, 16)
                sp.wait_ge(ab_clipped, NBLK)
                for b in range(B):
                    sp.dma_start(dram["delta_ab"][b], ab[:, b * T:(b + 1) * T]).then_inc(stored, 16)
                sp.wait_ge(gate_ready, NBLK * CT)
                sp.dma_start(dram["delta_gate"], gate[:]).then_inc(stored, 16)
                sp.wait_ge(stored, (B + 1) * 16)

            @block.tensor
            def _(pe):
                pe.wait_ge(loaded, 64)
                for n in range(NBLK + 1):
                    if n < NBLK:
                        if n >= 2:
                            pe.wait_ge(ab_ready, n - 1)
                            pe.wait_ge(down_ready, n - 1)
                        for t in range(CT):
                            mm = nc.tensor.matmul(acc[0:2 * HEADS, n % 2], w_ab[:, t], xn[:, t, tokens(n)], start=t == 0, stop=t == CT - 1)
                        mm.then_inc(ab_sum, 1)
                        for t in range(CT):
                            mm = nc.tensor.matmul(acc_down[:, n % 2], w_down[:, t], xn[:, t, tokens(n)], start=t == 0, stop=t == CT - 1)
                        mm.then_inc(down_sum, 1)
                    if n >= 1:
                        pe.wait_ge(down_ready, n)
                        if n >= 3:
                            pe.wait_ge(gate_ready, (n - 2) * CT)
                        for o in range(CT):
                            nc.tensor.matmul(acc_up[:, (n - 1) % 2, o], w_up[:, o * P:(o + 1) * P], down[:, (n - 1) % 2],
                                             start=True, stop=True).then_inc(up_sum, 1)

            @block.scalar
            def _(act):
                def gates(act, n):
                    for o in range(CT):
                        act.wait_ge(up_sum, n * CT + o + 1)
                        nc.scalar.activation(gate[:, o, tokens(n)], acc_up[:, n % 2, o], ACT.Sigmoid).then_inc(gate_ready, 1)

                act.wait_ge(loaded, 64)
                for n in range(NBLK):
                    act.wait_ge(ab_sum, n + 1)
                    nc.scalar.activation(ab[:, tokens(n)], acc[0:2 * HEADS, n % 2], ACT.Sigmoid, bias=b_ab[:, 0:1]).then_inc(ab_ready, 1)
                    act.wait_ge(down_sum, n + 1)
                    if n >= 2:
                        act.wait_ge(up_sum, (n - 1) * CT)
                    nc.scalar.activation(down[:, n % 2], acc_down[:, n % 2], ACT.Silu).then_inc(down_ready, 1)
                    if n >= 1:
                        gates(act, n - 1)
                gates(act, NBLK - 1)

            @block.vector
            def _(dve):
                for n in range(NBLK):
                    dve.wait_ge(ab_ready, n + 1)
                    nc.vector.tensor_scalar(ab[:, tokens(n)], ab[:, tokens(n)], b_ab[:, 1:2], 1.0, ALU.max, ALU.min).then_inc(ab_clipped, 1)


def delta_projections(nc, c, dram, stage, xn, qkv):
    with Scope(nc, stage) as s:
        w_in = s.sb("w_in", [P, 3, CT, D])
        taps = s.sb("taps", [P, 3, CT, TAPS + 1])
        pre = s.sb("pre", [P, 2, B, T + TAPS - 1])
        acc = s.ps("acc", [P, 4, BLK])
        loaded, zeroed, acc_ready, pre_ready, tap_done, silu_done = (
            s.sem("loaded"), s.sem("zeroed"), s.sem("acc_ready"), s.sem("pre_ready"), s.sem("tap_done"), s.sem("silu_done"))
        rounds = [(w, tile) for w in range(3) for tile in range(CT)]
        PER_ROUND = TAPS * B
        HALF = NBLK // B

        with nc.Block() as block:

            @block.sync
            def _(sp):
                sp.dma_start(w_in[:], dram["delta_w_in"]).then_inc(loaded, 16)
                sp.dma_start(taps[:], dram["delta_taps"]).then_inc(loaded, 16)

            @block.tensor
            def _(pe):
                pe.wait_ge(loaded, 32)
                for r, (w, tile) in enumerate(rounds):
                    for n in range(NBLK):
                        k = r * NBLK + n
                        if k >= 4:
                            pe.wait_ge(pre_ready, k - 3)
                        for t in range(CT):
                            mm = nc.tensor.matmul(acc[:, k % 4], w_in[:, w, t, tile * P:(tile + 1) * P], xn[:, t, tokens(n)],
                                                  start=t == 0, stop=t == CT - 1)
                        mm.then_inc(acc_ready, 1)

            @block.scalar
            def _(act):
                def silu(r):
                    w, tile = rounds[r]
                    for b in range(B):
                        act.wait_ge(tap_done, r * PER_ROUND + (TAPS - 1) * B + b + 1)
                        part = qkv[:, w, tile, b * T:(b + 1) * T]
                        nc.scalar.activation(part, part, ACT.Silu, bias=taps[:, w, tile, TAPS:TAPS + 1]).then_inc(silu_done, 1)

                act.wait_ge(zeroed, 1)
                for r in range(len(rounds)):
                    if r >= 2:
                        act.wait_ge(tap_done, (r - 1) * PER_ROUND)
                    for n in range(NBLK):
                        act.wait_ge(acc_ready, r * NBLK + n + 1)
                        at = TAPS - 1 + n % HALF * BLK
                        nc.scalar.activation(pre[:, r % 2, n // HALF, at:at + BLK], acc[:, (r * NBLK + n) % 4], ACT.Copy).then_inc(pre_ready, 1)
                    if r >= 1:
                        silu(r - 1)
                silu(len(rounds) - 1)

            @block.vector
            def _(dve):
                nc.vector.memset(pre[:, :, :, 0:TAPS - 1], 0.0).then_inc(zeroed, 1)
                for r, (w, tile) in enumerate(rounds):
                    for tap in range(TAPS):
                        for b in range(B):
                            part = qkv[:, w, tile, b * T:(b + 1) * T]
                            moved = pre[:, r % 2, b, tap:tap + T]
                            if tap == 0:
                                dve.wait_ge(pre_ready, r * NBLK + (b + 1) * HALF)
                                ins = nc.vector.tensor_scalar(part, moved, taps[:, w, tile, tap:tap + 1], None, ALU.mult)
                            else:
                                dve.wait_ge(tap_done, r * PER_ROUND + (tap - 1) * B + b + 1)
                                ins = nc.vector.scalar_tensor_tensor(part, moved, taps[:, w, tile, tap:tap + 1], part, ALU.mult, ALU.add)
                            ins.then_inc(tap_done, 1)


def delta_normalise(nc, c, dram, stage, qkv):
    with Scope(nc, stage) as s:
        squares = s.sb("squares", [P, 2, BLK])
        log_sq = s.sb("log_sq", [P, 2, BLK])
        inv = s.sb("inv", [P, 2, BLK])
        sums = s.ps("sums", [P, 2, BLK])
        squares_ready, sums_ready, log_ready, inv_ready, unit_ready = (
            s.sem("squares_ready"), s.sem("sums_ready"), s.sem("log_ready"), s.sem("inv_ready"), s.sem("unit_ready"))
        negated, stored = s.sem("negated"), s.sem("stored")
        steps = [(w, tile, n) for w in range(2) for tile in range(CT) for n in range(NBLK)]

        with nc.Block() as block:

            @block.sync
            def _(sp):
                def put(sp, name, tiles):
                    for b in range(B):
                        for tile in range(CT):
                            sp.dma_start(dram[name][b, :, tile * P:(tile + 1) * P].rearrange("r p t -> p r t"),
                                         tiles[:, tile, b * T:(b + 1) * T].rearrange("p (r t) -> p r t", t=SPAN)).then_inc(stored, 16)

                sp.wait_ge(negated, CT)
                put(sp, "delta_v", qkv[:, 2])
                sp.wait_ge(unit_ready, len(steps))
                put(sp, "delta_q", qkv[:, 0])
                put(sp, "delta_k", qkv[:, 1])
                sp.wait_ge(stored, 3 * CT * B * 16)

            @block.tensor
            def _(pe):
                for k, (w, tile, n) in enumerate(steps):
                    pe.wait_ge(squares_ready, k + 1)
                    if k >= 2:
                        pe.wait_ge(log_ready, k - 1)
                    nc.tensor.matmul(sums[:, k % 2], c["head_sum"][:], squares[:, k % 2], start=True, stop=True).then_inc(sums_ready, 1)

            @block.scalar
            def _(act):
                def lengths(k):
                    act.wait_ge(sums_ready, k + 1)
                    nc.scalar.activation(log_sq[:, k % 2], sums[:, k % 2], ACT.Ln).then_inc(log_ready, 1)
                    act.wait_ge(log_ready, k + 1)
                    if k >= 2:
                        act.wait_ge(unit_ready, k - 1)
                    nc.scalar.activation(inv[:, k % 2], log_sq[:, k % 2], ACT.Exp, scale=-0.5).then_inc(inv_ready, 1)

                nc.scalar.preload_act_table_set(LOG_EXP_SET)
                for k, (w, tile, n) in enumerate(steps):
                    if k >= 2:
                        act.wait_ge(sums_ready, k - 1)
                    nc.scalar.activation(squares[:, k % 2], qkv[:, w, tile, tokens(n)], ACT.Square).then_inc(squares_ready, 1)
                    if k >= 1:
                        lengths(k - 1)
                lengths(len(steps) - 1)

            @block.vector
            def _(dve):
                for tile in range(CT):
                    nc.vector.tensor_scalar(qkv[:, 2, tile], qkv[:, 2, tile], -1.0, None, ALU.mult).then_inc(negated, 1)
                for k, (w, tile, n) in enumerate(steps):
                    dve.wait_ge(inv_ready, k + 1)
                    part = qkv[:, w, tile, tokens(n)]
                    nc.vector.scalar_tensor_tensor(part, inv[:, k % 2], 1e6, part, ALU.min, ALU.mult).then_inc(unit_ready, 1)


def delta_chunks(nc, c, dram, stage, number):
    PARTS = P // BH
    RUNS = T // SPAN // PARTS // 2
    N_CHUNKS = RUNS * CHUNKS
    C = CHUNK
    with Scope(nc, stage) as s:
        kq = s.sb("kq", [P, 2, RUNS, HD, SPAN])
        ab = s.sb("ab", [P, 2, RUNS * SPAN])
        g = s.sb("g", [P, N_CHUNKS, C + 1, C + 1])
        gram = s.sb("gram", [P, 2, N_CHUNKS, C, C])
        solve = s.sb("solve", [P, N_CHUNKS, C, C])
        terms = s.sb("terms", [P, 4, CHUNKS, C, HD])
        own_terms = s.sb("own_terms", [P, 2, CHUNKS, C, HD])
        solve_terms = s.sb("solve_terms", [P, N_CHUNKS, C - 1, C - 1])
        record = s.sb("record", [P, 2, CHUNKS, RECORD])
        loaded, zeroed, terms_ready, terms_read, g_step = s.sem("loaded"), s.sem("zeroed"), s.sem("terms_ready"), s.sem("terms_read"), s.sem("g_step")
        own_ready, own_read = s.sem("own_ready"), s.sem("own_read")
        solve_step, copied, pool_done, dve_done = s.sem("solve_step"), s.sem("copied"), s.sem("pool_done"), s.sem("dve_done")
        stored = [s.sem(f"stored{slot}") for slot in range(2)]
        rows = [(run, w, t) for run in range(RUNS) for w in range(2) for t in range(C) if w == 1 or t >= 1]
        own_rows = [row for row in rows if row[2] % 3 == 1]
        pool_rows = [row for row in rows if row[2] % 3 != 1]
        LOADED = 4 * B * PARTS * 16
        alpha = ab[:, 0].rearrange("p (n t) -> p n t", t=C)
        beta = ab[:, 1].rearrange("p (n t) -> p n t", t=C)
        SLOTS = 4
        SOLVED = 3 + 2 * (C - 1)

        def by_token(w, run):
            return kq[:, w, run].rearrange("p i (m u) -> p m u i", u=C)

        def multiply_row(engine, out, run, w, t):
            return engine.tensor_tensor(out[:, :, 0:t + w], by_token(0, run)[:, :, 0:t + w],
                                        by_token(w, run)[:, :, t].unsqueeze(2).broadcast_to([P, CHUNKS, t + w, HD]), ALU.mult)

        with nc.Block() as block:

            @block.sync
            def _(sp):
                for b in range(B):
                    for part in range(PARTS):
                        at = slice((b * PARTS + part) * HEADS, (b * PARTS + part + 1) * HEADS)
                        first = (part * 2 + number) * RUNS
                        for w, name in enumerate(("delta_k", "delta_q")):
                            sp.dma_start(kq[at, w].rearrange("p r i t -> p r (i t)"),
                                         dram[name][b, first:first + RUNS].rearrange("r (h i) t -> h r (i t)", i=HD)).then_inc(loaded, 16)
                            sp.dma_start(ab[at, w], dram["delta_ab"][b, w * HEADS:(w + 1) * HEADS, first * SPAN:(first + RUNS) * SPAN]).then_inc(loaded, 16)
                for run in range(RUNS):
                    sp.wait_ge(copied, run * 2 + 2)
                    sp.wait_ge(pool_done, run * 2 + 2)
                    sp.wait_ge(dve_done, run * 2 + 2)
                    for b in range(B):
                        for part in range(PARTS):
                            at = slice((b * PARTS + part) * HEADS, (b * PARTS + part + 1) * HEADS)
                            sp.dma_start(dram["delta_record"][b, (part * 2 + number) * RUNS + run], record[at, run % 2].rearrange("p m e -> p (m e)")
                                         ).then_inc(stored[run % 2], 16)
                for slot in range(2):
                    sp.wait_ge(stored[slot], RUNS // 2 * B * PARTS * 16)

            @block.gpsimd
            def _(pool):
                pool.wait_ge(loaded, LOADED)
                for k, (run, w, t) in enumerate(pool_rows):
                    if k >= SLOTS:
                        pool.wait_ge(terms_read, k - SLOTS + 1)
                    multiply_row(nc.gpsimd, terms[:, k % SLOTS], run, w, t).then_inc(terms_ready, 1)
                pool.wait_ge(g_step, C + 1)
                for run in range(RUNS):
                    at = slice(run * CHUNKS, (run + 1) * CHUNKS)
                    if run >= 2:
                        pool.wait_ge(stored[run % 2], run // 2 * B * PARTS * 16)
                    for w, first, place in ((0, 0, K_IN), (1, 1, Q_IN)):
                        nc.gpsimd.tensor_tensor(record[:, run % 2, :, place:place + C * HD].rearrange("p m (t i) -> p m t i", i=HD), by_token(w, run),
                                                g[:, at, first:first + C, 0].unsqueeze(3).broadcast_to([P, CHUNKS, C, HD]), ALU.mult
                                                ).then_inc(pool_done, 1)

            @block.scalar
            def _(act):
                act.wait_ge(solve_step, SOLVED)
                for run in range(RUNS):
                    at = slice(run * CHUNKS, (run + 1) * CHUNKS)
                    if run >= 2:
                        act.wait_ge(stored[run % 2], run // 2 * B * PARTS * 16)
                    nc.scalar.activation(record[:, run % 2, :, SOLVE:SOLVE + C * C], solve[:, at].rearrange("p n t s -> p n (t s)"), ACT.Copy).then_inc(copied, 1)
                    nc.scalar.activation(record[:, run % 2, :, DECAY], g[:, at, C, 0], ACT.Copy).then_inc(copied, 1)

            @block.vector
            def _(dve):
                nc.vector.memset(g[:], 1.0).then_inc(g_step, 1)
                nc.vector.memset(gram[:], 0.0).then_inc(zeroed, 1)
                nc.vector.memset(solve[:], 0.0).then_inc(zeroed, 1)
                dve.wait_ge(loaded, LOADED)
                for t in range(C):
                    dve.wait_ge(g_step, t + 1)
                    nc.vector.tensor_tensor(g[:, :, t + 1, 0:t + 1], g[:, :, t, 0:t + 1], alpha[:, :, t].unsqueeze(2).broadcast_to([P, N_CHUNKS, t + 1]),
                                            ALU.mult).then_inc(g_step, 1)
                dve.wait_ge(zeroed, 2)
                def sum_row(out, run, w, t):
                    return nc.vector.tensor_reduce(gram[:, w, run * CHUNKS:(run + 1) * CHUNKS, t, 0:t + w], out[:, :, 0:t + w], AX.X, ALU.add)

                own = 0
                for k, row in enumerate(pool_rows):
                    dve.wait_ge(terms_ready, k + 1)
                    sum_row(terms[:, k % SLOTS], *row).then_inc(terms_read, 1)
                    if own < len(own_rows) and own * len(pool_rows) <= k * len(own_rows):
                        if own >= 2:
                            dve.wait_ge(own_read, own - 1)
                        multiply_row(nc.vector, own_terms[:, own % 2], *own_rows[own]).then_inc(own_ready, 1)
                        if own >= 1:
                            dve.wait_ge(own_ready, own)
                            sum_row(own_terms[:, (own - 1) % 2], *own_rows[own - 1]).then_inc(own_read, 1)
                        own += 1
                dve.wait_ge(own_ready, len(own_rows))
                sum_row(own_terms[:, (own - 1) % 2], *own_rows[-1]).then_inc(own_read, 1)
                dve.wait_ge(terms_read, len(pool_rows))
                dve.wait_ge(own_read, len(own_rows))
                dve.wait_ge(g_step, C + 1)
                low = gram[:, 0, :, 1:, 0:C - 1]
                nc.vector.tensor_tensor(low, low, g[:, :, 1:C, 1:C], ALU.mult).then_inc(solve_step, 1)
                nc.vector.tensor_scalar(solve[:].rearrange("p n t s -> p n (t s)")[:, :, 0:C * C:C + 1], beta, -1.0, None, ALU.mult).then_inc(solve_step, 1)
                dve.wait_ge(solve_step, 2)
                nc.vector.tensor_tensor(low, low, beta[:, :, 1:].unsqueeze(3).broadcast_to([P, N_CHUNKS, C - 1, C - 1]), ALU.mult).then_inc(solve_step, 1)
                for t in range(1, C):
                    dve.wait_ge(solve_step, 3 + 2 * (t - 1))
                    nc.vector.tensor_tensor(solve_terms[:, :, 0:t, 0:t], solve[:, :, 0:t, 0:t].rearrange("p n s c -> p n c s"),
                                            gram[:, 0, :, t, 0:t].unsqueeze(2).broadcast_to([P, N_CHUNKS, t, t]), ALU.mult).then_inc(solve_step, 1)
                    dve.wait_ge(solve_step, 3 + 2 * (t - 1) + 1)
                    nc.vector.tensor_reduce(solve[:, :, t, 0:t], solve_terms[:, :, 0:t, 0:t], AX.X, ALU.add, negate=True).then_inc(solve_step, 1)
                for run in range(RUNS):
                    at = slice(run * CHUNKS, (run + 1) * CHUNKS)
                    if run >= 2:
                        dve.wait_ge(stored[run % 2], run // 2 * B * PARTS * 16)
                    nc.vector.tensor_tensor(record[:, run % 2, :, MIX:MIX + C * C].rearrange("p m (t s) -> p m t s", s=C), gram[:, 1, at],
                                            g[:, at, 1:, 1:], ALU.mult).then_inc(dve_done, 1)
                    nc.vector.tensor_tensor(record[:, run % 2, :, K_OUT:K_OUT + C * HD].rearrange("p m (i s) -> p m i s", s=C),
                                            kq[:, 0, run].rearrange("p i (m u) -> p m i u", u=C),
                                            g[:, at, C, 1:].unsqueeze(2).broadcast_to([P, CHUNKS, HD, C]), ALU.mult).then_inc(dve_done, 1)


def delta_recurrence(nc, c, dram, stage):
    C = CHUNK
    with Scope(nc, stage) as s:
        record = s.sb("record", [P, 2, CHUNKS, RECORD])
        vt = s.sb("vt", [P, 2, JQ, SPAN])
        state = s.sb("state", [P, 4, JQ, HD])
        terms = s.sb("terms", [P, 2, CHUNKS, JQ, C, HD + 1])
        error = s.sb("error", [P, 2, JQ, C])
        u_terms = s.sb("u_terms", [P, 2, JQ, C, C])
        u = s.sb("u", [P, 4, JQ, C])
        s_terms = s.sb("s_terms", [P, 2, JQ, HD, C + 1])
        o_terms = s.sb("o_terms", [P, 2, JQ, C, HD + C])
        FOLD = (HD + C) // 2
        o_halves = s.sb("o_halves", [P, 2, JQ, C, FOLD])
        o_out = s.sb("o_out", [P, 2, JQ, SPAN])
        loaded = [s.sem(f"loaded{slot}") for slot in range(2)]
        stored = [s.sem(f"stored{slot}") for slot in range(2)]
        o_halves_ready = s.sem("o_halves_ready")
        chain, v_ready, decayed, o_terms_ready, o_ready = s.sem("chain"), s.sem("v_ready"), s.sem("decayed"), s.sem("o_terms_ready"), s.sem("o_ready")
        ROUNDS = T // SPAN
        LOADS = 3 * B * 16 - B * 16
        STEP = 6
        BEFORE = STEP * CHUNKS * 2
        C0 = BEFORE + 1
        O_CREDIT = 2 * CHUNKS

        with nc.Block() as block:

            @block.sync
            def _(sp):
                def load(pair, slot):
                    for b in range(B):
                        half = slice(b * P // B, (b + 1) * P // B)
                        chunk = bass.ds(pair * 2 + slot, 1)
                        sp.dma_start(record[half, slot].rearrange("p m e -> p (m e)"), dram["delta_record"][b, chunk].squeeze(0).unsqueeze(1)
                                     .broadcast_to([HEADS, QUARTERS, CHUNKS * RECORD])).then_inc(loaded[slot], 16)
                        sp.dma_start(vt[half, slot], dram["delta_v"][b, chunk].rearrange("r (p j) t -> (r p) (j t)", j=JQ)).then_inc(loaded[slot], 16)

                def store(pair, slot):
                    sp.wait_ge(o_ready, (pair * 2 + slot + 1) * CHUNKS + O_CREDIT)
                    for b in range(B):
                        half = slice(b * P // B, (b + 1) * P // B)
                        sp.dma_start(dram["delta_o"][b, bass.ds(pair * 2 + slot, 1)].rearrange("r (p j) t -> (r p) (j t)", j=JQ),
                                     o_out[half, slot]).then_inc(stored[slot], 16)

                for slot in range(2):
                    load(0, slot)
                with sp.Fori(1, ROUNDS // 2) as pair:
                    for slot in range(2):
                        store(pair - 1, slot)
                        load(pair, slot)
                for slot in range(2):
                    store(ROUNDS // 2 - 1, slot)
                for slot in range(2):
                    sp.wait_ge(stored[slot], ROUNDS // 2 * 32 + 32)

            @block.scalar
            def _(act):
                with act.Fori(0, ROUNDS // 2) as pair:
                    for slot in range(2):
                        act.wait_ge(loaded[slot], (pair + 1) * LOADS)
                        act.wait_ge(chain, (pair * 2 + slot) * CHUNKS * STEP + 1)
                        for j in range(JQ):
                            ins = nc.scalar.activation(terms[:, slot, :, j, :, HD], vt[:, slot, j].rearrange("p (m t) -> p m t", t=C), ACT.Copy)
                        ins.then_inc(v_ready, 1)
                        for m in range(CHUNKS):
                            act.wait_ge(chain, ((pair * 2 + slot) * CHUNKS + m) * STEP + C0)
                            nc.scalar.activation(s_terms[:, m % 2, :, :, C], state[:, (m - 1) % 4], ACT.Copy,
                                                 scale=record[:, slot, m, DECAY:DECAY + 1]).then_inc(decayed, 1)

            @block.gpsimd
            def _(pool):
                with pool.Fori(0, ROUNDS // 2) as pair:
                    for slot in range(2):
                        pool.wait_ge(loaded[slot], (pair + 1) * LOADS)
                        for m in range(CHUNKS):
                            number = (pair * 2 + slot) * CHUNKS + m
                            table = record[:, slot, m]
                            pool.wait_ge(chain, number * STEP + C0)
                            nc.gpsimd.tensor_tensor(o_terms[:, m % 2, :, :, 0:HD], state[:, (m - 1) % 4].unsqueeze(2).broadcast_to([P, JQ, C, HD]),
                                                    table[:, Q_IN:Q_IN + C * HD].rearrange("p (t i) -> p t i", i=HD).unsqueeze(1)
                                                    .broadcast_to([P, JQ, C, HD]), ALU.mult).then_inc(o_terms_ready, 1)
                            pool.wait_ge(chain, number * STEP + C0 + 4)
                            nc.gpsimd.tensor_tensor(o_terms[:, m % 2, :, :, HD:], u[:, m % 4].unsqueeze(2).broadcast_to([P, JQ, C, C]),
                                                    table[:, MIX:MIX + C * C].rearrange("p (t s) -> p t s", s=C).unsqueeze(1)
                                                    .broadcast_to([P, JQ, C, C]), ALU.mult).then_inc(o_terms_ready, 1)
                            pool.wait_ge(o_terms_ready, number * 2 + 2)
                            pool.wait_ge(o_ready, number + O_CREDIT - 1)
                            nc.gpsimd.tensor_tensor(o_halves[:, m % 2], o_terms[:, m % 2, :, :, 0:FOLD], o_terms[:, m % 2, :, :, FOLD:], ALU.add
                                                    ).then_inc(o_halves_ready, 1)

            @block.vector
            def _(dve):
                def outputs(pair, slot, m):
                    dve.wait_ge(o_halves_ready, (pair * 2 + slot) * CHUNKS + m + 1)
                    if m == 0:
                        dve.wait_ge(stored[slot], pair * 32 + 32)
                    nc.vector.tensor_reduce(o_out[:, slot, :, m * C:(m + 1) * C], o_halves[:, m % 2], AX.X, ALU.add).then_inc(o_ready, 1)

                def product(out, matrix, vector, rows, columns):
                    return nc.vector.tensor_tensor(out, matrix.rearrange("p (r c) -> p r c", c=columns).unsqueeze(1).broadcast_to([P, JQ, rows, columns]),
                                                   vector.unsqueeze(2).broadcast_to([P, JQ, rows, columns]), ALU.mult)

                dve.sem_inc(chain, BEFORE)
                dve.wait_ge(chain, BEFORE)
                nc.vector.memset(state[:, 3], 0.0).then_inc(chain, 1)
                dve.sem_inc(o_ready, O_CREDIT)
                for slot in range(2):
                    dve.sem_inc(stored[slot], 32)
                with dve.Fori(0, ROUNDS // 2) as pair:
                    for slot in range(2):
                        dve.wait_ge(v_ready, pair * 2 + slot + 1)
                        for m in range(CHUNKS):
                            number = (pair * 2 + slot) * CHUNKS + m
                            done = number * STEP + C0
                            table = record[:, slot, m]
                            dve.wait_ge(chain, done)
                            product(terms[:, slot, m, :, :, 0:HD], table[:, K_IN:K_IN + C * HD], state[:, (m - 1) % 4], C, HD).then_inc(chain, 1)
                            dve.wait_ge(chain, done + 1)
                            nc.vector.tensor_reduce(error[:, m % 2], terms[:, slot, m], AX.X, ALU.add).then_inc(chain, 1)
                            dve.wait_ge(chain, done + 2)
                            product(u_terms[:, m % 2], table[:, SOLVE:SOLVE + C * C], error[:, m % 2], C, C).then_inc(chain, 1)
                            dve.wait_ge(chain, done + 3)
                            nc.vector.tensor_reduce(u[:, m % 4], u_terms[:, m % 2], AX.X, ALU.add).then_inc(chain, 1)
                            dve.wait_ge(chain, done + 4)
                            product(s_terms[:, m % 2, :, :, 0:C], table[:, K_OUT:K_OUT + C * HD], u[:, m % 4], HD, C).then_inc(chain, 1)
                            if m >= 1:
                                outputs(pair, slot, m - 1)
                            dve.wait_ge(chain, done + 5)
                            dve.wait_ge(decayed, number + 1)
                            nc.vector.tensor_reduce(state[:, m % 4], s_terms[:, m % 2], AX.X, ALU.add).then_inc(chain, 1)
                        outputs(pair, slot, CHUNKS - 1)


def delta_output(nc, c, dram, stage):
    x = c["x"]
    with Scope(nc, stage) as s:
        o_all = s.sb("o_all", [P, CT, N])
        gate = s.sb("gate", [P, CT, N])
        w_o = s.sb("w_o", [P, CT, D])
        rms_w = s.sb("rms_w", [P, CT])
        eps = s.sb("eps", [P, 1])
        squares = s.sb("squares", [P, 2, CT, BLK])
        log_sq = s.sb("log_sq", [P, 2, CT, BLK])
        inv = s.sb("inv", [P, 2, CT, BLK])
        sums = s.ps("sums", [P, 2, CT, BLK])
        acc = s.ps("acc", [P, 2, CT, BLK])
        loaded, eps_ready, squares_ready, sums_ready, log_ready, inv_ready, step_done, acc_ready, added = (
            s.sem("loaded"), s.sem("eps_ready"), s.sem("squares_ready"), s.sem("sums_ready"), s.sem("log_ready"), s.sem("inv_ready"),
            s.sem("step_done"), s.sem("acc_ready"), s.sem("added"))

        with nc.Block() as block:

            @block.sync
            def _(sp):
                for tile in range(CT):
                    for b in range(B):
                        sp.dma_start(o_all[:, tile, b * T:(b + 1) * T].rearrange("p (r t) -> p r t", t=SPAN),
                                     dram["delta_o"][b, :, tile * P:(tile + 1) * P].rearrange("r p t -> p r t")).then_inc(loaded, 16)
                for tile, table in ((gate, "delta_gate"), (w_o, "delta_w_o"), (rms_w, "delta_rms_w")):
                    sp.dma_start(tile[:], dram[table]).then_inc(loaded, 16)

            @block.tensor
            def _(pe):
                for n in range(NBLK + 1):
                    if n < NBLK:
                        pe.wait_ge(squares_ready, n + 1)
                        if n >= 2:
                            pe.wait_ge(log_ready, n - 1)
                        for tile in range(CT):
                            mm = nc.tensor.matmul(sums[:, n % 2, tile], c["head_sum"][:], squares[:, n % 2, tile], start=True, stop=True)
                        mm.then_inc(sums_ready, 1)
                    if n >= 1:
                        pe.wait_ge(step_done, n * 2 * CT)
                        if n >= 3:
                            pe.wait_ge(added, n - 2)
                        for o in range(CT):
                            for tile in range(CT):
                                mm = nc.tensor.matmul(acc[:, (n - 1) % 2, o], w_o[:, tile, o * P:(o + 1) * P], o_all[:, tile, tokens(n - 1)],
                                                      start=tile == 0, stop=tile == CT - 1)
                        mm.then_inc(acc_ready, 1)

            @block.scalar
            def _(act):
                def lengths(n):
                    act.wait_ge(sums_ready, n + 1)
                    nc.scalar.activation(log_sq[:, n % 2], sums[:, n % 2], ACT.Ln, bias=eps[:, 0:1], scale=1.0 / 16).then_inc(log_ready, 1)
                    act.wait_ge(log_ready, n + 1)
                    if n >= 2:
                        act.wait_ge(step_done, (n - 1) * 2 * CT)
                    nc.scalar.activation(inv[:, n % 2], log_sq[:, n % 2], ACT.Exp, scale=-0.5).then_inc(inv_ready, 1)

                nc.scalar.preload_act_table_set(LOG_EXP_SET)
                act.wait_ge(eps_ready, 1)
                act.wait_ge(loaded, 16 * (CT * B + 3))
                for n in range(NBLK):
                    if n >= 2:
                        act.wait_ge(sums_ready, n - 1)
                    nc.scalar.activation(squares[:, n % 2], o_all[:, :, tokens(n)], ACT.Square).then_inc(squares_ready, 1)
                    if n >= 1:
                        lengths(n - 1)
                lengths(NBLK - 1)

            @block.vector
            def _(dve):
                nc.vector.memset(eps[:], RMS_EPS).then_inc(eps_ready, 1)
                dve.wait_ge(loaded, 16 * (CT * B + 3))
                for n in range(NBLK + 1):
                    if n < NBLK:
                        dve.wait_ge(inv_ready, n + 1)
                        for tile in range(CT):
                            nc.vector.scalar_tensor_tensor(inv[:, n % 2, tile], inv[:, n % 2, tile], rms_w[:, tile:tile + 1], gate[:, tile, tokens(n)],
                                                           ALU.mult, ALU.mult).then_inc(step_done, 1)
                        for tile in range(CT):
                            dve.wait_ge(step_done, n * 2 * CT + tile + 1)
                            nc.vector.tensor_tensor(o_all[:, tile, tokens(n)], o_all[:, tile, tokens(n)], inv[:, n % 2, tile], ALU.mult).then_inc(step_done, 1)
                    if n >= 1:
                        dve.wait_ge(acc_ready, n)
                        nc.vector.tensor_tensor(x[:, :, tokens(n - 1)], x[:, :, tokens(n - 1)], acc[:, (n - 1) % 2], ALU.add).then_inc(added, 1)


def delta_attention(nc, c, dram, stage):
    for name in ("delta_q", "delta_k", "delta_v", "delta_o"):
        dram[name] = nc.dram_tensor(name, (B, T // SPAN, D, SPAN), F32, kind="Internal").ap()
    dram["delta_ab"] = nc.dram_tensor("delta_ab", (B, 2 * HEADS, T), F32, kind="Internal").ap()
    dram["delta_record"] = nc.dram_tensor("delta_record", (B, T // SPAN, HEADS, CHUNKS * RECORD), F32, kind="Internal").ap()
    dram["delta_gate"] = nc.dram_tensor("delta_gate", (P, CT, N), F32, kind="Internal").ap()
    with Scope(nc, stage) as normed:
        xn = normed.sb("xn", [P, CT, N])
        layer_norm(nc, c, f"{stage}_ln", xn, None)
        delta_gates(nc, c, dram, f"{stage}_gates", xn)
        with Scope(nc, f"{stage}_qkv") as s:
            qkv = s.sb("qkv", [P, 3, CT, N])
            delta_projections(nc, c, dram, f"{stage}_in", xn, qkv)
            delta_normalise(nc, c, dram, f"{stage}_unit", qkv)
    for part in range(2):
        delta_chunks(nc, c, dram, f"{stage}_chunks{part}", part)
    delta_recurrence(nc, c, dram, f"{stage}_scan")
    delta_output(nc, c, dram, f"{stage}_out")



def build(nc, dram):
    with Scope(nc, "main") as s:
        c = {
            "x": s.sb("x", [P, CT, N]),
            "mean_matrix": s.sb("mean_matrix", [P, P]),
            "identity": s.sb("identity", [P, P]),
            "head_mask": s.sb("head_mask", [P, 8]),
            "head_sum": s.sb("head_sum", [P, P]),
            "ln_eps": s.sb("ln_eps", [P, 1]),
        }
        load_constants(nc, c, dram)
        gated_experts(nc, c, dram, "ffn0")
        delta_attention(nc, c, dram, "delta")
        gated_experts(nc, c, dram, "ffn1")
        prototype_mixture(nc, c, dram, "mix0")
        helical_attention(nc, c, dram, "att")
        prototype_mixture(nc, c, dram, "mix1")
        store_result(nc, c, dram)


def lay_out(inputs):
    import numpy as np

    def rows(a):
        return np.ascontiguousarray(a.reshape(CT, P, -1).transpose(1, 0, 2))

    def helical_weights(w):
        out = np.zeros((8, HD, CT, 2, 2, QG, PAIRS), np.float32)
        for head in range(HEADS):
            tile, of_eight = divmod(head, 8)
            half, of_four = divmod(of_eight, QG)
            out[of_eight, :, tile, half, :, of_four] = w[head].reshape(PAIRS, 2, HD).transpose(2, 1, 0)
        return out.reshape(P, CT, 2, 2, P)

    arrays = {
        "x": rows(inputs["L0_attn_x"].reshape(N, D).T),
        "mean_matrix": np.full((P, P), 1.0 / D, np.float32),
        "identity": np.eye(P, dtype=np.float32),
        "head_mask": np.kron(np.eye(8, dtype=np.float32), np.ones((16, 1), np.float32)),
        "head_sum": np.kron(np.eye(8, dtype=np.float32), np.ones((16, 16), np.float32)),
        "gate_w": rows(inputs["L0_ffn_gate_w"].T),
        "gate_b": np.tile(inputs["L0_ffn_gate_b"], (P, 1)),
        "expert": np.concatenate([
            inputs["L0_ffn_expert_w"].transpose(0, 2, 1).reshape(-1, CT, P, D).transpose(2, 0, 1, 3).reshape(P, -1, CT * D),
            inputs["L0_ffn_expert_b"].reshape(-1, CT, P).transpose(2, 0, 1)], axis=2),
        "proto": rows(inputs["L1_ffn_prototypes"].T),
        "proto_rows": inputs["L1_ffn_prototypes"],
        "temp": np.full((P, 1), inputs["L1_ffn_temp"]),
        "numbers": np.tile(np.arange(inputs["L1_ffn_prototypes"].shape[0], dtype=np.float32), (P, 1)),
        "proto_B": rows(inputs["L1_ffn_B"].reshape(-1, D).T),
        "proto_A": np.ascontiguousarray(inputs["L1_ffn_A"].transpose(0, 2, 1).reshape(-1, P, D).transpose(1, 0, 2)),
        "proto_bias": inputs["L1_ffn_bias"],
        "proto_spread": np.kron(np.eye(inputs["L1_ffn_B"].shape[0], dtype=np.float32), np.ones((1, inputs["L1_ffn_B"].shape[1]), np.float32)),
        "att_w_qk": np.stack([rows(inputs["L1_attn_Wq"].T), rows(inputs["L1_attn_Wk"].T)], axis=1),
        "att_w_v": rows(inputs["L1_attn_Wv"].T),
        "att_b_qk": np.stack([inputs["L1_attn_bq"].reshape(CT, P), inputs["L1_attn_bk"].reshape(CT, P)]).transpose(2, 0, 1).copy(),
        "att_b_v": np.tile(inputs["L1_attn_bv"], (P, 1)),
        "att_w_o": rows(inputs["L1_attn_Wo"].T),
        "att_b_o": inputs["L1_attn_bo"].reshape(CT, P).T.copy(),
        "att_hel_w": helical_weights(inputs["L1_attn_Whel"]),
        "att_hel_b": np.ascontiguousarray(inputs["L1_attn_bhel"].reshape(CT, 2, QG, PAIRS, 2).transpose(2, 3, 0, 1, 4).reshape(P, CT, 2, 2)),
        "delta_w_in": np.stack([rows(inputs[f"L0_attn_W{n}"]) for n in "qkv"], axis=1),
        "delta_taps": np.stack([np.concatenate([inputs[f"L0_attn_{n}cw"], inputs[f"L0_attn_{n}cb"][:, None]], axis=1).reshape(CT, P, TAPS + 1)
                                for n in "qkv"]).transpose(2, 0, 1, 3).copy(),
        "delta_w_ab": np.concatenate([rows(inputs["L0_attn_Wa"]), rows(inputs["L0_attn_Wb"])], axis=2),
        "delta_b_ab": np.stack([np.concatenate([inputs["L0_attn_ba"], inputs["L0_attn_bb"]]),
                                np.repeat(np.array([ALPHA_MIN, 0.0], np.float32), HEADS)], axis=1),
        "delta_w_down": rows(inputs["L0_attn_Wgd"]),
        "delta_w_up": inputs["L0_attn_Wgu"],
        "delta_spread": np.concatenate([np.zeros((HEADS, D), np.float32), np.kron(np.eye(HEADS, dtype=np.float32), np.ones((1, HD), np.float32))]
                                       ).reshape(2 * HEADS, CT, P),
        "delta_w_o": rows(inputs["L0_attn_Wo"]),
        "delta_rms_w": inputs["L0_attn_rms_w"].reshape(CT, P).T.copy(),
    }
    return arrays


def kernel(**inputs):
    import numpy as np
    import concourse.bacc as bacc
    from concourse.bass_utils import run_bass_kernel_spmd

    nc = bacc.Bacc("TRN2", target_bir_lowering=False, num_devices=1)
    arrays, dram = {}, {}
    for name, a in lay_out({k: np.asarray(v) for k, v in inputs.items()}).items():
        arrays[f"in_{name}"] = a
        dram[name] = nc.dram_tensor(f"in_{name}", a.shape, mybir.dt.from_np(a.dtype), kind="ExternalInput").ap()
    dram["out"] = nc.dram_tensor("out_x", (P, CT, N), F32, kind="ExternalOutput").ap()
    build(nc, dram)
    r = run_bass_kernel_spmd(nc, [arrays], core_ids=[0])
    return r.results[0]["out_x"].transpose(1, 0, 2).reshape(D, N).T.reshape(B, T, D)
```

```python
import math
from contextlib import ExitStack

import concourse.bass as bass
from concourse import mybir

F32 = mybir.dt.float32
F16 = mybir.dt.float16
U32 = mybir.dt.uint32
ALU = mybir.AluOpType
ACT = mybir.ActivationFunctionType
AX = mybir.AxisListType

P = 128
B = 2
T = 2048
N = B * T
D = 256
CT = D // P
BLK = 512
NBLK = N // BLK
X_PIECES = 4
LN_EPS = 1e-5
PRODUCTS = ((0, 0), (0, 1), (1, 0))
LOG_EXP_SET = "natural_log_exp_and_others"


class Scope:

    def __init__(self, nc, stage):
        self.nc, self.stage, self.stack, self.semaphores = nc, stage, ExitStack(), []

    def __enter__(self):
        return self

    def __exit__(self, *error):
        if self.semaphores:
            self.nc.clear_and_free_semaphores(self.semaphores)
            self.nc.all_engine_barrier()
        return self.stack.__exit__(*error)

    def sb(self, name, shape, dtype=F32):
        return self.stack.enter_context(self.nc.sbuf_tensor(f"{self.stage}_{name}", shape, dtype))

    def ps(self, name, shape, dtype=F32):
        return self.stack.enter_context(self.nc.psum_tensor(f"{self.stage}_{name}", shape, dtype))

    def sem(self, name):
        self.semaphores.append(self.nc.alloc_semaphore(f"{self.stage}_{name}"))
        return self.semaphores[-1]


def tokens(i, size=BLK):
    return bass.ds(i * size, size)


def over_tiles(ap, tiles):
    return ap.unsqueeze(1).broadcast_to([ap.shape[0], tiles, ap.shape[1]])


def load_constants(nc, c, dram):
    loaded = nc.alloc_semaphore("constants_loaded")
    c["x_loaded"] = [nc.alloc_semaphore(f"x_loaded{piece}") for piece in range(X_PIECES)]
    with nc.Block() as block:

        @block.sync
        def _(sp):
            for name in ("mean_matrix", "identity", "head_sum"):
                sp.dma_start(c[name][:], dram[name]).then_inc(loaded, 16)
            for piece in range(X_PIECES):
                at = tokens(piece, N // X_PIECES)
                sp.dma_start(c["x"][:, :, at], dram["x"][:, :, at]).then_inc(c["x_loaded"][piece], 16)
            sp.wait_ge(loaded, 16 * 3)

        @block.vector
        def _(dve):
            nc.vector.memset(c["ln_eps"][:], LN_EPS)


def layer_norm(nc, c, stage, xn, sums, parts=None, x_loaded=None):
    x, mean_matrix = c["x"], c["mean_matrix"]
    SLOTS = 4
    with Scope(nc, stage) as s:
        mean = s.ps("mean", [P, 2, BLK])
        var = s.ps("var", [P, 2, BLK])
        centred = s.sb("centred", [P, SLOTS, CT, BLK])
        squares = s.sb("squares", [P, SLOTS, CT, BLK])
        log_var = s.sb("log_var", [P, 2, BLK])
        rstd = s.sb("rstd", [P, 2, BLK])
        mean_ready, centred_ready, squares_ready = s.sem("mean_ready"), s.sem("centred_ready"), s.sem("squares_ready")
        var_ready, log_ready, rstd_ready, normed = s.sem("var_ready"), s.sem("log_ready"), s.sem("rstd_ready"), s.sem("normed")
        high_ready = s.sem("high_ready")

        with nc.Block() as block:

            @block.tensor
            def _(pe):
                for n in range(NBLK + 2):
                    if n < NBLK:
                        if n >= 2:
                            pe.wait_ge(centred_ready, n - 1)
                        if x_loaded is not None and n % (NBLK // X_PIECES) == 0:
                            pe.wait_ge(x_loaded[n // (NBLK // X_PIECES)], 16)
                        for tile in range(CT):
                            mm = nc.tensor.matmul(mean[:, n % 2], mean_matrix[:], x[:, tile, tokens(n)], start=tile == 0, stop=tile == CT - 1)
                        mm.then_inc(mean_ready, 1)
                    if n >= 2:
                        m = n - 2
                        pe.wait_ge(squares_ready, m + 1)
                        if m >= 2:
                            pe.wait_ge(log_ready, m - 1)
                        for tile in range(CT):
                            mm = nc.tensor.matmul(var[:, m % 2], mean_matrix[:], squares[:, m % SLOTS, tile], start=tile == 0, stop=tile == CT - 1)
                        mm.then_inc(var_ready, 1)

            @block.scalar
            def _(act):
                nc.scalar.preload_act_table_set(LOG_EXP_SET)
                for n in range(NBLK + 4):
                    if n < NBLK:
                        act.wait_ge(centred_ready, n + 1)
                        if n >= SLOTS:
                            act.wait_ge(var_ready, n - SLOTS + 1)
                        nc.scalar.activation(squares[:, n % SLOTS], centred[:, n % SLOTS], ACT.Square).then_inc(squares_ready, 1)
                    if 2 <= n < NBLK + 2:
                        m = n - 2
                        act.wait_ge(var_ready, m + 1)
                        nc.scalar.activation(log_var[:, m % 2], var[:, m % 2], ACT.Ln, bias=c["ln_eps"][:, 0:1]).then_inc(log_ready, 1)
                        act.wait_ge(log_ready, m + 1)
                        if m >= 2:
                            act.wait_ge(normed, (m - 1) * CT)
                        nc.scalar.activation(rstd[:, m % 2], log_var[:, m % 2], ACT.Exp, scale=-0.5).then_inc(rstd_ready, 1)
                    if n >= 4 and parts is not None:
                        m = n - 4
                        act.wait_ge(normed, (m + 1) * CT)
                        nc.scalar.activation(parts[:, 0, :, tokens(m)], xn[:, :, tokens(m)], ACT.Copy).then_inc(high_ready, 1)

            @block.vector
            def _(dve):
                for n in range(NBLK + 5 if parts is not None else NBLK + 3):
                    if n < NBLK:
                        dve.wait_ge(mean_ready, n + 1)
                        if n >= SLOTS:
                            dve.wait_ge(normed, (n - SLOTS + 1) * CT)
                        nc.vector.tensor_tensor(centred[:, n % SLOTS], x[:, :, tokens(n)], over_tiles(mean[:, n % 2], CT), ALU.subtract
                                                ).then_inc(centred_ready, 1)
                    if 3 <= n < NBLK + 3:
                        m = n - 3
                        dve.wait_ge(rstd_ready, m + 1)
                        for tile in range(CT):
                            if sums is None:
                                mult = nc.vector.tensor_tensor(xn[:, tile, tokens(m)], centred[:, m % SLOTS, tile], rstd[:, m % 2], ALU.mult)
                            else:
                                mult = nc.vector.scalar_tensor_tensor(xn[:, tile, tokens(m)], centred[:, m % SLOTS, tile], 1.0, rstd[:, m % 2],
                                                                      ALU.mult, ALU.mult, accum_out=sums[:, tile, m:m + 1])
                            mult.then_inc(normed, 1)
                    if n >= 5 and parts is not None:
                        m = n - 5
                        dve.wait_ge(high_ready, m + 1)
                        nc.vector.tensor_tensor(parts[:, 1, 0, tokens(m)], xn[:, 0, tokens(m)], parts[:, 0, 0, tokens(m)], ALU.subtract)

            @block.gpsimd
            def _(pool):
                if parts is not None:
                    for n in range(NBLK):
                        pool.wait_ge(high_ready, n + 1)
                        nc.gpsimd.tensor_tensor(parts[:, 1, 1:, tokens(n)], xn[:, 1:, tokens(n)], parts[:, 0, 1:, tokens(n)], ALU.subtract)


def gated_experts(nc, c, dram, stage, x_loaded=None):
    E = dram["gate_w"].shape[2]
    x = c["x"]
    with Scope(nc, stage) as s:
        xn = s.sb("xn", [P, CT, N])
        sums = s.sb("sums", [P, CT, NBLK])
        xn_parts = s.sb("xn_parts", [P, 2, CT, N], F16)
        layer_norm(nc, c, f"{stage}_ln", xn, sums, xn_parts, x_loaded)

        gate_w = s.sb("gate_w", [P, CT, E])
        gate_b = s.sb("gate_b", [P, E])
        expert = s.sb("expert", [P, 2, CT * D + CT])
        weights = s.sb("weights", [P, 2, 2, CT, D], F16)
        bias = expert[:, :, CT * D:]
        hidden = s.sb("hidden", [P, 4, BLK])
        pooled = s.sb("pooled", [P, CT, B])
        terms = s.sb("terms", [P, CT, B, E])
        logits = s.sb("logits", [P, B, E])
        top = s.sb("top", [P, B, 8])
        minus_max = s.sb("minus_max", [P, B])
        chosen = s.sb("chosen", [P, B, E])
        powers = s.sb("powers", [P, B, E])
        total = s.sb("total", [P, B])
        gate = s.sb("gate", [P, B, E])
        logit_sum = s.ps("logit_sum", [P, B * E])
        pre = s.ps("pre", [P, 4, BLK])

        tables_loaded = s.sem("tables_loaded")
        expert_loaded = [s.sem(f"expert_loaded{slot}") for slot in range(2)]
        terms_ready, logits_ready, gate_step, powers_ready = s.sem("terms_ready"), s.sem("logits_ready"), s.sem("gate_step"), s.sem("powers_ready")
        high_ready, rest_ready = s.sem("high_ready"), s.sem("rest_ready")
        pre_ready, hidden_ready, added = s.sem("pre_ready"), s.sem("hidden_ready"), s.sem("added")
        SLOTS = 4
        PER_EXPERT = NBLK * CT
        CREDIT = 2 * PER_EXPERT

        with nc.Block() as block:

            @block.sync
            def _(sp):
                for tile, table in ((gate_w, "gate_w"), (gate_b, "gate_b")):
                    sp.dma_start(tile[:], dram[table]).then_inc(tables_loaded, 16)
                with sp.Fori(0, E // 2) as pair:
                    for slot in range(2):
                        sp.wait_ge(pre_ready, (pair * 2 + slot + 1) * PER_EXPERT)
                        sp.wait_ge(hidden_ready, (pair * 2 + slot + 1) * PER_EXPERT)
                        sp.dma_start(expert[:, slot], dram["expert"][:, bass.ds(pair * 2 + slot, 1)].squeeze(1)
                                     ).then_inc(expert_loaded[slot], 16)

            @block.tensor
            def _(pe):
                pe.wait_ge(terms_ready, 1)
                for tile in range(CT):
                    mm = nc.tensor.matmul(logit_sum[:], c["mean_matrix"][:], terms[:, tile].rearrange("p b e -> p (b e)"),
                                          start=tile == 0, stop=tile == CT - 1)
                mm.then_inc(logits_ready, 1)
                pe.sem_inc(pre_ready, CREDIT)
                with pe.Fori(0, E // 2) as pair:
                    for u in range(2):
                        pe.wait_ge(rest_ready, pair * 2 + u + 1)
                        for n in range(NBLK):
                            for o in range(CT):
                                k = (u * NBLK + n) * CT + o
                                pe.wait_ge(hidden_ready, pair * 2 * PER_EXPERT + k + 1 + CREDIT - SLOTS)
                                for tile in range(CT):
                                    for w_part, x_part in PRODUCTS:
                                        mm = nc.tensor.matmul(pre[:, k % SLOTS], weights[:, u, w_part, tile, o * P:(o + 1) * P],
                                                              xn_parts[:, x_part, tile, tokens(n)], start=tile == 0 and (w_part, x_part) == PRODUCTS[0],
                                                              stop=tile == CT - 1 and (w_part, x_part) == PRODUCTS[-1])
                                mm.then_inc(pre_ready, 1)

            @block.scalar
            def _(act):
                for b in range(B):
                    act.wait_ge(gate_step, 5)
                    nc.scalar.activation(powers[:, b], logits[:, b], ACT.Exp,
                                         bias=minus_max[:, b:b + 1]).then_inc(powers_ready, 1)
                act.sem_inc(hidden_ready, CREDIT)

                def high_weights(pair, slot):
                    act.wait_ge(expert_loaded[slot], (pair + 1) * 16)
                    act.wait_ge(pre_ready, (pair * 2 + slot + 1) * PER_EXPERT)
                    nc.scalar.activation(weights[:, slot, 0].rearrange("p t d -> p (t d)"), expert[:, slot, 0:CT * D], ACT.Copy).then_inc(high_ready, 1)

                def gelus(pair, last):
                    for k in range(2 * PER_EXPERT):
                        if k % PER_EXPERT == SLOTS and not (last and k >= PER_EXPERT):
                            high_weights(pair + k // PER_EXPERT, 1 - k // PER_EXPERT)
                        act.wait_ge(pre_ready, pair * 2 * PER_EXPERT + k + 1 + CREDIT)
                        act.wait_ge(added, pair * 2 * PER_EXPERT + k + 1)
                        nc.scalar.activation(hidden[:, k % SLOTS], pre[:, k % SLOTS], ACT.Gelu,
                                             bias=bias[:, k // PER_EXPERT, k % CT:k % CT + 1]
                                             ).then_inc(hidden_ready, 1)

                high_weights(0, 0)
                with act.Fori(0, E // 2 - 1) as pair:
                    gelus(pair, False)
                gelus(E // 2 - 1, True)

            @block.gpsimd
            def _(pool):
                with pool.Fori(0, E // 2) as pair:
                    for slot in range(2):
                        pool.wait_ge(high_ready, pair * 2 + slot + 1)
                        nc.gpsimd.tensor_tensor(weights[:, slot, 1].rearrange("p t d -> p (t d)"), expert[:, slot, 0:CT * D],
                                                weights[:, slot, 0].rearrange("p t d -> p (t d)"), ALU.subtract).then_inc(rest_ready, 1)

            @block.vector
            def _(dve):
                dve.wait_ge(tables_loaded, 32)
                nc.vector.tensor_reduce(pooled[:], sums[:].rearrange("p c (b n) -> p c b n", b=B), AX.X, ALU.add).then_inc(gate_step, 1)
                dve.wait_ge(gate_step, 1)
                for tile in range(CT):
                    for b in range(B):
                        last = nc.vector.tensor_scalar(terms[:, tile, b], gate_w[:, tile], pooled[:, tile, b:b + 1], None, ALU.mult)
                last.then_inc(terms_ready, 1)
                dve.wait_ge(logits_ready, 1)
                nc.vector.scalar_tensor_tensor(logits[:], logit_sum[:].rearrange("p (b e) -> p b e", b=B), float(D) / T,
                                               over_tiles(gate_b[:], B), ALU.mult, ALU.add).then_inc(gate_step, 1)
                dve.wait_ge(gate_step, 2)
                for b in range(B):
                    nc.vector.max(top[:, b], logits[:, b]).then_inc(gate_step, 1)
                dve.wait_ge(gate_step, 4)
                nc.vector.tensor_scalar(minus_max[:], top[:, :, 0], -1.0, None, ALU.mult).then_inc(gate_step, 1)
                for b in range(B):
                    nc.vector.tensor_scalar(chosen[:, b], logits[:, b], top[:, b, 1:2], None, ALU.is_ge).then_inc(gate_step, 1)
                dve.wait_ge(gate_step, 7)
                dve.wait_ge(powers_ready, 2)
                nc.vector.tensor_tensor(chosen[:], chosen[:], powers[:], ALU.mult).then_inc(gate_step, 1)
                dve.wait_ge(gate_step, 8)
                nc.vector.tensor_reduce(total[:], chosen[:], AX.X, ALU.add).then_inc(gate_step, 1)
                dve.wait_ge(gate_step, 9)
                nc.vector.reciprocal(total[:], total[:]).then_inc(gate_step, 1)
                dve.wait_ge(gate_step, 10)
                for b in range(B):
                    nc.vector.tensor_scalar(gate[:, b], chosen[:, b], total[:, b:b + 1], 0.5, ALU.mult, ALU.mult).then_inc(gate_step, 1)
                dve.wait_ge(gate_step, 12)
                dve.sem_inc(added, SLOTS)
                with dve.Fori(0, E // 2) as pair:
                    for u in range(2):
                        for n in range(NBLK):
                            for o in range(CT):
                                k = (u * NBLK + n) * CT + o
                                b = n * BLK // T
                                dve.wait_ge(hidden_ready, pair * 2 * PER_EXPERT + k + 1 + CREDIT)
                                dve.wait_ge(added, pair * 2 * PER_EXPERT + k + 1)
                                nc.vector.scalar_tensor_tensor(x[:, o, tokens(n)], hidden[:, k % SLOTS],
                                                               gate[:, b, bass.ds(pair * 2 + u, 1)], x[:, o, tokens(n)],
                                                               ALU.mult, ALU.add).then_inc(added, 1)


def prototype_mixture(nc, c, dram, stage, result=None):
    NP = dram["proto_rows"].shape[0]
    RANK = dram["proto_B"].shape[2] // NP
    RT = NP * RANK // P
    TILES = N // P
    PER_BLK = BLK // P
    x = c["x"]
    with Scope(nc, stage) as s:
        xn = s.sb("xn", [P, CT, N])
        xn_parts = s.sb("xn_parts", [P, 2, CT, N], F16)
        layer_norm(nc, c, f"{stage}_ln", xn, None, xn_parts)

        proto = s.sb("proto", [P, CT, NP])
        proto_rows = s.sb("proto_rows", [NP, D])
        proto_sq = s.sb("proto_sq", [NP, D])
        p2 = s.sb("p2", [NP, 1])
        ones = s.sb("ones", [P, NP])
        temp = s.sb("temp", [P, 1])
        minus_inv_t = s.sb("minus_inv_t", [P, 1])
        down = s.sb("down", [P, CT, NP * RANK])
        up = s.sb("up", [P, RT, D])
        bias = s.sb("bias", [NP, D])
        spread = s.sb("spread", [NP, NP * RANK])
        numbers = s.sb("numbers", [P, NP])
        squares = s.sb("squares", [P, 2, CT, BLK])
        dist = s.sb("dist", [NP, N])
        scores = s.sb("scores", [P, TILES, NP])
        top = s.sb("top", [P, TILES, 8])
        which = s.sb("which", [P, TILES, 8], U32)
        whichf = s.sb("whichf", [P, TILES, 8])
        gap = s.sb("gap", [P, TILES])
        ratio = s.sb("ratio", [P, TILES])
        share = s.sb("share", [P, 2, TILES])
        picked = s.sb("picked", [P, 2, TILES, NP])
        down_parts = s.sb("down_parts", [P, 2, CT, NP * RANK], F16)
        up_parts = s.sb("up_parts", [P, 2, RT, D], F16)
        bias_parts = s.sb("bias_parts", [NP, 2, D], F16)
        spread_exact = s.sb("spread_exact", [NP, NP * RANK], F16)
        mix_parts = s.sb("mix_parts", [NP, 2, N], F16)
        wide = s.sb("wide", [P, 2, BLK])
        low = s.sb("low", [P, 2, BLK])
        low_parts = s.sb("low_parts", [P, 2, 4, BLK], F16)

        d2 = s.ps("d2", [P, 2, BLK])
        turned = s.ps("turned", [P, 2, BLK])
        low_sum = s.ps("low_sum", [P, 2, BLK])
        out = s.ps("out", [P, 2, BLK])
        mix_turned, wide_sum = d2, turned

        loaded, table_step = s.sem("loaded"), s.sem("table_step")
        squares_ready, d2_ready, clamped_ready, dist_ready = s.sem("squares_ready"), s.sem("d2_ready"), s.sem("clamped_ready"), s.sem("dist_ready")
        turned_ready, route_step, ratio_ready, picked_ready = s.sem("turned_ready"), s.sem("route_step"), s.sem("ratio_ready"), s.sem("picked_ready")
        mix_turned_ready, mix_ready = s.sem("mix_turned_ready"), s.sem("mix_ready")
        stored = s.sem("stored")
        sums_ready, wide_ready, low_ready, added = s.sem("sums_ready"), s.sem("wide_ready"), s.sem("low_ready"), s.sem("added")
        tables_high, tables_rest, mix_high_ready = s.sem("tables_high"), s.sem("tables_rest"), s.sem("mix_high_ready")
        low_high_ready, low_rest_ready, used = s.sem("low_high_ready"), s.sem("low_rest_ready"), s.sem("used")
        TABLES = ((down, down_parts), (up, up_parts), (bias, bias_parts))
        AHEAD = 2
        CREDIT = 4

        with nc.Block() as block:

            @block.sync
            def _(sp):
                for tile, table in ((proto, "proto"), (proto_rows, "proto_rows"), (temp, "temp"), (numbers, "numbers"), (down, "proto_B"),
                                    (up, "proto_A"), (bias, "proto_bias"), (spread, "proto_spread")):
                    sp.dma_start(tile[:], dram[table]).then_inc(loaded, 16)
                if result is not None:
                    for n in range(NBLK):
                        sp.wait_ge(added, (n + 2) * CT)
                        sp.dma_start(result[:, :, tokens(n)], x[:, :, tokens(n)]).then_inc(stored, 16)
                    sp.wait_ge(stored, NBLK * 16)

            def turn_distances(pe, n):
                pe.wait_ge(dist_ready, n + 1)
                for k in range(PER_BLK):
                    tile = n * PER_BLK + k
                    half, at = divmod(tile * NP, BLK)
                    mm = nc.tensor.transpose(turned[:, half, at:at + NP], dist[:, tile * P:(tile + 1) * P], c["identity"][0:NP, 0:NP])
                mm.then_inc(turned_ready, 1)

            @block.tensor
            def _(pe):
                pe.wait_ge(table_step, 4)
                for n in range(NBLK):
                    if n >= 2:
                        pe.wait_ge(clamped_ready, n - 1)
                    for tile in range(CT):
                        nc.tensor.matmul(d2[0:NP, n % 2], proto[:, tile], xn[:, tile, tokens(n)], start=tile == 0, stop=False)
                    pe.wait_ge(squares_ready, n + 1)
                    for tile in range(CT):
                        mm = nc.tensor.matmul(d2[0:NP, n % 2], ones[:], squares[:, n % 2, tile], start=False, stop=tile == CT - 1)
                    mm.then_inc(d2_ready, 1)
                    if n >= 1:
                        turn_distances(pe, n - 1)
                turn_distances(pe, NBLK - 1)
                pe.wait_ge(clamped_ready, NBLK)
                for n in range(NBLK):
                    pe.wait_ge(picked_ready, 1)
                    if n >= 2:
                        pe.wait_ge(mix_ready, n - 1)
                    for k in range(PER_BLK):
                        mm = nc.tensor.transpose(mix_turned[0:NP, n % 2, k * P:(k + 1) * P], picked[:, 0, n * PER_BLK + k], c["identity"][:])
                    mm.then_inc(mix_turned_ready, 1)
                pe.wait_ge(mix_ready, NBLK)
                pe.wait_ge(tables_rest, len(TABLES))
                pe.wait_ge(tables_high, len(TABLES) + 1)

                def sums(pair, k):
                    u, m = divmod(k, RT)
                    count = pair * 2 * RT + k
                    pe.wait_ge(wide_ready, count + 1)
                    pe.wait_ge(low_ready, count + 1)
                    for tile in range(CT):
                        for w_part, x_part in PRODUCTS:
                            nc.tensor.matmul(low_sum[:, m % 2], down_parts[:, w_part, tile, m * P:(m + 1) * P], xn_parts[:, x_part, tile, tokens(pair * 2 + u)],
                                             start=tile == 0 and (w_part, x_part) == PRODUCTS[0], stop=tile == CT - 1 and (w_part, x_part) == PRODUCTS[-1])
                    for part in range(2):
                        mm = nc.tensor.matmul(wide_sum[:, m % 2], spread_exact[:, m * P:(m + 1) * P], mix_parts[:, part, tokens(pair * 2 + u)],
                                              start=part == 0, stop=part == 1)
                    mm.then_inc(sums_ready, 1)

                def raise_ranks(pair, k):
                    u, m = divmod(k, RT)
                    if m == 0:
                        pe.wait_ge(added, (pair * 2 + u + 1) * CT)
                    pe.wait_ge(low_rest_ready, pair * 2 * RT + k + 1 + AHEAD)
                    for o in range(CT):
                        for w_part, x_part in PRODUCTS:
                            mm = nc.tensor.matmul(out[:, o], up_parts[:, w_part, m, o * P:(o + 1) * P], low_parts[:, x_part, m % 4],
                                                  start=m == 0 and (w_part, x_part) == PRODUCTS[0], stop=False)
                    if m == RT - 1:
                        for o in range(CT):
                            for w_part, x_part in PRODUCTS:
                                mm = nc.tensor.matmul(out[:, o], bias_parts[:, w_part, o * P:(o + 1) * P], mix_parts[:, x_part, tokens(pair * 2 + u)],
                                                      start=False, stop=(w_part, x_part) == PRODUCTS[-1])
                    mm.then_inc(used, 1)

                for k in range(AHEAD):
                    sums(0, k)
                with pe.Fori(0, NBLK // 2 - 1) as pair:
                    for k in range(2 * RT):
                        sums(pair, k + AHEAD)
                        raise_ranks(pair, k)
                for k in range(2 * RT):
                    if k + AHEAD < 2 * RT:
                        sums(NBLK // 2 - 1, k + AHEAD)
                    raise_ranks(NBLK // 2 - 1, k)

            @block.gpsimd
            def _(pool):
                for i, (table, parts) in enumerate(TABLES):
                    pool.wait_ge(tables_high, i + 1)
                    nc.gpsimd.tensor_tensor(parts[:, 1], table[:], parts[:, 0], ALU.subtract).then_inc(tables_rest, 1)
                with pool.Fori(0, NBLK // 2) as pair:
                    for k in range(2 * RT):
                        pool.wait_ge(low_high_ready, pair * 2 * RT + k + 1)
                        nc.gpsimd.tensor_tensor(low_parts[:, 1, k % 4], low[:, k % 2], low_parts[:, 0, k % 4], ALU.subtract).then_inc(low_rest_ready, 1)

            @block.scalar
            def _(act):
                for n in range(NBLK + 1):
                    if n < NBLK:
                        if n >= 2:
                            act.wait_ge(d2_ready, n - 1)
                        nc.scalar.activation(squares[:, n % 2], xn[:, :, tokens(n)], ACT.Square).then_inc(squares_ready, 1)
                    if n >= 1:
                        act.wait_ge(clamped_ready, n)
                        nc.scalar.activation(dist[:, tokens(n - 1)], dist[:, tokens(n - 1)], ACT.Sqrt).then_inc(dist_ready, 1)
                act.wait_ge(loaded, 16 * 8)
                for table, parts in TABLES:
                    nc.scalar.activation(parts[:, 0], table[:], ACT.Copy).then_inc(tables_high, 1)
                nc.scalar.activation(spread_exact[:], spread[:], ACT.Copy).then_inc(tables_high, 1)
                act.wait_ge(route_step, 2 + 2 * TILES)
                nc.scalar.activation(ratio[:], gap[:], ACT.Exp).then_inc(ratio_ready, 1)
                for n in range(NBLK):
                    act.wait_ge(mix_turned_ready, n + 1)
                    nc.scalar.activation(mix_parts[:, 0, tokens(n)], mix_turned[0:NP, n % 2], ACT.Copy).then_inc(mix_high_ready, 1)
                act.sem_inc(wide_ready, AHEAD)
                with act.Fori(0, NBLK // 2) as pair:
                    for k in range(2 * RT):
                        count = pair * 2 * RT + k
                        act.wait_ge(sums_ready, count + 1)
                        act.wait_ge(low_ready, count + 1)
                        nc.scalar.activation(wide[:, k % 2], wide_sum[:, k % 2], ACT.Copy).then_inc(wide_ready, 1)
                        act.wait_ge(low_ready, count + 1 + AHEAD)
                        act.wait_ge(used, count + 1)
                        nc.scalar.activation(low_parts[:, 0, k % 4], low[:, k % 2], ACT.Copy).then_inc(low_high_ready, 1)

            @block.vector
            def _(dve):
                nc.vector.memset(ones[:], 1.0).then_inc(table_step, 1)
                dve.wait_ge(loaded, 16 * 8)
                for tile in range(CT):
                    nc.vector.tensor_scalar(proto[:, tile], proto[:, tile], -2.0, None, ALU.mult).then_inc(table_step, 1)
                nc.vector.scalar_tensor_tensor(proto_sq[:], proto_rows[:], 1.0, proto_rows[:], ALU.mult, ALU.mult,
                                               accum_out=p2[:, 0:1]).then_inc(table_step, 1)
                nc.vector.scalar_tensor_tensor(minus_inv_t[:], temp[:], -1.0, temp[:], ALU.mult, ALU.max).then_inc(table_step, 1)
                dve.wait_ge(table_step, 5)
                nc.vector.tensor_scalar(temp[:], minus_inv_t[:], 0.1, -1.0, ALU.max, ALU.mult).then_inc(table_step, 1)
                dve.wait_ge(table_step, 6)
                nc.vector.reciprocal(minus_inv_t[:], temp[:]).then_inc(table_step, 1)
                dve.wait_ge(table_step, 7)
                for n in range(NBLK):
                    dve.wait_ge(d2_ready, n + 1)
                    nc.vector.tensor_scalar(dist[:, tokens(n)], d2[0:NP, n % 2], p2[:, 0:1], 0.0, ALU.add, ALU.max).then_inc(clamped_ready, 1)
                dve.wait_ge(turned_ready, NBLK)
                nc.vector.tensor_scalar(scores[:].rearrange("p t n -> p (t n)"), turned[:].rearrange("p a b -> p (a b)"),
                                        minus_inv_t[:, 0:1], None, ALU.mult).then_inc(route_step, 1)
                dve.wait_ge(route_step, 1)
                for tile in range(TILES):
                    nc.vector.max(top[:, tile], scores[:, tile]).then_inc(route_step, 1)
                for tile in range(TILES):
                    dve.wait_ge(route_step, 2 + tile)
                    nc.vector.max_index(which[:, tile], top[:, tile], scores[:, tile]).then_inc(route_step, 1)
                nc.vector.tensor_tensor(gap[:], top[:, :, 1], top[:, :, 0], ALU.subtract).then_inc(route_step, 1)
                done = 2 + 2 * TILES
                dve.wait_ge(route_step, done)
                nc.vector.tensor_copy(whichf[:], which[:]).then_inc(route_step, 1)
                dve.wait_ge(ratio_ready, 1)
                nc.vector.tensor_scalar(share[:, 1], ratio[:], 1.0, None, ALU.add).then_inc(route_step, 1)
                dve.wait_ge(route_step, done + 2)
                nc.vector.reciprocal(share[:, 0], share[:, 1]).then_inc(route_step, 1)
                dve.wait_ge(route_step, done + 3)
                nc.vector.tensor_scalar(share[:, 0], share[:, 0], 0.5, None, ALU.mult).then_inc(route_step, 1)
                dve.wait_ge(route_step, done + 4)
                nc.vector.tensor_tensor(share[:, 1], share[:, 0], ratio[:], ALU.mult).then_inc(route_step, 1)
                for rank in range(2):
                    nc.vector.tensor_tensor(picked[:, rank], numbers[:].unsqueeze(1).broadcast_to([P, TILES, NP]),
                                            whichf[:, :, rank:rank + 1].broadcast_to([P, TILES, NP]), ALU.is_equal).then_inc(route_step, 1)
                dve.wait_ge(route_step, done + 7)
                for rank in range(2):
                    nc.vector.tensor_tensor(picked[:, rank], picked[:, rank],
                                            share[:, rank].unsqueeze(2).broadcast_to([P, TILES, NP]), ALU.mult).then_inc(route_step, 1)
                dve.wait_ge(route_step, done + 9)
                nc.vector.tensor_tensor(picked[:, 0], picked[:, 0], picked[:, 1], ALU.add).then_inc(picked_ready, 1)
                for n in range(NBLK):
                    dve.wait_ge(mix_high_ready, n + 1)
                    nc.vector.tensor_tensor(mix_parts[:, 1, tokens(n)], mix_turned[0:NP, n % 2], mix_parts[:, 0, tokens(n)], ALU.subtract
                                            ).then_inc(mix_ready, 1)
                dve.sem_inc(low_ready, AHEAD)
                dve.sem_inc(used, CREDIT)
                dve.sem_inc(added, CT)
                dve.sem_inc(low_rest_ready, AHEAD)
                with dve.Fori(0, NBLK // 2) as pair:
                    for k in range(2 * RT + 1):
                        count = pair * 2 * RT + k
                        if k < 2 * RT:
                            dve.wait_ge(wide_ready, count + 1 + AHEAD)
                            dve.wait_ge(low_rest_ready, count + 1)
                            nc.vector.tensor_tensor(low[:, k % 2], low_sum[:, k % 2], wide[:, k % 2], ALU.mult).then_inc(low_ready, 1)
                        if k > 0 and k % RT == 0:
                            n = pair * 2 + k // RT - 1
                            dve.wait_ge(used, (n + 1) * RT + CREDIT)
                            for o in range(CT):
                                nc.vector.tensor_tensor(x[:, o, tokens(n)], x[:, o, tokens(n)], out[:, o], ALU.add).then_inc(added, 1)
HEADS = 16
HD = D // HEADS
HX = 64
PAIRS = HX // 2
BH = B * HEADS
QG = P // PAIRS
QT = T // P
LOGIT_SCALE = 1.0 / 64
DOT_SCALE = 8.0
MAX_ROW = HX + 3 * HD
V_SCALE = 16.0
PROB_SCALE = 256.0
ONES = 2 * HD
V_COLS = ONES + 1


def project_qkv(nc, c, dram, stage, xn, qk, v):
    with Scope(nc, stage) as s:
        w_qk = s.sb("w_qk", [P, 2, CT, D])
        w_v = s.sb("w_v", [P, CT, D])
        b_qk = s.sb("b_qk", [P, 2, CT])
        b_v = s.sb("b_v", [P, D])
        v_sum = s.sb("v_sum", [P, 2, D])
        high = s.sb("high", [P, 2, T], F16)
        rest = s.sb("rest", [P, 2, T], F16)
        acc = s.ps("acc", [P, 4, BLK])
        loaded, acc_ready, qk_ready, v_ready = s.sem("loaded"), s.sem("acc_ready"), s.sem("qk_ready"), s.sem("v_ready")
        high_ready, rest_ready, v_step = s.sem("high_ready"), s.sem("rest_ready"), s.sem("v_step")
        stored = [s.sem(f"stored{slot}") for slot in range(2)]
        steps = [(w, tile, n) for w in range(2) for tile in range(CT) for n in range(NBLK)]
        HALF = NBLK // B

        with nc.Block() as block:

            @block.sync
            def _(sp):
                for tile, table in ((w_qk, "att_w_qk"), (w_v, "att_w_v"), (b_qk, "att_b_qk"), (b_v, "att_b_v")):
                    sp.dma_start(tile[:], dram[table]).then_inc(loaded, 16)
                for r in range(len(steps) // HALF):
                    w, tile, n = steps[r * HALF]
                    rows = w * BH * HD + (n // HALF) * D + tile * P
                    sp.wait_ge(rest_ready, (r + 1) * HALF)
                    sp.dma_start(dram["att_dot"][0, rows:rows + P], high[:, r % 2]).then_inc(stored[r % 2], 16)
                    sp.dma_start(dram["att_dot"][1, rows:rows + P], rest[:, r % 2]).then_inc(stored[r % 2], 16)
                for slot in range(2):
                    sp.wait_ge(stored[slot], len(steps) // HALF * 16)

            @block.tensor
            def _(pe):
                pe.wait_ge(loaded, 64)
                for k, (w, tile, n) in enumerate(steps):
                    if k >= 4:
                        pe.wait_ge(qk_ready, k - 3)
                    for t in range(CT):
                        mm = nc.tensor.matmul(acc[:, k % 4], w_qk[:, w, t, tile * P:(tile + 1) * P], xn[:, t, tokens(n)],
                                              start=t == 0, stop=t == CT - 1)
                    mm.then_inc(acc_ready, 1)
                for i in range(N // P):
                    k = len(steps) + i
                    if i < 4:
                        pe.wait_ge(qk_ready, k - 3)
                    else:
                        pe.wait_ge(v_ready, i - 3)
                    for t in range(CT):
                        mm = nc.tensor.matmul(acc[:, k % 4, 0:D], xn[:, t, i * P:(i + 1) * P], w_v[:, t], start=t == 0, stop=t == CT - 1)
                    mm.then_inc(acc_ready, 1)

            @block.scalar
            def _(act):
                for k, (w, tile, n) in enumerate(steps):
                    act.wait_ge(acc_ready, k + 1)
                    nc.scalar.activation(qk[:, tile, w, tokens(n)], acc[:, k % 4], ACT.Identity,
                                         bias=b_qk[:, w, tile:tile + 1]).then_inc(qk_ready, 1)

            @block.vector
            def _(dve):
                for k, (w, tile, n) in enumerate(steps):
                    r, at = divmod(k, HALF)
                    scale = 1.0 if w else DOT_SCALE
                    dve.wait_ge(qk_ready, k + 1)
                    if r >= 2:
                        dve.wait_ge(stored[r % 2], r // 2 * 32)
                    nc.vector.tensor_scalar(high[:, r % 2, tokens(at)], qk[:, tile, w, tokens(n)], scale, None, ALU.mult).then_inc(high_ready, 1)
                    dve.wait_ge(high_ready, k + 1)
                    nc.vector.scalar_tensor_tensor(rest[:, r % 2, tokens(at)], qk[:, tile, w, tokens(n)], scale,
                                                   high[:, r % 2, tokens(at)], ALU.mult, ALU.subtract).then_inc(rest_ready, 1)
                for i in range(N // P):
                    k = len(steps) + i
                    dve.wait_ge(acc_ready, k + 1)
                    nc.vector.tensor_tensor(v_sum[:, i % 2], acc[:, k % 4, 0:D], b_v[:], ALU.add).then_inc(v_ready, 1)
                    by_head = v_sum[:, i % 2].rearrange("p (h d) -> p h d", h=HEADS)
                    columns = v[:, i // QT * HEADS:(i // QT + 1) * HEADS, i % QT]
                    dve.wait_ge(v_ready, i + 1)
                    nc.vector.tensor_scalar(columns[:, :, 0:HD], by_head, V_SCALE, None, ALU.mult).then_inc(v_step, 1)
                    dve.wait_ge(v_step, 2 * i + 1)
                    nc.vector.scalar_tensor_tensor(columns[:, :, HD:ONES], by_head, V_SCALE, columns[:, :, 0:HD],
                                                   ALU.mult, ALU.subtract).then_inc(v_step, 1)
                nc.vector.memset(v[:, :, :, ONES], V_SCALE)


def helical_features(nc, c, dram, stage, qk):
    with Scope(nc, stage) as s:
        w_hel = s.sb("w", [P, CT, 2, 2, P])
        bias = s.sb("bias", [P, CT, 2, 2])
        raw = s.sb("raw", [P, 2, 2, BLK])
        squares = s.sb("squares", [P, 2, 2, BLK])
        norm_sq = s.sb("norm_sq", [P, 2, BLK])
        log_sq = s.sb("log_sq", [P, 2, BLK])
        inv = s.sb("inv", [P, 2, BLK])
        unit = s.sb("unit", [P, 2, 2, BLK])
        high = s.sb("high", [P, B, 2, 2, T // 2], F16)
        rest = s.sb("rest", [P, B, 2, 2, T // 2], F16)
        acc = s.ps("acc", [P, 2, 2, BLK])
        loaded, acc_ready, raw_ready, squares_ready = s.sem("loaded"), s.sem("acc_ready"), s.sem("raw_ready"), s.sem("squares_ready")
        norm_ready, log_ready, inv_ready, unit_ready = s.sem("norm_ready"), s.sem("log_ready"), s.sem("inv_ready"), s.sem("unit_ready")
        high_ready, rest_ready = s.sem("high_ready"), s.sem("rest_ready")
        stored = [s.sem(f"stored{b}") for b in range(B)]
        CREDIT = 2
        STEPS = T // BLK
        ROUNDS = 2 * CT * 2

        def number(group, w, b, n):
            return ((w + group * 2) * B + b) * STEPS + n

        with nc.Block() as block:

            @block.sync
            def _(sp):
                sp.dma_start(w_hel[:], dram["att_hel_w"]).then_inc(loaded, 16)
                sp.dma_start(bias[:], dram["att_hel_b"]).then_inc(loaded, 16)
                for group in range(2 * CT):
                    with sp.Fori(0, 2) as w:
                        for b in range(B):
                            sp.wait_ge(rest_ready, number(group, w, b, STEPS) + CREDIT)
                            rows = bass.ds((w * B + b) * (HEADS * PAIRS) + group * P, P)
                            for parity in range(2):
                                for part, tile in ((0, high), (1, rest)):
                                    sp.dma_start(dram["att_hel"][part, parity, rows].rearrange("r (i u) -> r i u", i=2),
                                                 tile[:, b, :, parity]).then_inc(stored[b], 16)
                for b in range(B):
                    sp.wait_ge(stored[b], ROUNDS * 64 + 1)

            @block.tensor
            def _(pe):
                pe.wait_ge(loaded, 32)
                for group in range(2 * CT):
                    tile, half = divmod(group, 2)
                    with pe.Fori(0, 2) as w:
                        for b in range(B):
                            for n in range(STEPS):
                                k = number(group, w, b, n)
                                pe.wait_ge(raw_ready, k * 2 + 2)
                                pe.wait_ge(squares_ready, k * 2 + 2)
                                for comp in range(2):
                                    mm = nc.tensor.matmul(acc[:, n % 2, comp], w_hel[:, tile, half, comp],
                                                          qk[:, tile].rearrange("p w n -> p (w n)")[:, bass.ds(w * N + b * T + n * BLK, BLK)],
                                                          start=True, stop=True)
                                mm.then_inc(acc_ready, 1)

            @block.scalar
            def _(act):
                nc.scalar.preload_act_table_set(LOG_EXP_SET)
                act.sem_inc(raw_ready, 2 * CREDIT)
                act.sem_inc(squares_ready, 2 * CREDIT)
                act.sem_inc(log_ready, CREDIT)

                def squares_and_raw(group, w, b, n):
                    tile, half = divmod(group, 2)
                    k = number(group, w, b, n)
                    act.wait_ge(acc_ready, k + 1)
                    act.wait_ge(norm_ready, k + 1)
                    for comp in range(2):
                        nc.scalar.activation(squares[:, n % 2, comp], acc[:, n % 2, comp], ACT.Square,
                                             bias=bias[:, tile, half, comp:comp + 1]).then_inc(squares_ready, 1)
                    act.wait_ge(unit_ready, k + 1)
                    for comp in range(2):
                        nc.scalar.activation(raw[:, n % 2, comp], acc[:, n % 2, comp], ACT.Identity,
                                             bias=bias[:, tile, half, comp:comp + 1]).then_inc(raw_ready, 1)

                def inverse_length(group, w, b, n):
                    k = number(group, w, b, n)
                    act.wait_ge(norm_ready, k + 1 + CREDIT)
                    nc.scalar.activation(log_sq[:, n % 2], norm_sq[:, n % 2], ACT.Ln).then_inc(log_ready, 1)
                    act.wait_ge(log_ready, k + 1 + CREDIT)
                    act.wait_ge(unit_ready, k + 1)
                    nc.scalar.activation(inv[:, n % 2], log_sq[:, n % 2], ACT.Exp, scale=-0.5).then_inc(inv_ready, 1)

                for group in range(2 * CT):
                    with act.Fori(0, 2) as w:
                        steps = [(b, n) for b in range(B) for n in range(STEPS)]
                        for at in range(len(steps) + 1):
                            if at < len(steps):
                                squares_and_raw(group, w, *steps[at])
                            if at >= 1:
                                inverse_length(group, w, *steps[at - 1])

            @block.vector
            def _(dve):
                dve.sem_inc(norm_ready, CREDIT)
                dve.sem_inc(unit_ready, CREDIT)
                for b in range(B):
                    dve.sem_inc(stored[b], 1)

                def square_sum(group, w, b, n):
                    k = number(group, w, b, n)
                    dve.wait_ge(squares_ready, k * 2 + 2 + 2 * CREDIT)
                    dve.wait_ge(log_ready, k + 1)
                    nc.vector.tensor_tensor(norm_sq[:, n % 2], squares[:, n % 2, 0], squares[:, n % 2, 1], ALU.add).then_inc(norm_ready, 1)

                def unit_length(group, w, b, n):
                    k = number(group, w, b, n)
                    half_blk = slice(n * BLK // 2, (n + 1) * BLK // 2)
                    dve.wait_ge(inv_ready, k + 1)
                    dve.wait_ge(rest_ready, k + 1)
                    nc.vector.scalar_tensor_tensor(unit[:, n % 2], over_tiles(inv[:, n % 2], 2), 1e12, raw[:, n % 2],
                                                   ALU.min, ALU.mult).then_inc(unit_ready, 1)
                    dve.wait_ge(unit_ready, k + 1 + CREDIT)
                    if n == 0:
                        dve.wait_ge(stored[b], (w + group * 2) * 64 + 1)
                    nc.vector.tensor_copy(high[:, b, :, :, half_blk], unit[:, n % 2].rearrange("p i (u c) -> p i c u", c=2)).then_inc(high_ready, 1)

                for group in range(2 * CT):
                    with dve.Fori(0, 2) as w:
                        steps = [(b, n) for b in range(B) for n in range(STEPS)]
                        for at in range(len(steps) + 1):
                            if at < len(steps):
                                square_sum(group, w, *steps[at])
                            if at >= 1:
                                unit_length(group, w, *steps[at - 1])

            @block.gpsimd
            def _(pool):
                pool.sem_inc(rest_ready, CREDIT)
                for group in range(2 * CT):
                    with pool.Fori(0, 2) as w:
                        for b in range(B):
                            for n in range(STEPS):
                                half_blk = slice(n * BLK // 2, (n + 1) * BLK // 2)
                                pool.wait_ge(high_ready, number(group, w, b, n) + 1)
                                nc.gpsimd.tensor_tensor(rest[:, b, :, :, half_blk], unit[:, n % 2].rearrange("p i (u c) -> p i c u", c=2),
                                                        high[:, b, :, :, half_blk], ALU.subtract).then_inc(rest_ready, 1)


def head_attention(nc, c, dram, stage, v):
    with Scope(nc, stage) as s:
        q = s.sb("q", [P, 2, 2, T], F16)
        k = s.sb("k", [P, 2, 2, T], F16)
        probs = s.sb("probs", [P, 2, T // 2])
        high = s.sb("high", [P, 4, T // 2], F16)
        rest = s.sb("rest", [P, 4, T // 2], F16)
        log_scale = s.sb("log_scale", [P, 1])
        v_head = s.sb("v_head", [P, 2, QT, V_COLS], F16)
        maxima = s.sb("maxima", [P, QT * 4])
        tile_max = s.sb("tile_max", [P, QT])
        shift = s.sb("shift", [P, QT])
        shift_row = s.sb("shift_row", [QT, P], F16)
        out_copy = s.sb("out_copy", [V_COLS, 2, T // 2])
        scores = s.ps("scores", [P, 2, T // 2])
        peek = s.ps("peek", [P, 2, BLK])
        out = s.ps("out", [P, T // 2])

        ones_ready = s.sem("ones_ready")
        loaded = [s.sem(f"loaded{slot}") for slot in range(2)]
        shift_stored = [s.sem(f"shift_stored{slot}") for slot in range(2)]
        out_stored = [s.sem(f"out_stored{half}") for half in range(2)]
        v_ready, peek_ready, peek_read = s.sem("v_ready"), s.sem("peek_ready"), s.sem("peek_read")
        max_step, shift_ready, shift_turned, shift_row_ready = s.sem("max_step"), s.sem("shift_ready"), s.sem("shift_turned"), s.sem("shift_row_ready")
        scores_ready, probs_ready, high_ready = s.sem("scores_ready"), s.sem("probs_ready"), s.sem("high_ready")
        rest_a_ready, rest_b_ready, weighed, out_copied = s.sem("rest_a_ready"), s.sem("rest_b_ready"), s.sem("weighed"), s.sem("out_copied")
        STEPS = 2 * QT
        AHEAD = 3
        BEFORE_COPY = 2
        PEEKS = QT * 4
        FIRST_PEEK = 2
        TURN_AT = FIRST_PEEK + (PEEKS + 2) // 3
        LOADS = 18 * 16
        SPLIT = 384
        W_CREDIT, H_CREDIT, R_CREDIT, K_CREDIT = 2 * STEPS, 2, 2, 2

        def peeks_at(step):
            first = 3 * (step - FIRST_PEEK)
            return range(first, min(first + 3, PEEKS)) if step >= FIRST_PEEK else range(0)

        with nc.Block() as block:

            @block.sync
            def _(sp):
                hel, dot = dram["att_hel"], dram["att_dot"]

                def load(pair, slot):
                    head = pair * 2 + slot
                    at_q, at_k = bass.ds(head * PAIRS, PAIRS), bass.ds(head * PAIRS + BH * PAIRS, PAIRS)
                    for parity in range(2):
                        rows = slice(parity * PAIRS, (parity + 1) * PAIRS)
                        more_rows = slice(HX + parity * PAIRS, HX + (parity + 1) * PAIRS)
                        for tile, rows_of, number, source in (
                                (q, rows, 0, hel[0, parity, at_q]), (k, rows, 0, hel[0, parity, at_k]),
                                (q, rows, 1, hel[0, parity, at_q]), (k, rows, 1, hel[1, parity, at_k]),
                                (q, more_rows, 1, hel[1, parity, at_q]), (k, more_rows, 1, hel[0, parity, at_k])):
                            sp.dma_start(tile[rows_of, slot, number], source).then_inc(loaded[slot], 16)
                    for part, (q_part, k_part) in enumerate(((0, 0), (0, 1), (1, 0))):
                        rows = slice(HX + part * HD, HX + (part + 1) * HD)
                        sp.dma_start(q[rows, slot, 0], dot[q_part, bass.ds(head * HD, HD)]).then_inc(loaded[slot], 16)
                        sp.dma_start(k[rows, slot, 0], dot[k_part, bass.ds(head * HD + BH * HD, HD)]).then_inc(loaded[slot], 16)

                def store_shift(pair, slot):
                    sp.wait_ge(shift_row_ready, pair * 2 + slot + 1)
                    sp.dma_start(q[MAX_ROW:MAX_ROW + 1, slot, 0].rearrange("a (t n) -> a t n", t=QT), shift_row[:]
                                 ).then_inc(shift_stored[slot], 16)

                def store_out(pair, slot, half):
                    head = pair * 2 + slot
                    queries = slice(half * T // 2, (half + 1) * T // 2)
                    sp.wait_ge(out_copied, head * 2 + half + 1 + 1)
                    for part in range(2):
                        sp.dma_start(dram["att_o"][part, bass.ds(head * HD, HD), queries], out_copy[part * HD:(part + 1) * HD, half]
                                     ).then_inc(out_stored[half], 16)
                    sp.dma_start(dram["att_sum"][bass.ds(head, 1), queries], out_copy[ONES:V_COLS, half]).then_inc(out_stored[half], 16)

                def follow(pair, slot, more_shift, more_load):
                    store_out(pair, slot, 0)
                    if more_shift:
                        store_shift(pair + slot, 1 - slot)
                    if more_load:
                        sp.wait_ge(scores_ready, (pair * 2 + slot + 1) * STEPS)
                        load(pair + 1, slot)
                    store_out(pair, slot, 1)

                sp.wait_ge(ones_ready, 2)
                load(0, 0)
                load(0, 1)
                store_shift(0, 0)
                with sp.Fori(0, BH // 2 - 1) as pair:
                    for slot in range(2):
                        follow(pair, slot, True, True)
                follow(BH // 2 - 1, 0, True, False)
                follow(BH // 2 - 1, 1, False, False)
                for half in range(2):
                    sp.wait_ge(out_stored[half], BH * 48 + 1)

            @block.gpsimd
            def _(pool):
                pool.sem_inc(rest_b_ready, R_CREDIT)
                with pool.Fori(0, BH // 2) as pair:
                    for slot in range(2):
                        head = pair * 2 + slot
                        pool.wait_ge(weighed, (head + 1) * STEPS)
                        nc.gpsimd.tensor_copy(v_head[:, slot], v[:, bass.ds(head, 1)].squeeze(1)).then_inc(v_ready, 1)
                        for step in range(STEPS):
                            pool.wait_ge(high_ready, head * STEPS + step + 1 + H_CREDIT)
                            nc.gpsimd.tensor_tensor(rest[:, step % 4, SPLIT:], probs[:, step % 2, SPLIT:], high[:, step % 4, SPLIT:],
                                                    ALU.subtract).then_inc(rest_b_ready, 1)

            @block.tensor
            def _(pe):
                def peek_scores(pair, slot, numbers):
                    head = pair * 2 + slot
                    for m in numbers:
                        tile, blk = divmod(m, 4)
                        if m == 0:
                            pe.wait_ge(loaded[slot], (pair + 1) * LOADS)
                        pe.wait_ge(peek_read, head * PEEKS + m + 1)
                        nc.tensor.matmul(peek[:, m % 2], q[0:MAX_ROW, slot, 0, tile * P:(tile + 1) * P], k[0:MAX_ROW, slot, 0, tokens(blk)],
                                         start=True, stop=True).then_inc(peek_ready, 1)

                def turn_shifts(pair, slot):
                    pe.wait_ge(shift_ready, pair * 2 + slot + 1)
                    nc.tensor.transpose(peek[0:QT, 0, 0:P], shift[:], c["identity"][:]).then_inc(shift_turned, 1)

                def score(pair, slot, step):
                    half, tile = divmod(step, QT)
                    head = pair * 2 + slot
                    if step == 0:
                        pe.wait_ge(shift_stored[slot], (pair + 1) * 16)
                    pe.wait_ge(high_ready, head * STEPS + step + 1)
                    for number, rows in ((1, P), (0, MAX_ROW + 1)):
                        for j in range(2):
                            mm = nc.tensor.matmul(scores[:, step % 2, tokens(j)], k[0:rows, slot, number, tile * P:(tile + 1) * P],
                                                  q[0:rows, slot, number, tokens(half * 2 + j)], start=number == 1, stop=number == 0)
                    mm.then_inc(scores_ready, 1)

                def weigh(pair, slot, step):
                    half, tile = divmod(step, QT)
                    head = pair * 2 + slot
                    if step == 0:
                        pe.wait_ge(v_ready, head + 1)
                    if tile == 0:
                        pe.wait_ge(out_copied, head * 2 + half + 1)
                    pe.wait_ge(rest_a_ready, head * STEPS + step + 1 + R_CREDIT)
                    pe.wait_ge(rest_b_ready, head * STEPS + step + 1 + R_CREDIT)
                    for part in (high, rest):
                        for j in range(2):
                            mm = nc.tensor.matmul(out[0:V_COLS, tokens(j)], v_head[:, slot, tile], part[:, step % 4, tokens(j)],
                                                  start=tile == 0 and part is high, stop=tile == QT - 1 and part is rest)
                    mm.then_inc(weighed, 1)

                def attend(pair, slot, more):
                    ahead = (pair + slot, 1 - slot)
                    for step in range(STEPS):
                        peeks = peeks_at(step) if more else range(0)
                        peek_scores(*ahead, peeks[0:1])
                        if step + AHEAD < STEPS:
                            score(pair, slot, step + AHEAD)
                        elif more:
                            score(*ahead, step + AHEAD - STEPS)
                        peek_scores(*ahead, peeks[1:2])
                        weigh(pair, slot, step)
                        peek_scores(*ahead, peeks[2:])
                        if more and step == TURN_AT:
                            turn_shifts(*ahead)

                pe.sem_inc(weighed, W_CREDIT)
                peek_scores(0, 0, range(PEEKS))
                turn_shifts(0, 0)
                for step in range(AHEAD):
                    score(0, 0, step)
                with pe.Fori(0, BH // 2 - 1) as pair:
                    for slot in range(2):
                        attend(pair, slot, True)
                attend(BH // 2 - 1, 0, True)
                attend(BH // 2 - 1, 1, False)

            @block.scalar
            def _(act):
                def powers(head, step):
                    count = head * STEPS + step
                    act.wait_ge(scores_ready, count + 1)
                    act.wait_ge(rest_a_ready, count + 1)
                    act.wait_ge(rest_b_ready, count + 1)
                    nc.scalar.activation(probs[:, step % 2], scores[:, step % 2], ACT.Exp, bias=log_scale[:, 0:1], scale=LOGIT_SCALE).then_inc(probs_ready, 1)
                    act.wait_ge(weighed, count + 1 + W_CREDIT - 4)
                    nc.scalar.activation(high[:, step % 4], scores[:, step % 2], ACT.Exp, bias=log_scale[:, 0:1], scale=LOGIT_SCALE).then_inc(high_ready, 1)

                def copy_out(head, half):
                    act.wait_ge(weighed, head * STEPS + (half + 1) * QT + W_CREDIT)
                    act.wait_ge(out_stored[half], head * 48 + 1)
                    nc.scalar.activation(out_copy[:, half], out[0:V_COLS], ACT.Copy).then_inc(out_copied, 1)

                def turn(head, more):
                    for step in range(BEFORE_COPY, STEPS + BEFORE_COPY if more else STEPS):
                        powers(head, step)
                        if step == QT + BEFORE_COPY - 1:
                            copy_out(head, 0)
                    copy_out(head, 1)

                act.wait_ge(ones_ready, 3)
                act.sem_inc(high_ready, H_CREDIT)
                act.sem_inc(out_copied, 1)
                for step in range(BEFORE_COPY):
                    powers(0, step)
                with act.Fori(0, BH - 1) as head:
                    turn(head, True)
                turn(BH - 1, False)

            @block.vector
            def _(dve):
                def read_peeks(head, numbers):
                    for m in numbers:
                        dve.wait_ge(peek_ready, head * PEEKS + m + 1)
                        if m == 0:
                            dve.wait_ge(max_step, head + 1)
                        nc.vector.tensor_reduce(maxima[:, m:m + 1], peek[:, m % 2], AX.X, ALU.max).then_inc(peek_read, 1)

                def shifts(head):
                    dve.wait_ge(peek_read, (head + 1) * PEEKS + K_CREDIT)
                    nc.vector.tensor_reduce(tile_max[:], maxima[:].rearrange("p (t b) -> p t b", b=4), AX.X, ALU.max).then_inc(max_step, 1)
                    dve.wait_ge(max_step, head + 2)
                    nc.vector.tensor_scalar(shift[:], tile_max[:], -LOGIT_SCALE, None, ALU.mult).then_inc(shift_ready, 1)

                def shift_rows(pair, slot, stored):
                    head = pair * 2 + slot
                    dve.wait_ge(shift_turned, head + 1)
                    if stored:
                        dve.wait_ge(shift_stored[1 - slot], (pair + slot) * 16)
                    nc.vector.tensor_copy(shift_row[:], peek[0:QT, 0, 0:P]).then_inc(shift_row_ready, 1)

                def split(head, step):
                    dve.wait_ge(high_ready, head * STEPS + step + 1 + H_CREDIT)
                    nc.vector.tensor_tensor(rest[:, step % 4, 0:SPLIT], probs[:, step % 2, 0:SPLIT], high[:, step % 4, 0:SPLIT],
                                            ALU.subtract).then_inc(rest_a_ready, 1)

                def turn(pair, slot, more):
                    head = pair * 2 + slot
                    ahead = (pair + slot, 1 - slot)
                    for step in range(STEPS):
                        if more or step + 1 < STEPS:
                            split(head, step + 1)
                        if more:
                            read_peeks(head + 1, peeks_at(step))
                            if step == TURN_AT:
                                shifts(head + 1)
                            if step == TURN_AT + 1:
                                shift_rows(*ahead, True)

                for slot in range(2):
                    nc.vector.memset(k[96:P, slot, 0], 1.0 / LOGIT_SCALE).then_inc(ones_ready, 1)
                nc.vector.memset(log_scale[:], math.log(PROB_SCALE)).then_inc(ones_ready, 1)
                dve.sem_inc(peek_read, K_CREDIT)
                dve.sem_inc(max_step, 1)
                dve.sem_inc(rest_a_ready, R_CREDIT)
                for half in range(2):
                    dve.sem_inc(out_stored[half], 1)
                read_peeks(0, range(PEEKS))
                shifts(0)
                shift_rows(0, 0, False)
                split(0, 0)
                with dve.Fori(0, BH // 2 - 1) as pair:
                    for slot in range(2):
                        turn(pair, slot, True)
                turn(BH // 2 - 1, 0, True)
                turn(BH // 2 - 1, 1, False)


def project_out(nc, c, dram, stage):
    x = c["x"]
    ROWS = P // BH
    with Scope(nc, stage) as s:
        w_o = s.sb("w_o", [P, CT, D])
        b_o = s.sb("b_o", [P, CT])
        sums = s.sb("sums", [P, T // ROWS])
        inv = s.sb("inv", [P, CT, N])
        parts = s.sb("parts", [P, 2, CT, N])
        acc = s.ps("acc", [P, 2, CT, BLK])
        sums_loaded, inverted, inv_stored, tables_loaded = s.sem("sums_loaded"), s.sem("inverted"), s.sem("inv_stored"), s.sem("tables_loaded")
        inv_loaded, loaded = ([s.sem(f"{name}{b}") for b in range(B)] for name in ("inv_loaded", "loaded"))
        whole, att_ready, acc_ready, added = s.sem("whole"), s.sem("att_ready"), s.sem("acc_ready"), s.sem("added")

        with nc.Block() as block:

            @block.sync
            def _(sp):
                sp.dma_start(sums[:], dram["att_sum"].rearrange("h (r t) -> (h r) t", r=ROWS)).then_inc(sums_loaded, 16)
                sp.wait_ge(inverted, 1)
                sp.dma_start(dram["att_inv"].rearrange("h (r t) -> (h r) t", r=ROWS), sums[:]).then_inc(inv_stored, 16)
                sp.wait_ge(inv_stored, 16)
                for b in range(B):
                    for tile in range(CT):
                        first = b * HEADS + tile * HEADS // CT
                        sp.dma_start(inv[:, tile, b * T:(b + 1) * T],
                                     dram["att_inv"][first:first + HEADS // CT].unsqueeze(1).broadcast_to([HEADS // CT, HD, T])).then_inc(inv_loaded[b], 16)

            @block.scalar
            def _(act):
                act.dma_start(w_o[:], dram["att_w_o"]).then_inc(tables_loaded, 16)
                act.dma_start(b_o[:], dram["att_b_o"]).then_inc(tables_loaded, 16)
                for b in range(B):
                    for part in range(2):
                        for tile in range(CT):
                            act.dma_start(parts[:, part, tile, b * T:(b + 1) * T], dram["att_o"][part, b * D + tile * P:b * D + (tile + 1) * P]
                                          ).then_inc(loaded[b], 16)

            @block.tensor
            def _(pe):
                pe.wait_ge(tables_loaded, 32)
                for n in range(NBLK):
                    pe.wait_ge(att_ready, n + 1)
                    if n >= 2:
                        pe.wait_ge(added, (n - 1) * CT)
                    for o in range(CT):
                        for tile in range(CT):
                            mm = nc.tensor.matmul(acc[:, n % 2, o], w_o[:, tile, o * P:(o + 1) * P], parts[:, 0, tile, tokens(n)],
                                                  start=tile == 0, stop=tile == CT - 1)
                        mm.then_inc(acc_ready, 1)

            @block.vector
            def _(dve):
                def add(n):
                    for o in range(CT):
                        dve.wait_ge(acc_ready, n * CT + o + 1)
                        nc.vector.scalar_tensor_tensor(x[:, o, tokens(n)], acc[:, n % 2, o], b_o[:, o:o + 1], x[:, o, tokens(n)],
                                                       ALU.add, ALU.add).then_inc(added, 1)

                dve.wait_ge(sums_loaded, 16)
                nc.vector.reciprocal(sums[:], sums[:]).then_inc(inverted, 1)
                dve.wait_ge(tables_loaded, 32)
                for n in range(NBLK):
                    b, first = divmod(n, NBLK // B)
                    if first == 0:
                        dve.wait_ge(loaded[b], 4 * 16)
                    nc.vector.tensor_tensor(parts[:, 0, :, tokens(n)], parts[:, 0, :, tokens(n)], parts[:, 1, :, tokens(n)], ALU.add).then_inc(whole, 1)
                    if first == 0:
                        dve.wait_ge(inv_loaded[b], 16 * CT)
                    dve.wait_ge(whole, n + 1)
                    nc.vector.tensor_tensor(parts[:, 0, :, tokens(n)], parts[:, 0, :, tokens(n)], inv[:, :, tokens(n)], ALU.mult).then_inc(att_ready, 1)
                    if n >= 1:
                        add(n - 1)
                add(NBLK - 1)


def helical_attention(nc, c, dram, stage):
    dram["att_dot"] = nc.dram_tensor("att_dot", (2, 2 * BH * HD, T), F16, kind="Internal").ap()
    dram["att_hel"] = nc.dram_tensor("att_hel", (2, 2, 2 * BH * PAIRS, T), F16, kind="Internal").ap()
    dram["att_o"] = nc.dram_tensor("att_o", (2, BH * HD, T), F32, kind="Internal").ap()
    dram["att_sum"] = nc.dram_tensor("att_sum", (BH, T), F32, kind="Internal").ap()
    dram["att_inv"] = nc.dram_tensor("att_inv", (BH, T), F32, kind="Internal").ap()
    with Scope(nc, stage) as s:
        v = s.sb("v", [P, BH, QT, V_COLS], F16)
        with Scope(nc, f"{stage}_prepare") as prepare:
            qk = prepare.sb("qk", [P, CT, 2, N])
            with Scope(nc, f"{stage}_normed") as normed:
                xn = normed.sb("xn", [P, CT, N])
                layer_norm(nc, c, f"{stage}_ln", xn, None)
                project_qkv(nc, c, dram, f"{stage}_qkv", xn, qk, v)
            helical_features(nc, c, dram, f"{stage}_hel", qk)
        head_attention(nc, c, dram, f"{stage}_heads", v)
    project_out(nc, c, dram, f"{stage}_out")

TAPS = 4
ALPHA_MIN = 0.1
RMS_EPS = 1e-6
QUARTERS = 4
JQ = 16 // QUARTERS
SPAN = 64
CHUNK = 8
CHUNKS = SPAN // CHUNK
SOLVE, MIX = 0, CHUNK * CHUNK
K_IN = MIX + CHUNK * CHUNK
K_OUT = K_IN + CHUNK * HD
Q_IN = K_OUT + CHUNK * HD
DECAY = Q_IN + CHUNK * HD
RECORD = DECAY + 1


def delta_gates(nc, c, dram, stage, xn):
    with Scope(nc, stage) as s:
        w_ab = s.sb("w_ab", [P, CT, 2 * HEADS])
        b_ab = s.sb("b_ab", [2 * HEADS, 2])
        w_down = s.sb("w_down", [P, CT, P])
        w_up = s.sb("w_up", [P, D])
        ab = s.sb("ab", [2 * HEADS, N])
        down = s.sb("down", [P, 2, BLK])
        gate = s.sb("gate", [P, CT, N])
        acc = s.ps("acc", [P, 2, BLK])
        acc_down = s.ps("acc_down", [P, 2, BLK])
        acc_up = s.ps("acc_up", [P, 2, CT, BLK])
        loaded, ab_sum, ab_ready, ab_clipped = s.sem("loaded"), s.sem("ab_sum"), s.sem("ab_ready"), s.sem("ab_clipped")
        down_sum, down_ready, up_sum, gate_ready, stored = s.sem("down_sum"), s.sem("down_ready"), s.sem("up_sum"), s.sem("gate_ready"), s.sem("stored")

        with nc.Block() as block:

            @block.sync
            def _(sp):
                for tile, table in ((w_ab, "delta_w_ab"), (b_ab, "delta_b_ab"), (w_down, "delta_w_down"), (w_up, "delta_w_up")):
                    sp.dma_start(tile[:], dram[table]).then_inc(loaded, 16)
                for n in range(NBLK):
                    sp.wait_ge(gate_ready, (n + 1) * CT)
                    sp.dma_start(dram["delta_gate"][:, :, tokens(n)], gate[:, :, tokens(n)]).then_inc(stored, 16)
                sp.wait_ge(ab_clipped, NBLK)
                for b in range(B):
                    sp.dma_start(dram["delta_ab"][b], ab[:, b * T:(b + 1) * T]).then_inc(stored, 16)
                sp.wait_ge(stored, (B + NBLK) * 16)

            @block.tensor
            def _(pe):
                pe.wait_ge(loaded, 64)
                for n in range(NBLK + 1):
                    if n < NBLK:
                        if n >= 2:
                            pe.wait_ge(ab_ready, n - 1)
                            pe.wait_ge(down_ready, n - 1)
                        for t in range(CT):
                            mm = nc.tensor.matmul(acc[0:2 * HEADS, n % 2], w_ab[:, t], xn[:, t, tokens(n)], start=t == 0, stop=t == CT - 1)
                        mm.then_inc(ab_sum, 1)
                        for t in range(CT):
                            mm = nc.tensor.matmul(acc_down[:, n % 2], w_down[:, t], xn[:, t, tokens(n)], start=t == 0, stop=t == CT - 1)
                        mm.then_inc(down_sum, 1)
                    if n >= 1:
                        pe.wait_ge(down_ready, n)
                        if n >= 3:
                            pe.wait_ge(gate_ready, (n - 2) * CT)
                        for o in range(CT):
                            nc.tensor.matmul(acc_up[:, (n - 1) % 2, o], w_up[:, o * P:(o + 1) * P], down[:, (n - 1) % 2],
                                             start=True, stop=True).then_inc(up_sum, 1)

            @block.scalar
            def _(act):
                def gates(act, n):
                    for o in range(CT):
                        act.wait_ge(up_sum, n * CT + o + 1)
                        nc.scalar.activation(gate[:, o, tokens(n)], acc_up[:, n % 2, o], ACT.Sigmoid).then_inc(gate_ready, 1)

                act.wait_ge(loaded, 64)
                for n in range(NBLK):
                    act.wait_ge(ab_sum, n + 1)
                    nc.scalar.activation(ab[:, tokens(n)], acc[0:2 * HEADS, n % 2], ACT.Sigmoid, bias=b_ab[:, 0:1]).then_inc(ab_ready, 1)
                    act.wait_ge(down_sum, n + 1)
                    if n >= 2:
                        act.wait_ge(up_sum, (n - 1) * CT)
                    nc.scalar.activation(down[:, n % 2], acc_down[:, n % 2], ACT.Silu).then_inc(down_ready, 1)
                    if n >= 1:
                        gates(act, n - 1)
                gates(act, NBLK - 1)

            @block.vector
            def _(dve):
                for n in range(NBLK):
                    dve.wait_ge(ab_ready, n + 1)
                    nc.vector.tensor_scalar(ab[:, tokens(n)], ab[:, tokens(n)], b_ab[:, 1:2], 1.0, ALU.max, ALU.min).then_inc(ab_clipped, 1)


def delta_projections(nc, c, dram, stage, xn, qkv):
    with Scope(nc, stage) as s:
        w_in = s.sb("w_in", [P, 3, CT, D])
        taps = s.sb("taps", [P, 3, CT, TAPS + 1])
        pre = s.sb("pre", [P, 2, B, T + TAPS - 1])
        acc = s.ps("acc", [P, 4, BLK])
        loaded, zeroed, acc_ready, pre_ready, first_tap_done, tap_done, silu_done = (
            s.sem("loaded"), s.sem("zeroed"), s.sem("acc_ready"), s.sem("pre_ready"), s.sem("first_tap_done"), s.sem("tap_done"), s.sem("silu_done"))
        rounds = [(w, tile) for w in range(3) for tile in range(CT)]
        PER_ROUND = (TAPS - 1) * B
        HALF = NBLK // B

        with nc.Block() as block:

            @block.sync
            def _(sp):
                sp.dma_start(w_in[:], dram["delta_w_in"]).then_inc(loaded, 16)
                sp.dma_start(taps[:], dram["delta_taps"]).then_inc(loaded, 16)

            @block.tensor
            def _(pe):
                pe.wait_ge(loaded, 32)
                for r, (w, tile) in enumerate(rounds):
                    for n in range(NBLK):
                        k = r * NBLK + n
                        if k >= 4:
                            pe.wait_ge(pre_ready, k - 3)
                        for t in range(CT):
                            mm = nc.tensor.matmul(acc[:, k % 4], w_in[:, w, t, tile * P:(tile + 1) * P], xn[:, t, tokens(n)],
                                                  start=t == 0, stop=t == CT - 1)
                        mm.then_inc(acc_ready, 1)

            @block.scalar
            def _(act):
                def silu(r):
                    w, tile = rounds[r]
                    for b in range(B):
                        act.wait_ge(tap_done, r * PER_ROUND + (TAPS - 2) * B + b + 1)
                        part = qkv[:, w, tile, b * T:(b + 1) * T]
                        nc.scalar.activation(part, part, ACT.Silu, bias=taps[:, w, tile, TAPS:TAPS + 1]).then_inc(silu_done, 1)

                act.wait_ge(zeroed, 1)
                for r in range(len(rounds)):
                    if r >= 2:
                        act.wait_ge(tap_done, (r - 1) * PER_ROUND)
                    for n in range(NBLK):
                        act.wait_ge(acc_ready, r * NBLK + n + 1)
                        at = TAPS - 1 + n % HALF * BLK
                        nc.scalar.activation(pre[:, r % 2, n // HALF, at:at + BLK], acc[:, (r * NBLK + n) % 4], ACT.Copy).then_inc(pre_ready, 1)
                        if n % HALF == HALF - 1:
                            b = n // HALF
                            w, tile = rounds[r]
                            act.wait_ge(pre_ready, r * NBLK + n + 1)
                            nc.scalar.activation(qkv[:, w, tile, b * T:(b + 1) * T], pre[:, r % 2, b, 0:T], ACT.Copy,
                                                 scale=taps[:, w, tile, 0:1]).then_inc(first_tap_done, 1)
                    if r >= 1:
                        silu(r - 1)
                silu(len(rounds) - 1)

            @block.vector
            def _(dve):
                nc.vector.memset(pre[:, :, :, 0:TAPS - 1], 0.0).then_inc(zeroed, 1)
                for r, (w, tile) in enumerate(rounds):
                    for tap in range(1, TAPS):
                        for b in range(B):
                            part = qkv[:, w, tile, b * T:(b + 1) * T]
                            if tap == 1:
                                dve.wait_ge(first_tap_done, r * B + b + 1)
                            else:
                                dve.wait_ge(tap_done, r * PER_ROUND + (tap - 2) * B + b + 1)
                            nc.vector.scalar_tensor_tensor(part, pre[:, r % 2, b, tap:tap + T], taps[:, w, tile, tap:tap + 1], part,
                                                           ALU.mult, ALU.add).then_inc(tap_done, 1)


def delta_normalise(nc, c, dram, stage, qkv):
    with Scope(nc, stage) as s:
        squares = s.sb("squares", [P, 2, BLK])
        log_sq = s.sb("log_sq", [P, 2, BLK])
        inv = s.sb("inv", [P, 2, BLK])
        sums = s.ps("sums", [P, 2, BLK])
        squares_ready, sums_ready, log_ready, inv_ready, unit_ready = (
            s.sem("squares_ready"), s.sem("sums_ready"), s.sem("log_ready"), s.sem("inv_ready"), s.sem("unit_ready"))
        negated, stored = s.sem("negated"), s.sem("stored")
        steps = [(w, tile, n) for w in range(2) for tile in range(CT) for n in range(NBLK)]

        with nc.Block() as block:

            @block.sync
            def _(sp):
                def put(name, tiles, tile):
                    for b in range(B):
                        sp.dma_start(dram[name][b, :, tile * P:(tile + 1) * P].rearrange("r p t -> p r t"),
                                     tiles[:, tile, b * T:(b + 1) * T].rearrange("p (r t) -> p r t", t=SPAN)).then_inc(stored, 16)

                for tile in range(CT):
                    sp.wait_ge(negated, tile + 1)
                    put("delta_v", qkv[:, 2], tile)
                for w, name in enumerate(("delta_q", "delta_k")):
                    for tile in range(CT):
                        sp.wait_ge(unit_ready, (w * CT + tile + 1) * NBLK)
                        put(name, qkv[:, w], tile)
                sp.wait_ge(stored, 3 * CT * B * 16)

            @block.tensor
            def _(pe):
                for k, (w, tile, n) in enumerate(steps):
                    pe.wait_ge(squares_ready, k + 1)
                    if k >= 2:
                        pe.wait_ge(log_ready, k - 1)
                    nc.tensor.matmul(sums[:, k % 2], c["head_sum"][:], squares[:, k % 2], start=True, stop=True).then_inc(sums_ready, 1)

            @block.scalar
            def _(act):
                def lengths(k):
                    act.wait_ge(sums_ready, k + 1)
                    nc.scalar.activation(log_sq[:, k % 2], sums[:, k % 2], ACT.Ln).then_inc(log_ready, 1)
                    act.wait_ge(log_ready, k + 1)
                    if k >= 2:
                        act.wait_ge(unit_ready, k - 1)
                    nc.scalar.activation(inv[:, k % 2], log_sq[:, k % 2], ACT.Exp, scale=-0.5).then_inc(inv_ready, 1)

                nc.scalar.preload_act_table_set(LOG_EXP_SET)
                for k, (w, tile, n) in enumerate(steps):
                    if k >= 2:
                        act.wait_ge(sums_ready, k - 1)
                    nc.scalar.activation(squares[:, k % 2], qkv[:, w, tile, tokens(n)], ACT.Square).then_inc(squares_ready, 1)
                    if k >= 1:
                        lengths(k - 1)
                lengths(len(steps) - 1)

            @block.vector
            def _(dve):
                for tile in range(CT):
                    nc.vector.tensor_scalar(qkv[:, 2, tile], qkv[:, 2, tile], -1.0, None, ALU.mult).then_inc(negated, 1)
                for k, (w, tile, n) in enumerate(steps):
                    dve.wait_ge(inv_ready, k + 1)
                    part = qkv[:, w, tile, tokens(n)]
                    nc.vector.scalar_tensor_tensor(part, inv[:, k % 2], 1e6, part, ALU.min, ALU.mult).then_inc(unit_ready, 1)


def delta_chunks(nc, c, dram, stage, number):
    PARTS = P // BH
    RUNS = T // SPAN // PARTS // 2
    N_CHUNKS = RUNS * CHUNKS
    C = CHUNK
    with Scope(nc, stage) as s:
        kq = s.sb("kq", [P, 2, RUNS, HD, SPAN])
        ab = s.sb("ab", [P, 2, RUNS * SPAN])
        g = s.sb("g", [P, N_CHUNKS, C + 1, C + 1])
        gram = s.sb("gram", [P, 2, N_CHUNKS, C, C])
        solve = s.sb("solve", [P, N_CHUNKS, C, C])
        terms = s.sb("terms", [P, 4, CHUNKS, C, HD])
        own_terms = s.sb("own_terms", [P, 2, CHUNKS, C, HD])
        solve_terms = s.sb("solve_terms", [P, N_CHUNKS, C - 1, C - 1])
        record = s.sb("record", [P, 2, CHUNKS, RECORD])
        loaded, zeroed, terms_ready, terms_read, g_step = s.sem("loaded"), s.sem("zeroed"), s.sem("terms_ready"), s.sem("terms_read"), s.sem("g_step")
        own_ready, own_read = s.sem("own_ready"), s.sem("own_read")
        solve_step, copied, pool_done, dve_done = s.sem("solve_step"), s.sem("copied"), s.sem("pool_done"), s.sem("dve_done")
        stored = [s.sem(f"stored{slot}") for slot in range(2)]
        rows = [(run, w, t) for run in range(RUNS) for w in range(2) for t in range(C) if w == 1 or t >= 1]
        own_rows = [row for row in rows if row[2] % 3 == 1 or row[1:] == (1, 3)]
        pool_rows = [row for row in rows if row not in own_rows]
        LOADED = 4 * B * PARTS * 16
        alpha = ab[:, 0].rearrange("p (n t) -> p n t", t=C)
        beta = ab[:, 1].rearrange("p (n t) -> p n t", t=C)
        SLOTS = 4
        SOLVED = 3 + 2 * (C - 1)

        def by_token(w, run):
            return kq[:, w, run].rearrange("p i (m u) -> p m u i", u=C)

        def multiply_row(engine, out, run, w, t):
            return engine.tensor_tensor(out[:, :, 0:t + w], by_token(0, run)[:, :, 0:t + w],
                                        by_token(w, run)[:, :, t].unsqueeze(2).broadcast_to([P, CHUNKS, t + w, HD]), ALU.mult)

        with nc.Block() as block:

            @block.sync
            def _(sp):
                for b in range(B):
                    for part in range(PARTS):
                        at = slice((b * PARTS + part) * HEADS, (b * PARTS + part + 1) * HEADS)
                        first = (part * 2 + number) * RUNS
                        for w, name in enumerate(("delta_k", "delta_q")):
                            sp.dma_start(kq[at, w].rearrange("p r i t -> p r (i t)"),
                                         dram[name][b, first:first + RUNS].rearrange("r (h i) t -> h r (i t)", i=HD)).then_inc(loaded, 16)
                            sp.dma_start(ab[at, w], dram["delta_ab"][b, w * HEADS:(w + 1) * HEADS, first * SPAN:(first + RUNS) * SPAN]).then_inc(loaded, 16)
                for run in range(RUNS):
                    sp.wait_ge(copied, run * 2 + 2)
                    sp.wait_ge(pool_done, run * 2 + 2)
                    sp.wait_ge(dve_done, run * 2 + 2)
                    for b in range(B):
                        for part in range(PARTS):
                            at = slice((b * PARTS + part) * HEADS, (b * PARTS + part + 1) * HEADS)
                            sp.dma_start(dram["delta_record"][b, (part * 2 + number) * RUNS + run], record[at, run % 2].rearrange("p m e -> p (m e)")
                                         ).then_inc(stored[run % 2], 16)
                for slot in range(2):
                    sp.wait_ge(stored[slot], RUNS // 2 * B * PARTS * 16)

            @block.gpsimd
            def _(pool):
                pool.wait_ge(loaded, LOADED)
                for k, (run, w, t) in enumerate(pool_rows):
                    if k >= SLOTS:
                        pool.wait_ge(terms_read, k - SLOTS + 1)
                    multiply_row(nc.gpsimd, terms[:, k % SLOTS], run, w, t).then_inc(terms_ready, 1)
                pool.wait_ge(g_step, C + 1)
                for run in range(RUNS):
                    at = slice(run * CHUNKS, (run + 1) * CHUNKS)
                    if run >= 2:
                        pool.wait_ge(stored[run % 2], run // 2 * B * PARTS * 16)
                    for w, first, place in ((0, 0, K_IN), (1, 1, Q_IN)):
                        nc.gpsimd.tensor_tensor(record[:, run % 2, :, place:place + C * HD].rearrange("p m (t i) -> p m t i", i=HD), by_token(w, run),
                                                g[:, at, first:first + C, 0].unsqueeze(3).broadcast_to([P, CHUNKS, C, HD]), ALU.mult
                                                ).then_inc(pool_done, 1)

            @block.scalar
            def _(act):
                act.wait_ge(solve_step, SOLVED)
                for run in range(RUNS):
                    at = slice(run * CHUNKS, (run + 1) * CHUNKS)
                    if run >= 2:
                        act.wait_ge(stored[run % 2], run // 2 * B * PARTS * 16)
                    nc.scalar.activation(record[:, run % 2, :, SOLVE:SOLVE + C * C], solve[:, at].rearrange("p n t s -> p n (t s)"), ACT.Copy).then_inc(copied, 1)
                    nc.scalar.activation(record[:, run % 2, :, DECAY], g[:, at, C, 0], ACT.Copy).then_inc(copied, 1)

            @block.vector
            def _(dve):
                nc.vector.memset(g[:], 1.0).then_inc(g_step, 1)
                nc.vector.memset(gram[:], 0.0).then_inc(zeroed, 1)
                nc.vector.memset(solve[:], 0.0).then_inc(zeroed, 1)
                dve.wait_ge(loaded, LOADED)
                for t in range(C):
                    dve.wait_ge(g_step, t + 1)
                    nc.vector.tensor_tensor(g[:, :, t + 1, 0:t + 1], g[:, :, t, 0:t + 1], alpha[:, :, t].unsqueeze(2).broadcast_to([P, N_CHUNKS, t + 1]),
                                            ALU.mult).then_inc(g_step, 1)
                dve.wait_ge(zeroed, 2)
                def sum_row(out, run, w, t):
                    return nc.vector.tensor_reduce(gram[:, w, run * CHUNKS:(run + 1) * CHUNKS, t, 0:t + w], out[:, :, 0:t + w], AX.X, ALU.add)

                own = 0
                for k, row in enumerate(pool_rows):
                    dve.wait_ge(terms_ready, k + 1)
                    sum_row(terms[:, k % SLOTS], *row).then_inc(terms_read, 1)
                    if own < len(own_rows) and own * len(pool_rows) <= k * len(own_rows):
                        if own >= 2:
                            dve.wait_ge(own_read, own - 1)
                        multiply_row(nc.vector, own_terms[:, own % 2], *own_rows[own]).then_inc(own_ready, 1)
                        if own >= 1:
                            dve.wait_ge(own_ready, own)
                            sum_row(own_terms[:, (own - 1) % 2], *own_rows[own - 1]).then_inc(own_read, 1)
                        own += 1
                dve.wait_ge(own_ready, len(own_rows))
                sum_row(own_terms[:, (own - 1) % 2], *own_rows[-1]).then_inc(own_read, 1)
                dve.wait_ge(terms_read, len(pool_rows))
                dve.wait_ge(own_read, len(own_rows))
                dve.wait_ge(g_step, C + 1)
                low = gram[:, 0, :, 1:, 0:C - 1]
                nc.vector.tensor_tensor(low, low, g[:, :, 1:C, 1:C], ALU.mult).then_inc(solve_step, 1)
                nc.vector.tensor_scalar(solve[:].rearrange("p n t s -> p n (t s)")[:, :, 0:C * C:C + 1], beta, -1.0, None, ALU.mult).then_inc(solve_step, 1)
                dve.wait_ge(solve_step, 2)
                nc.vector.tensor_tensor(low, low, beta[:, :, 1:].unsqueeze(3).broadcast_to([P, N_CHUNKS, C - 1, C - 1]), ALU.mult).then_inc(solve_step, 1)
                for t in range(1, C):
                    dve.wait_ge(solve_step, 3 + 2 * (t - 1))
                    nc.vector.tensor_tensor(solve_terms[:, :, 0:t, 0:t], solve[:, :, 0:t, 0:t].rearrange("p n s c -> p n c s"),
                                            gram[:, 0, :, t, 0:t].unsqueeze(2).broadcast_to([P, N_CHUNKS, t, t]), ALU.mult).then_inc(solve_step, 1)
                    dve.wait_ge(solve_step, 3 + 2 * (t - 1) + 1)
                    nc.vector.tensor_reduce(solve[:, :, t, 0:t], solve_terms[:, :, 0:t, 0:t], AX.X, ALU.add, negate=True).then_inc(solve_step, 1)
                for run in range(RUNS):
                    at = slice(run * CHUNKS, (run + 1) * CHUNKS)
                    if run >= 2:
                        dve.wait_ge(stored[run % 2], run // 2 * B * PARTS * 16)
                    nc.vector.tensor_tensor(record[:, run % 2, :, MIX:MIX + C * C].rearrange("p m (t s) -> p m t s", s=C), gram[:, 1, at],
                                            g[:, at, 1:, 1:], ALU.mult).then_inc(dve_done, 1)
                    nc.vector.tensor_tensor(record[:, run % 2, :, K_OUT:K_OUT + C * HD].rearrange("p m (i s) -> p m i s", s=C),
                                            kq[:, 0, run].rearrange("p i (m u) -> p m i u", u=C),
                                            g[:, at, C, 1:].unsqueeze(2).broadcast_to([P, CHUNKS, HD, C]), ALU.mult).then_inc(dve_done, 1)


def delta_recurrence(nc, c, dram, stage):
    C = CHUNK
    LANES = 2
    JL = JQ // LANES
    with Scope(nc, stage) as s:
        record = s.sb("record", [P, 2, CHUNKS, RECORD])
        vt = s.sb("vt", [P, 2, JQ, SPAN])
        state = s.sb("state", [P, 4, JQ, HD])
        terms = s.sb("terms", [P, 2, CHUNKS, JQ, C, HD + 1])
        error = s.sb("error", [P, 2, JQ, C])
        u_terms = s.sb("u_terms", [P, 2, JQ, C, C])
        u = s.sb("u", [P, 4, JQ, C])
        s_terms = s.sb("s_terms", [P, 2, JQ, HD, C + 1])
        o_terms = s.sb("o_terms", [P, 2, JQ, C, HD + C])
        FOLD = (HD + C) // 2
        o_halves = s.sb("o_halves", [P, 2, JQ, C, FOLD])
        o_quarters = s.sb("o_quarters", [P, 2, JQ, C, FOLD // 2])
        o_out = s.sb("o_out", [P, 2, JQ, SPAN])
        loaded = [s.sem(f"loaded{slot}") for slot in range(2)]
        stored = [s.sem(f"stored{slot}") for slot in range(2)]
        o_halves_ready, o_quarters_ready = s.sem("o_halves_ready"), s.sem("o_quarters_ready")
        chain = [s.sem(f"chain{lane}") for lane in range(LANES)]
        v_ready, decayed, o_terms_ready, o_ready = s.sem("v_ready"), s.sem("decayed"), s.sem("o_terms_ready"), s.sem("o_ready")
        ROUNDS = T // SPAN
        LOADS = 3 * B * 16 - B * 16
        STEP = 6
        BEFORE = STEP * CHUNKS * 2
        C0 = BEFORE + 1
        O_CREDIT = 2 * CHUNKS

        def wait_chains(queue, count):
            for lane in range(LANES):
                queue.wait_ge(chain[lane], count)

        with nc.Block() as block:

            @block.sync
            def _(sp):
                def load(pair, slot):
                    for b in range(B):
                        half = slice(b * P // B, (b + 1) * P // B)
                        chunk = bass.ds(pair * 2 + slot, 1)
                        sp.dma_start(record[half, slot].rearrange("p m e -> p (m e)"), dram["delta_record"][b, chunk].squeeze(0).unsqueeze(1)
                                     .broadcast_to([HEADS, QUARTERS, CHUNKS * RECORD])).then_inc(loaded[slot], 16)
                        sp.dma_start(vt[half, slot], dram["delta_v"][b, chunk].rearrange("r (p j) t -> (r p) (j t)", j=JQ)).then_inc(loaded[slot], 16)

                def store(pair, slot):
                    sp.wait_ge(o_ready, (pair * 2 + slot + 1) * CHUNKS + O_CREDIT)
                    for b in range(B):
                        half = slice(b * P // B, (b + 1) * P // B)
                        sp.dma_start(dram["delta_o"][b, bass.ds(pair * 2 + slot, 1)].rearrange("r (p j) t -> (r p) (j t)", j=JQ),
                                     o_out[half, slot]).then_inc(stored[slot], 16)

                for slot in range(2):
                    load(0, slot)
                with sp.Fori(1, ROUNDS // 2) as pair:
                    for slot in range(2):
                        store(pair - 1, slot)
                        load(pair, slot)
                for slot in range(2):
                    store(ROUNDS // 2 - 1, slot)
                for slot in range(2):
                    sp.wait_ge(stored[slot], ROUNDS // 2 * 32 + 32)

            @block.scalar
            def _(act):
                with act.Fori(0, ROUNDS // 2) as pair:
                    for slot in range(2):
                        act.wait_ge(loaded[slot], (pair + 1) * LOADS)
                        wait_chains(act, (pair * 2 + slot) * CHUNKS * STEP + 1)
                        for j in range(JQ):
                            ins = nc.scalar.activation(terms[:, slot, :, j, :, HD], vt[:, slot, j].rearrange("p (m t) -> p m t", t=C), ACT.Copy)
                        ins.then_inc(v_ready, 1)
                        for m in range(CHUNKS):
                            wait_chains(act, ((pair * 2 + slot) * CHUNKS + m) * STEP + C0)
                            nc.scalar.activation(s_terms[:, m % 2, :, :, C], state[:, (m - 1) % 4], ACT.Copy,
                                                 scale=record[:, slot, m, DECAY:DECAY + 1]).then_inc(decayed, 1)

            @block.gpsimd
            def _(pool):
                with pool.Fori(0, ROUNDS // 2) as pair:
                    for slot in range(2):
                        pool.wait_ge(loaded[slot], (pair + 1) * LOADS)
                        for m in range(CHUNKS):
                            number = (pair * 2 + slot) * CHUNKS + m
                            table = record[:, slot, m]
                            wait_chains(pool, number * STEP + C0)
                            nc.gpsimd.tensor_tensor(o_terms[:, m % 2, :, :, 0:HD], state[:, (m - 1) % 4].unsqueeze(2).broadcast_to([P, JQ, C, HD]),
                                                    table[:, Q_IN:Q_IN + C * HD].rearrange("p (t i) -> p t i", i=HD).unsqueeze(1)
                                                    .broadcast_to([P, JQ, C, HD]), ALU.mult).then_inc(o_terms_ready, 1)
                            wait_chains(pool, number * STEP + C0 + 4)
                            nc.gpsimd.tensor_tensor(o_terms[:, m % 2, :, :, HD:], u[:, m % 4].unsqueeze(2).broadcast_to([P, JQ, C, C]),
                                                    table[:, MIX:MIX + C * C].rearrange("p (t s) -> p t s", s=C).unsqueeze(1)
                                                    .broadcast_to([P, JQ, C, C]), ALU.mult).then_inc(o_terms_ready, 1)
                            pool.wait_ge(o_terms_ready, number * 2 + 2)
                            nc.gpsimd.tensor_tensor(o_halves[:, m % 2], o_terms[:, m % 2, :, :, 0:FOLD], o_terms[:, m % 2, :, :, FOLD:], ALU.add
                                                    ).then_inc(o_halves_ready, 1)
                            pool.wait_ge(o_halves_ready, number + 1)
                            pool.wait_ge(o_ready, number + O_CREDIT - 1)
                            nc.gpsimd.tensor_tensor(o_quarters[:, m % 2], o_halves[:, m % 2, :, :, 0:FOLD // 2], o_halves[:, m % 2, :, :, FOLD // 2:],
                                                    ALU.add).then_inc(o_quarters_ready, 1)

            @block.vector
            def _(dve):
                def outputs(pair, slot, m):
                    dve.wait_ge(o_quarters_ready, (pair * 2 + slot) * CHUNKS + m + 1)
                    if m == 0:
                        dve.wait_ge(stored[slot], pair * 32 + 32)
                    nc.vector.tensor_reduce(o_out[:, slot, :, m * C:(m + 1) * C], o_quarters[:, m % 2], AX.X, ALU.add).then_inc(o_ready, 1)

                def product(out, matrix, vector, rows, columns):
                    return nc.vector.tensor_tensor(out, matrix.rearrange("p (r c) -> p r c", c=columns).unsqueeze(1).broadcast_to([P, JL, rows, columns]),
                                                   vector.unsqueeze(2).broadcast_to([P, JL, rows, columns]), ALU.mult)

                def link(slot, m, number, at):
                    table = record[:, slot, m]
                    for lane in range(LANES):
                        js = slice(lane * JL, (lane + 1) * JL)
                        dve.wait_ge(chain[lane], number * STEP + C0 + at)
                        if at == 0:
                            ins = product(terms[:, slot, m, js, :, 0:HD], table[:, K_IN:K_IN + C * HD], state[:, (m - 1) % 4, js], C, HD)
                        elif at == 1:
                            ins = nc.vector.tensor_reduce(error[:, m % 2, js], terms[:, slot, m, js], AX.X, ALU.add)
                        elif at == 2:
                            ins = product(u_terms[:, m % 2, js], table[:, SOLVE:SOLVE + C * C], error[:, m % 2, js], C, C)
                        elif at == 3:
                            ins = nc.vector.tensor_reduce(u[:, m % 4, js], u_terms[:, m % 2, js], AX.X, ALU.add)
                        elif at == 4:
                            ins = product(s_terms[:, m % 2, js, :, 0:C], table[:, K_OUT:K_OUT + C * HD], u[:, m % 4, js], HD, C)
                        else:
                            ins = nc.vector.tensor_reduce(state[:, m % 4, js], s_terms[:, m % 2, js], AX.X, ALU.add)
                        ins.then_inc(chain[lane], 1)

                for lane in range(LANES):
                    dve.sem_inc(chain[lane], BEFORE)
                    dve.wait_ge(chain[lane], BEFORE)
                    nc.vector.memset(state[:, 3, lane * JL:(lane + 1) * JL], 0.0).then_inc(chain[lane], 1)
                dve.sem_inc(o_ready, O_CREDIT)
                for slot in range(2):
                    dve.sem_inc(stored[slot], 32)
                with dve.Fori(0, ROUNDS // 2) as pair:
                    for slot in range(2):
                        dve.wait_ge(v_ready, pair * 2 + slot + 1)
                        for m in range(CHUNKS):
                            number = (pair * 2 + slot) * CHUNKS + m
                            for at in range(STEP):
                                if at == 5:
                                    if m >= 1:
                                        outputs(pair, slot, m - 1)
                                    dve.wait_ge(decayed, number + 1)
                                link(slot, m, number, at)
                        outputs(pair, slot, CHUNKS - 1)


def delta_output(nc, c, dram, stage):
    x = c["x"]
    with Scope(nc, stage) as s:
        o_all = s.sb("o_all", [P, CT, N])
        gate = s.sb("gate", [P, CT, N])
        w_o = s.sb("w_o", [P, CT, D])
        rms_w = s.sb("rms_w", [P, CT])
        eps = s.sb("eps", [P, 1])
        squares = s.sb("squares", [P, 2, CT, BLK])
        log_sq = s.sb("log_sq", [P, 2, CT, BLK])
        inv = s.sb("inv", [P, 2, CT, BLK])
        sums = s.ps("sums", [P, 2, CT, BLK])
        acc = s.ps("acc", [P, 2, CT, BLK])
        tables_loaded, loaded = s.sem("tables_loaded"), [s.sem(f"loaded{b}") for b in range(B)]
        eps_ready, squares_ready, sums_ready, log_ready, inv_ready, step_done, acc_ready, added = (
            s.sem("eps_ready"), s.sem("squares_ready"), s.sem("sums_ready"), s.sem("log_ready"), s.sem("inv_ready"),
            s.sem("step_done"), s.sem("acc_ready"), s.sem("added"))

        with nc.Block() as block:

            @block.sync
            def _(sp):
                for tile, table in ((w_o, "delta_w_o"), (rms_w, "delta_rms_w")):
                    sp.dma_start(tile[:], dram[table]).then_inc(tables_loaded, 16)
                for b in range(B):
                    for tile in range(CT):
                        sp.dma_start(o_all[:, tile, b * T:(b + 1) * T].rearrange("p (r t) -> p r t", t=SPAN),
                                     dram["delta_o"][b, :, tile * P:(tile + 1) * P].rearrange("r p t -> p r t")).then_inc(loaded[b], 16)
                    sp.dma_start(gate[:, :, b * T:(b + 1) * T], dram["delta_gate"][:, :, b * T:(b + 1) * T]).then_inc(loaded[b], 16)

            @block.tensor
            def _(pe):
                pe.wait_ge(tables_loaded, 32)
                for n in range(NBLK + 1):
                    if n < NBLK:
                        pe.wait_ge(squares_ready, n + 1)
                        if n >= 2:
                            pe.wait_ge(log_ready, n - 1)
                        for tile in range(CT):
                            mm = nc.tensor.matmul(sums[:, n % 2, tile], c["head_sum"][:], squares[:, n % 2, tile], start=True, stop=True)
                        mm.then_inc(sums_ready, 1)
                    if n >= 1:
                        pe.wait_ge(step_done, n * 2 * CT)
                        if n >= 3:
                            pe.wait_ge(added, n - 2)
                        for o in range(CT):
                            for tile in range(CT):
                                mm = nc.tensor.matmul(acc[:, (n - 1) % 2, o], w_o[:, tile, o * P:(o + 1) * P], o_all[:, tile, tokens(n - 1)],
                                                      start=tile == 0, stop=tile == CT - 1)
                        mm.then_inc(acc_ready, 1)

            @block.scalar
            def _(act):
                def lengths(n):
                    act.wait_ge(sums_ready, n + 1)
                    nc.scalar.activation(log_sq[:, n % 2], sums[:, n % 2], ACT.Ln, bias=eps[:, 0:1], scale=1.0 / 16).then_inc(log_ready, 1)
                    act.wait_ge(log_ready, n + 1)
                    if n >= 2:
                        act.wait_ge(step_done, (n - 1) * 2 * CT)
                    nc.scalar.activation(inv[:, n % 2], log_sq[:, n % 2], ACT.Exp, scale=-0.5).then_inc(inv_ready, 1)

                nc.scalar.preload_act_table_set(LOG_EXP_SET)
                act.wait_ge(eps_ready, 1)
                for n in range(NBLK):
                    if n % (NBLK // B) == 0:
                        act.wait_ge(loaded[n // (NBLK // B)], 16 * (CT + 1))
                    if n >= 2:
                        act.wait_ge(sums_ready, n - 1)
                    nc.scalar.activation(squares[:, n % 2], o_all[:, :, tokens(n)], ACT.Square).then_inc(squares_ready, 1)
                    if n >= 1:
                        lengths(n - 1)
                lengths(NBLK - 1)

            @block.vector
            def _(dve):
                nc.vector.memset(eps[:], RMS_EPS).then_inc(eps_ready, 1)
                dve.wait_ge(tables_loaded, 32)
                for n in range(NBLK + 1):
                    if n < NBLK:
                        if n % (NBLK // B) == 0:
                            dve.wait_ge(loaded[n // (NBLK // B)], 16 * (CT + 1))
                        dve.wait_ge(inv_ready, n + 1)
                        for tile in range(CT):
                            nc.vector.scalar_tensor_tensor(inv[:, n % 2, tile], inv[:, n % 2, tile], rms_w[:, tile:tile + 1], gate[:, tile, tokens(n)],
                                                           ALU.mult, ALU.mult).then_inc(step_done, 1)
                        for tile in range(CT):
                            dve.wait_ge(step_done, n * 2 * CT + tile + 1)
                            nc.vector.tensor_tensor(o_all[:, tile, tokens(n)], o_all[:, tile, tokens(n)], inv[:, n % 2, tile], ALU.mult).then_inc(step_done, 1)
                    if n >= 1:
                        dve.wait_ge(acc_ready, n)
                        nc.vector.tensor_tensor(x[:, :, tokens(n - 1)], x[:, :, tokens(n - 1)], acc[:, (n - 1) % 2], ALU.add).then_inc(added, 1)


def delta_attention(nc, c, dram, stage):
    for name in ("delta_q", "delta_k", "delta_v", "delta_o"):
        dram[name] = nc.dram_tensor(name, (B, T // SPAN, D, SPAN), F32, kind="Internal").ap()
    dram["delta_ab"] = nc.dram_tensor("delta_ab", (B, 2 * HEADS, T), F32, kind="Internal").ap()
    dram["delta_record"] = nc.dram_tensor("delta_record", (B, T // SPAN, HEADS, CHUNKS * RECORD), F32, kind="Internal").ap()
    dram["delta_gate"] = nc.dram_tensor("delta_gate", (P, CT, N), F32, kind="Internal").ap()
    with Scope(nc, stage) as normed:
        xn = normed.sb("xn", [P, CT, N])
        layer_norm(nc, c, f"{stage}_ln", xn, None)
        delta_gates(nc, c, dram, f"{stage}_gates", xn)
        with Scope(nc, f"{stage}_qkv") as s:
            qkv = s.sb("qkv", [P, 3, CT, N])
            delta_projections(nc, c, dram, f"{stage}_in", xn, qkv)
            delta_normalise(nc, c, dram, f"{stage}_unit", qkv)
    for part in range(2):
        delta_chunks(nc, c, dram, f"{stage}_chunks{part}", part)
    delta_recurrence(nc, c, dram, f"{stage}_scan")
    delta_output(nc, c, dram, f"{stage}_out")



def build(nc, dram):
    with Scope(nc, "main") as s:
        c = {
            "x": s.sb("x", [P, CT, N]),
            "mean_matrix": s.sb("mean_matrix", [P, P]),
            "identity": s.sb("identity", [P, P]),
            "head_sum": s.sb("head_sum", [P, P]),
            "ln_eps": s.sb("ln_eps", [P, 1]),
        }
        load_constants(nc, c, dram)
        gated_experts(nc, c, dram, "ffn0", c["x_loaded"])
        delta_attention(nc, c, dram, "delta")
        gated_experts(nc, c, dram, "ffn1")
        prototype_mixture(nc, c, dram, "mix0")
        helical_attention(nc, c, dram, "att")
        prototype_mixture(nc, c, dram, "mix1", dram["out"])


def lay_out(inputs):
    import numpy as np

    def rows(a):
        return np.ascontiguousarray(a.reshape(CT, P, -1).transpose(1, 0, 2))

    def helical_weights(w):
        out = np.zeros((8, HD, CT, 2, 2, QG, PAIRS), np.float32)
        for head in range(HEADS):
            tile, of_eight = divmod(head, 8)
            half, of_four = divmod(of_eight, QG)
            out[of_eight, :, tile, half, :, of_four] = w[head].reshape(PAIRS, 2, HD).transpose(2, 1, 0)
        return out.reshape(P, CT, 2, 2, P)

    arrays = {
        "x": rows(inputs["L0_attn_x"].reshape(N, D).T),
        "mean_matrix": np.full((P, P), 1.0 / D, np.float32),
        "identity": np.eye(P, dtype=np.float32),
        "head_sum": np.kron(np.eye(8, dtype=np.float32), np.ones((16, 16), np.float32)),
        "gate_w": rows(inputs["L0_ffn_gate_w"].T),
        "gate_b": np.tile(inputs["L0_ffn_gate_b"], (P, 1)),
        "expert": np.concatenate([
            inputs["L0_ffn_expert_w"].transpose(0, 2, 1).reshape(-1, CT, P, D).transpose(2, 0, 1, 3).reshape(P, -1, CT * D),
            inputs["L0_ffn_expert_b"].reshape(-1, CT, P).transpose(2, 0, 1)], axis=2),
        "proto": rows(inputs["L1_ffn_prototypes"].T),
        "proto_rows": inputs["L1_ffn_prototypes"],
        "temp": np.full((P, 1), inputs["L1_ffn_temp"]),
        "numbers": np.tile(np.arange(inputs["L1_ffn_prototypes"].shape[0], dtype=np.float32), (P, 1)),
        "proto_B": rows(inputs["L1_ffn_B"].reshape(-1, D).T),
        "proto_A": np.ascontiguousarray(inputs["L1_ffn_A"].transpose(0, 2, 1).reshape(-1, P, D).transpose(1, 0, 2)),
        "proto_bias": inputs["L1_ffn_bias"],
        "proto_spread": np.kron(np.eye(inputs["L1_ffn_B"].shape[0], dtype=np.float32), np.ones((1, inputs["L1_ffn_B"].shape[1]), np.float32)),
        "att_w_qk": np.stack([rows(inputs["L1_attn_Wq"].T), rows(inputs["L1_attn_Wk"].T)], axis=1),
        "att_w_v": rows(inputs["L1_attn_Wv"].T),
        "att_b_qk": np.stack([inputs["L1_attn_bq"].reshape(CT, P), inputs["L1_attn_bk"].reshape(CT, P)]).transpose(2, 0, 1).copy(),
        "att_b_v": np.tile(inputs["L1_attn_bv"], (P, 1)),
        "att_w_o": rows(inputs["L1_attn_Wo"].T),
        "att_b_o": inputs["L1_attn_bo"].reshape(CT, P).T.copy(),
        "att_hel_w": helical_weights(inputs["L1_attn_Whel"]),
        "att_hel_b": np.ascontiguousarray(inputs["L1_attn_bhel"].reshape(CT, 2, QG, PAIRS, 2).transpose(2, 3, 0, 1, 4).reshape(P, CT, 2, 2)),
        "delta_w_in": np.stack([rows(inputs[f"L0_attn_W{n}"]) for n in "qkv"], axis=1),
        "delta_taps": np.stack([np.concatenate([inputs[f"L0_attn_{n}cw"], inputs[f"L0_attn_{n}cb"][:, None]], axis=1).reshape(CT, P, TAPS + 1)
                                for n in "qkv"]).transpose(2, 0, 1, 3).copy(),
        "delta_w_ab": np.concatenate([rows(inputs["L0_attn_Wa"]), rows(inputs["L0_attn_Wb"])], axis=2),
        "delta_b_ab": np.stack([np.concatenate([inputs["L0_attn_ba"], inputs["L0_attn_bb"]]),
                                np.repeat(np.array([ALPHA_MIN, 0.0], np.float32), HEADS)], axis=1),
        "delta_w_down": rows(inputs["L0_attn_Wgd"]),
        "delta_w_up": inputs["L0_attn_Wgu"],
        "delta_w_o": rows(inputs["L0_attn_Wo"]),
        "delta_rms_w": inputs["L0_attn_rms_w"].reshape(CT, P).T.copy(),
    }
    return arrays


def kernel(**inputs):
    import numpy as np
    import concourse.bacc as bacc
    from concourse.bass_utils import run_bass_kernel_spmd

    nc = bacc.Bacc("TRN2", target_bir_lowering=False, num_devices=1)
    arrays, dram = {}, {}
    for name, a in lay_out({k: np.asarray(v) for k, v in inputs.items()}).items():
        arrays[f"in_{name}"] = a
        dram[name] = nc.dram_tensor(f"in_{name}", a.shape, mybir.dt.from_np(a.dtype), kind="ExternalInput").ap()
    dram["out"] = nc.dram_tensor("out_x", (P, CT, N), F32, kind="ExternalOutput").ap()
    build(nc, dram)
    r = run_bass_kernel_spmd(nc, [arrays], core_ids=[0])
    return r.results[0]["out_x"].transpose(1, 0, 2).reshape(D, N).T.reshape(B, T, D)
```
